# Optimizing a Trainium2 kernel written in Bass

```python
import numpy as np
import jax
import jax.numpy as jnp

def _softmax(x, axis=-1):
    return jax.nn.softmax(x, axis=axis)

def _gelu(x):
    return jax.nn.gelu(x, approximate=True)

def _silu(x):
    return jax.nn.silu(x)

def _sigmoid(x):
    return jax.nn.sigmoid(x)

def _layernorm(x, axis=-1, eps=1e-05):
    m = jnp.mean(x, axis=axis, keepdims=True)
    v = jnp.var(x, axis=axis, keepdims=True)
    return (x - m) / jnp.sqrt(v + eps)

def _scatter_add(tgt, idx, src, axis=0):
    return tgt.at[idx].add(src)

def _segment_sum(src, seg, n):
    return jax.ops.segment_sum(src, seg, n)
kernel_name = 'mk_conv_attn_hybrid_d2_conv_nchw384_r4_ec6125'

def setup_inputs(seed: int=0):
    np.random.seed(seed)
    _w = jnp.asarray

    def _rec_inputs():
        import jax
        import jax.numpy as jnp
        _gk = jax.random.key(seed)
        x = -0.0002221 + 1 * jax.random.normal(jax.random.fold_in(_gk, 1), (16, 96, 16, 16), jnp.float32)
        return x
    x = _rec_inputs()

    def _L0_conv_setup():
        import jax, jax.numpy as jnp
        import numpy as np
        from jax import lax
        PLANES = 96
        N_POINTS = 4
        KERNEL_SIZE = 11
        INIT_RADIUS = 2.0 * (2.0 / KERNEL_SIZE)

        def _make_kernels(weight_coord, radius, weights):
            K = KERNEL_SIZE
            lin = jnp.linspace(-1.0, 1.0, K)
            gy, gx = jnp.meshgrid(lin, lin, indexing='ij')
            kernel_coord = jnp.stack([gy, gx], axis=0).reshape(2, K * K)
            diff = weight_coord[:, :, None, :] - kernel_coord.T[None, None, :, :]
            diff = jnp.transpose(diff, (0, 1, 3, 2)).reshape(1, N_POINTS, 2, K, K)
            d = jax.nn.relu(1.0 - jnp.abs(diff).sum(axis=2) / radius)
            kernels = jnp.matmul(weights, d.reshape(1, N_POINTS, K * K)).reshape(PLANES, K, K)
            kernels = jnp.flip(jnp.transpose(kernels, (0, 2, 1)), axis=1)
            return kernels
        key = jax.random.key(seed)
        k1, k2, k3 = jax.random.split(key, 3)
        x = jax.random.normal(k1, (16, PLANES, 16, 16), dtype=jnp.float32)
        weight_coord = jnp.clip(0.2 * jax.random.normal(k2, (1, N_POINTS, 2), dtype=jnp.float32), -1.0, 1.0)
        radius = jnp.full((1, N_POINTS, 1, 1), INIT_RADIUS, dtype=jnp.float32)
        weights = 0.02 * jax.random.normal(k3, (1, PLANES, N_POINTS), dtype=jnp.float32)
        return {'x': x, 'weight_coord': weight_coord, 'radius': radius, 'weights': weights}
    _L0_conv_all = _L0_conv_setup()
    _L0_conv_in = {k: v for k, v in _L0_conv_all.items() if k in ('weight_coord', 'radius', 'weights')}
    del _L0_conv_all

    def _L1_attn_setup():
        import jax, jax.numpy as jnp
        import numpy as np
        N_EMBED = 96
        N_HEAD = 6
        HEAD_DIM = N_EMBED // N_HEAD
        ROPE_BASE = 10000.0

        def _rope_emb(T, head_dim):
            inv_freq = 1.0 / ROPE_BASE ** (jnp.arange(0, head_dim, 2, dtype=jnp.float32) / head_dim)
            t = jnp.arange(T, dtype=jnp.float32)
            freqs = t[:, None] * inv_freq[None, :]
            return jnp.repeat(freqs, 2, axis=1)

        def _apply_rope(x, emb):
            cos = jnp.cos(emb)[None, None]
            sin = jnp.sin(emb)[None, None]
            x2 = x.reshape(*x.shape[:-1], -1, 2)
            partner = jnp.stack([-x2[..., 1], x2[..., 0]], axis=-1).reshape(x.shape)
            return x * cos + partner * sin
        key = jax.random.key(seed)
        k1, k2, k3 = jax.random.split(key, 3)
        B, T = (16, 64)
        x = jax.random.normal(k1, (B, T, N_EMBED), dtype=jnp.float32)
        w_attn = jax.random.normal(k2, (N_EMBED, 3 * N_EMBED), dtype=jnp.float32) * N_EMBED ** (-0.5)
        w_proj = jax.random.normal(k3, (N_EMBED, N_EMBED), dtype=jnp.float32) * N_EMBED ** (-0.5)
        return {'x': x, 'w_attn': w_attn, 'w_proj': w_proj}
    _L1_attn_all = _L1_attn_setup()
    _L1_attn_in = {k: v for k, v in _L1_attn_all.items() if k in ('w_attn', 'w_proj')}
    del _L1_attn_all

    def _L1_ffn_setup():
        import jax, jax.numpy as jnp
        import numpy as np
        NUM_GROUPS = 5
        EPS = 1e-05
        QB = 128.0

        def _binarize_weights_groupwise(W):
            n_out = W.shape[0]
            gs = n_out // NUM_GROUPS
            Wb = jnp.zeros_like(W)
            for g in range(NUM_GROUPS):
                wg = W[g * gs:(g + 1) * gs]
                z = wg - wg.mean()
                ste = z + jax.lax.stop_gradient(jnp.sign(z) - z)
                Wb = Wb.at[g * gs:(g + 1) * gs].set(ste)
            return Wb

        def _quantize_activations_groupwise(x):
            n = x.shape[0]
            gs = n // NUM_GROUPS
            xq = jnp.zeros_like(x)
            for g in range(NUM_GROUPS):
                ag = x[g * gs:(g + 1) * gs]
                gamma = jnp.max(jnp.abs(ag))
                xq = xq.at[g * gs:(g + 1) * gs].set(jnp.clip(ag * QB / (gamma + EPS), -QB + EPS, QB - EPS))
            return xq

        def _bitlinear(x, W, b):
            Wb = _binarize_weights_groupwise(W)
            y = jnp.einsum('btc,oc->bto', x, Wb) + b
            return _quantize_activations_groupwise(y)
        key = jax.random.key(seed)
        k1, k2, k3, k4, k5 = jax.random.split(key, 5)
        B, T, C = (10, 512, 96)
        H = 4 * C
        lim1 = 1.0 / np.sqrt(C)
        lim2 = 1.0 / np.sqrt(H)
        x = jax.random.normal(k1, (B, T, C), dtype=jnp.float32)
        W1 = jax.random.uniform(k2, (H, C), minval=-lim1, maxval=lim1, dtype=jnp.float32)
        b1 = jax.random.uniform(k3, (H,), minval=-lim1, maxval=lim1, dtype=jnp.float32)
        W2 = jax.random.uniform(k4, (C, H), minval=-lim2, maxval=lim2, dtype=jnp.float32)
        b2 = jax.random.uniform(k5, (C,), minval=-lim2, maxval=lim2, dtype=jnp.float32)
        return {'x': x, 'W1': W1, 'b1': b1, 'W2': W2, 'b2': b2}
    _L1_ffn_all = _L1_ffn_setup()
    _L1_ffn_in = {k: v for k, v in _L1_ffn_all.items() if k in ('W1', 'b1', 'W2', 'b2')}
    del _L1_ffn_all
    return {'x': x, 'L0_conv_weight_coord': _L0_conv_in['weight_coord'], 'L0_conv_radius': _L0_conv_in['radius'], 'L0_conv_weights': _L0_conv_in['weights'], 'L1_attn_w_attn': _L1_attn_in['w_attn'], 'L1_attn_w_proj': _L1_attn_in['w_proj'], 'L1_ffn_W1': _L1_ffn_in['W1'], 'L1_ffn_b1': _L1_ffn_in['b1'], 'L1_ffn_W2': _L1_ffn_in['W2'], 'L1_ffn_b2': _L1_ffn_in['b2']}

def reference(x, L0_conv_weight_coord, L0_conv_radius, L0_conv_weights, L1_attn_w_attn, L1_attn_w_proj, L1_ffn_W1, L1_ffn_b1, L1_ffn_W2, L1_ffn_b2):
    import jax
    import jax.numpy as jnp

    def _L0_conv_ref(x, weight_coord, radius, weights):
        import jax, jax.numpy as jnp
        import numpy as np
        from jax import lax
        PLANES = 96
        N_POINTS = 4
        KERNEL_SIZE = 11
        INIT_RADIUS = 2.0 * (2.0 / KERNEL_SIZE)

        def _make_kernels(weight_coord, radius, weights):
            K = KERNEL_SIZE
            lin = jnp.linspace(-1.0, 1.0, K)
            gy, gx = jnp.meshgrid(lin, lin, indexing='ij')
            kernel_coord = jnp.stack([gy, gx], axis=0).reshape(2, K * K)
            diff = weight_coord[:, :, None, :] - kernel_coord.T[None, None, :, :]
            diff = jnp.transpose(diff, (0, 1, 3, 2)).reshape(1, N_POINTS, 2, K, K)
            d = jax.nn.relu(1.0 - jnp.abs(diff).sum(axis=2) / radius)
            kernels = jnp.matmul(weights, d.reshape(1, N_POINTS, K * K)).reshape(PLANES, K, K)
            kernels = jnp.flip(jnp.transpose(kernels, (0, 2, 1)), axis=1)
            return kernels
        kernels = _make_kernels(weight_coord, radius, weights)
        pad = KERNEL_SIZE // 2
        out = lax.conv_general_dilated(x, kernels[:, None, :, :], window_strides=(1, 1), padding=[(pad, pad), (pad, pad)], dimension_numbers=('NCHW', 'OIHW', 'NCHW'), feature_group_count=PLANES)
        return out

    def _L1_attn_ref(x, w_attn, w_proj):
        import jax, jax.numpy as jnp
        import numpy as np
        N_EMBED = 96
        N_HEAD = 6
        HEAD_DIM = N_EMBED // N_HEAD
        ROPE_BASE = 10000.0

        def _rope_emb(T, head_dim):
            inv_freq = 1.0 / ROPE_BASE ** (jnp.arange(0, head_dim, 2, dtype=jnp.float32) / head_dim)
            t = jnp.arange(T, dtype=jnp.float32)
            freqs = t[:, None] * inv_freq[None, :]
            return jnp.repeat(freqs, 2, axis=1)

        def _apply_rope(x, emb):
            cos = jnp.cos(emb)[None, None]
            sin = jnp.sin(emb)[None, None]
            x2 = x.reshape(*x.shape[:-1], -1, 2)
            partner = jnp.stack([-x2[..., 1], x2[..., 0]], axis=-1).reshape(x.shape)
            return x * cos + partner * sin
        B, T, C = x.shape
        qkv = x @ w_attn
        q, k, v = jnp.split(qkv, 3, axis=-1)
        q = q.reshape(B, T, N_HEAD, HEAD_DIM).transpose(0, 2, 1, 3)
        k = k.reshape(B, T, N_HEAD, HEAD_DIM).transpose(0, 2, 1, 3)
        v = v.reshape(B, T, N_HEAD, HEAD_DIM).transpose(0, 2, 1, 3)
        emb = _rope_emb(T, HEAD_DIM)
        q = _apply_rope(q, emb)
        k = _apply_rope(k, emb)
        scale = HEAD_DIM ** (-0.5)
        wei = jnp.einsum('bhqd,bhkd->bhqk', q, k) * scale
        causal = jnp.tril(jnp.ones((T, T), dtype=bool))
        wei = jnp.where(causal[None, None], wei, -jnp.inf)
        wei = jax.nn.softmax(wei, axis=-1)
        out = jnp.einsum('bhqk,bhkd->bhqd', wei, v)
        out = out.transpose(0, 2, 1, 3).reshape(B, T, C)
        out = out @ w_proj
        return out

    def _L1_ffn_ref(x, W1, b1, W2, b2):
        import jax, jax.numpy as jnp
        import numpy as np
        NUM_GROUPS = 5
        EPS = 1e-05
        QB = 128.0

        def _binarize_weights_groupwise(W):
            n_out = W.shape[0]
            gs = n_out // NUM_GROUPS
            Wb = jnp.zeros_like(W)
            for g in range(NUM_GROUPS):
                wg = W[g * gs:(g + 1) * gs]
                z = wg - wg.mean()
                ste = z + jax.lax.stop_gradient(jnp.sign(z) - z)
                Wb = Wb.at[g * gs:(g + 1) * gs].set(ste)
            return Wb

        def _quantize_activations_groupwise(x):
            n = x.shape[0]
            gs = n // NUM_GROUPS
            xq = jnp.zeros_like(x)
            for g in range(NUM_GROUPS):
                ag = x[g * gs:(g + 1) * gs]
                gamma = jnp.max(jnp.abs(ag))
                xq = xq.at[g * gs:(g + 1) * gs].set(jnp.clip(ag * QB / (gamma + EPS), -QB + EPS, QB - EPS))
            return xq

        def _bitlinear(x, W, b):
            Wb = _binarize_weights_groupwise(W)
            y = jnp.einsum('btc,oc->bto', x, Wb) + b
            return _quantize_activations_groupwise(y)
        h = _bitlinear(x, W1, b1)
        h = jax.nn.gelu(h, approximate=False)
        out = _bitlinear(h, W2, b2)
        return out

    def _gn(v, G=32, eps=1e-05):
        B_, C_, H_, W_ = v.shape
        g = v.reshape(B_, G, C_ // G, H_, W_)
        m = jnp.mean(g, axis=(2, 3, 4), keepdims=True)
        s = jnp.var(g, axis=(2, 3, 4), keepdims=True)
        return ((g - m) / jnp.sqrt(s + eps)).reshape(v.shape)

    def _ln_c(v, eps=1e-06):
        m = jnp.mean(v, axis=1, keepdims=True)
        s = jnp.var(v, axis=1, keepdims=True)
        return (v - m) / jnp.sqrt(s + eps)

    def _ln_t(v, eps=1e-05):
        m = jnp.mean(v, axis=-1, keepdims=True)
        s = jnp.var(v, axis=-1, keepdims=True)
        return (v - m) / jnp.sqrt(s + eps)

    def _to_tokens(v):
        B_, C_, H_, W_ = v.shape
        return v.reshape(B_, C_, H_ * W_).transpose(0, 2, 1)

    def _from_tokens(t, like):
        B_, C_, H_, W_ = like.shape
        return t.transpose(0, 2, 1).reshape(B_, C_, H_, W_)
    x = x + _L0_conv_ref(_gn(x), L0_conv_weight_coord, L0_conv_radius, L0_conv_weights)
    t = _to_tokens(x)
    t = t + _L1_attn_ref(_ln_t(t), L1_attn_w_attn, L1_attn_w_proj)
    t = t + _L1_ffn_ref(_ln_t(t), L1_ffn_W1, L1_ffn_b1, L1_ffn_W2, L1_ffn_b2)
    x = _from_tokens(t, x)
    return x

_drawn_inputs = setup_inputs


def setup_inputs(seed=0):
    import zlib

    import numpy as np

    out = dict(_drawn_inputs(seed))
    spreads = {'L0_conv_radius': (0.3636363744735718, 0.6)}
    factors = {'L1_ffn_b1': 8.0, 'L1_ffn_b2': 8.0}
    for name, (base, spread) in spreads.items():
        noise = np.random.default_rng([zlib.crc32(name.encode()), seed]).standard_normal(out[name].shape)
        drawn = base * np.exp(spread * noise) if base else spread * noise
        out[name] = jnp.asarray(drawn.astype(out[name].dtype))
    for name, factor in factors.items():
        out[name] = (out[name] * factor).astype(out[name].dtype)
    return out
```

```python
from contextlib import ExitStack

import numpy as np

import concourse.bass as bass
from concourse import mybir

F32 = mybir.dt.float32
BF16 = mybir.dt.bfloat16
ALU = mybir.AluOpType
ACT = mybir.ActivationFunctionType
AX = mybir.AxisListType
ds = bass.ds

P = 128
B, C, SIDE = 16, 96, 16
T = SIDE * SIDE
NT = T // P
HEADS = 6
HD = C // HEADS
KSIZE = 11
POINTS = 4
PAIRS = B // 2
HID = 4 * C
HC = HID // P
QGROUPS = 5
GB = B // QGROUPS
GT = GB * T
HALF = GT // 2
BPAD = (QGROUPS + 1) * GB
GN_GROUP = 3
W1_ROWS = HID // QGROUPS
W2_ROWS = C // QGROUPS
GN_EPS, LN_EPS, Q_EPS, QB = 1e-5, 1e-5, 1e-5, 128.0
NEG = -1e30
SLOTS = [(0, 0), (0, 1), (0, 2), (1, 0), (1, 1), (2, 0)]
KROWS = len(SLOTS) * HD
RING = 4


def shape_constants():
    lin = np.linspace(-1.0, 1.0, KSIZE).astype(np.float32)
    pad = KSIZE // 2
    row = np.arange(P)
    ix, o = row % SIDE, np.arange(SIDE)
    dx = ix[:, None] - o[None] + pad
    gx = np.where((dx >= 0) & (dx < KSIZE), lin[np.clip(dx, 0, KSIZE - 1)], np.float32(1e30))
    gy = []
    for half in range(NT):
        iy = half * (P // SIDE) + row // SIDE
        dy = iy[:, None] - o[None] + pad
        gy.append(np.where((dy >= 0) & (dy < KSIZE), lin[np.clip(KSIZE - 1 - dy, 0, KSIZE - 1)], np.float32(1e30)))
    inv = (1.0 / np.float32(10000.0) ** (np.arange(0, HD, 2, dtype=np.float32) / np.float32(HD))).astype(np.float32)
    ang = np.repeat(np.arange(T, dtype=np.float32)[:, None] * inv[None], 2, axis=1)
    sign = np.where(np.arange(HD) % 2 == 0, -1.0, 1.0).astype(np.float32)
    lay = lambda t: np.tile(t.reshape(NT, P, 1, HD), (1, 1, 2 * HEADS, 1)).transpose(1, 0, 2, 3).reshape(P, -1)
    same = np.zeros((P, C), np.float32)
    c = np.arange(C)
    same[:C] = (c[:, None] // GN_GROUP == c[None] // GN_GROUP)
    parts = [gx, gy[0], gy[1], lay(np.cos(ang)), lay(np.sin(ang) * sign), same]
    return np.ascontiguousarray(np.concatenate([a.astype(np.float32) for a in parts], axis=1))


N_GRID = SIDE + NT * SIDE
N_ROPE = NT * 2 * C
O_COS, O_SIN, O_SAME = N_GRID, N_GRID + N_ROPE, N_GRID + 2 * N_ROPE
N_CONST = O_SAME + C


def build(nc, x, weight_coord, radius, conv_w, w_attn, w_proj, w1, b1, w2, b2, const, out):
    x_v = x.rearrange("b c h w -> c b (h w)")
    out_v = out.rearrange("b c h w -> c b (h w)")
    with ExitStack() as ctx:
        def sb(name, shape, dt=F32):
            return ctx.enter_context(nc.sbuf_tensor(name, shape, dt))

        def sem(name):
            return ctx.enter_context(nc.semaphore(name))

        x_ring = sb("x_ring", [C, 2, 2, T])
        xn_ring = sb("xn_ring", [C, 2, 2, T])
        tok = sb("tok", [P, BPAD, NT, C])
        xs_ring = sb("xs_ring", [P, 2, POINTS, NT, 2, C])
        toep = sb("toep", [P, POINTS, NT, SIDE, SIDE])
        cst = sb("cst", [P, N_CONST])
        wc_bc = sb("wc_bc", [P, POINTS * 2])
        rad_bc = sb("rad_bc", [P, POINTS])
        cw_bc = sb("cw_bc", [P, C, POINTS])
        grid_t = sb("grid_t", [P, POINTS, N_GRID])
        grid_n = sb("grid_n", [P, POINTS, N_GRID])
        nrinv = sb("nrinv", [P, 2, POINTS])
        ident = sb("ident", [P, P])
        ident16 = sb("ident16", [P, P], BF16)
        mask = sb("mask", [P, P])
        mask16 = sb("mask16", [P, P], BF16)
        ones = sb("ones", [P, P])
        mhalf = sb("mhalf", [P, BPAD * NT])
        gn_st = sb("gn_st", [C, B, 6])
        gn_mv = sb("gn_mv", [C, B, 2])
        gn_tmp = sb("gn_tmp", [C, 3, B])
        gn_mean = sb("gn_mean", [C, B])
        gn_rstd = sb("gn_rstd", [C, B])
        ln_st = sb("ln_st", [P, 2, 4, 6])
        ln_mv = sb("ln_mv", [P, 2, 4, 2])
        ln_var = sb("ln_var", [P, 2, 4])
        ln_rstd = sb("ln_rstd", [P, 2, 4])
        xl_ring = sb("xl_ring", [P, 2, 4, C])
        lt_ring = sb("lt_ring", [C, 2, 4 * P])
        wa = sb("wa", [C, 3 * C])
        wp = sb("wp", [C, C])
        qk_ring = sb("qk_ring", [P, 2, N_ROPE])
        rc_ring = sb("rc_ring", [P, 2, N_ROPE])
        rs_tmp = sb("rs_tmp", [P, N_ROPE])
        qr_ring = sb("qr_ring", [P, 2, N_ROPE])
        rest_ring = sb("rest_ring", [C, 2, 2, T])
        parts = sb("parts", [P, B * 3 * 2 * T], BF16)
        v_all = sb("v_all", [P, B, NT, C])
        stack = sb("stack", [P, RING, HEADS, 2, T], BF16)
        x_all = stack[0:C, :, :, :, :].rearrange("p r h s n -> p (r h s n)").bitcast(F32)[:, 0:B * T]
        x_all = x_all.rearrange("c (b n) -> c b n", b=B)
        v_ring = sb("v_ring", [P, 2, NT, HEADS, 2 * HD])
        pt_ring = sb("pt_ring", [P, 2, HEADS, T + P])
        nmax = sb("nmax", [P, 2, HEADS * NT])
        nmax_t = sb("nmax_t", [HEADS * NT, 2, P], BF16)
        o_ring = sb("o_ring", [C, 2, 2 * T])
        rsum = sb("rsum", [P, NT * HEADS])
        o_norm = sb("o_norm", [P, NT, C])
        ot_ring = sb("ot_ring", [C, 2, T])
        ln2_st = sb("ln2_st", [P, BPAD * NT, 6])
        ln2_mean = sb("ln2_mean", [P, BPAD * NT])
        ln2_tmp = sb("ln2_tmp", [P, 3, BPAD * NT])
        ln2_var = sb("ln2_var", [P, BPAD * NT])
        ln2_rstd = sb("ln2_rstd", [P, BPAD * NT])
        w1_in = sb("w1_in", [P, HC, C])
        w1_b = sb("w1_b", [C, HID])
        w2_in = sb("w2_in", [C, HID])
        w2_b = sb("w2_b", [P, HC, C])
        w_sum = sb("w_sum", [P, 2, QGROUPS])
        w_mean = sb("w_mean", [P, 2, QGROUPS])
        b1_s = sb("b1_s", [P, HC])
        b2_s = sb("b2_s", [C, 1])
        x2_ring = sb("x2_ring", [P, 2, GB * NT, C])
        amax1 = sb("amax1", [P, 2 * HC])
        amax2 = sb("amax2", [P, 2])
        gmax1 = sb("gmax1", [P, 4])
        gmax2 = sb("gmax2", [P, 4])
        lim1 = sb("lim1", [P, 4])
        lim2 = sb("lim2", [P, 4])

        parts_v = parts[0:C, :].rearrange("c (b s k n) -> c (b s) k n", b=B, s=2, k=3)
        wide = parts[:, :].bitcast(F32)
        n_y1 = 2 * HC * HALF
        y1_ring = wide[:, 0:2 * n_y1].rearrange("p (s n) -> p s n", s=2)
        h_ring = wide[:, 2 * n_y1:4 * n_y1].rearrange("p (s n) -> p s n", s=2)
        x2t_ring = wide[0:C, 4 * n_y1:4 * n_y1 + 2 * GT].rearrange("p (s n) -> p s n", s=2)
        y2_ring = wide[0:C, 4 * n_y1 + 2 * GT:4 * n_y1 + 4 * GT].rearrange("p (s n) -> p s n", s=2)
        flat = xs_ring[:, :, :, :, :, :].rearrange("p s q t b c -> p (s q t b c)")
        out_ring = flat[0:C, 0:2 * GT].rearrange("p (s n) -> p s n", s=2)
        t2_ring = flat[:, 2 * GT:2 * GT + 2 * GB * NT * C].rearrange("p (s n) -> p s n", s=2)

        bank = ctx.enter_context(nc.psum_tensor("bank", [P, 8, 512], F32))

        s_xall = [sem(f"s_xall{i}") for i in range(4)]
        s_small = sem("s_small")
        s_weights = sem("s_weights")
        s_xr = [sem(f"s_xr{i}") for i in range(2)]
        s_zero = sem("s_zero")
        s_ident = sem("s_ident")
        s_setup = sem("s_setup")
        s_id16 = sem("s_id16")
        s_vones = sem("s_vones")
        s_rinv = sem("s_rinv")
        s_grid = sem("s_grid")
        s_kones = sem("s_kones")
        s_grid2 = sem("s_grid2")
        s_cone = sem("s_cone")
        s_toep = sem("s_toep")
        s_gst = sem("s_gst")
        s_gmv = sem("s_gmv")
        s_gps = sem("s_gps")
        s_gdve = sem("s_gdve")
        s_grstd = sem("s_grstd")
        s_wtr = sem("s_wtr")
        s_wcopy = sem("s_wcopy")
        s_wsum = sem("s_wsum")
        s_wps = sem("s_wps")
        s_wmean = sem("s_wmean")
        s_wcen = sem("s_wcen")
        s_wsign = sem("s_wsign")
        s_wready = sem("s_wready")
        s_xn = sem("s_xn")
        s_xnt = sem("s_xnt")
        s_xs = sem("s_xs")
        s_cv = sem("s_cv")
        s_tok = sem("s_tok")
        s_lnst = sem("s_lnst")
        s_lnmv = sem("s_lnmv")
        s_lnvar = sem("s_lnvar")
        s_lnrstd = sem("s_lnrstd")
        s_xl = sem("s_xl")
        s_xlt = sem("s_xlt")
        s_lt = sem("s_lt")
        s_qkv = sem("s_qkv")
        s_qk = sem("s_qk")
        s_rcos = sem("s_rcos")
        s_rsin = sem("s_rsin")
        s_rope = sem("s_rope")
        s_qkt = sem("s_qkt")
        s_p0 = sem("s_p0")
        s_rest = sem("s_rest")
        s_p1 = sem("s_p1")
        s_p2 = sem("s_p2")
        s_stack = [sem(f"s_stack{i}") for i in range(RING)]
        s_mrow = [sem(f"s_mrow{i}") for i in range(RING)]
        s_sq = sem("s_sq")
        s_max = sem("s_max")
        s_mt = sem("s_mt")
        s_mtc = sem("s_mtc")
        s_sk = sem("s_sk")
        s_exp = sem("s_exp")
        s_sel = sem("s_sel")
        s_v = sem("s_v")
        s_pv = sem("s_pv")
        s_o = sem("s_o")
        s_otr = sem("s_otr")
        s_rsum = sem("s_rsum")
        s_on = sem("s_on")
        s_ont = sem("s_ont")
        s_ontc = sem("s_ontc")
        s_proj = sem("s_proj")
        s_res = sem("s_res")
        s_l2st = sem("s_l2st")
        s_l2mv = sem("s_l2mv")
        s_l2var = sem("s_l2var")
        s_l2rstd = sem("s_l2rstd")
        s_t2 = [sem(f"s_t2{i}") for i in range(2)]
        s_x2 = sem("s_x2")
        s_x2t = sem("s_x2t")
        s_x2c = sem("s_x2c")
        s_f1 = sem("s_f1")
        s_y1 = sem("s_y1")
        s_am1 = sem("s_am1")
        s_gm1 = sem("s_gm1")
        s_ar1 = sem("s_ar1")
        s_bd1 = sem("s_bd1")
        s_sc1 = sem("s_sc1")
        s_clip1 = sem("s_clip1")
        s_h = sem("s_h")
        s_f2 = sem("s_f2")
        s_y2 = sem("s_y2")
        s_am2 = sem("s_am2")
        s_gm2 = sem("s_gm2")
        s_ar2 = sem("s_ar2")
        s_bd2 = sem("s_bd2")
        s_sc2 = sem("s_sc2")
        s_clip2 = sem("s_clip2")
        s_t2t = sem("s_t2t")
        s_out = sem("s_out")
        s_store = [sem(f"s_store{i}") for i in range(2)]

        block = ctx.enter_context(nc.Block())

        def wait(eng, semaphore, count):
            if isinstance(count, int) and count <= 0:
                return
            eng.wait_ge(semaphore, count)

        def wait_apart(eng, semaphore, count):
            if not isinstance(count, int):
                eng.compute_val(count)
            eng.wait_ge(s_ident, 1)
            wait(eng, semaphore, count)

        def run(eng, step, first, unroll, laps, last):
            for n in range(first):
                step(0, n)
            with eng.Fori(0, laps) as i:
                for u in range(unroll):
                    step(i, first + u)
            for n in range(first + unroll * laps, last):
                step(0, n)

        A = dict(first=2, unroll=2, laps=2, last=PAIRS + 2)
        BB = dict(first=2, unroll=RING, laps=3, last=B + 1)
        CC = dict(first=1, unroll=2, laps=2, last=QGROUPS + 1)

        @block.sync
        def _(sp):
            sp.dma_start(cst[:], const).then_inc(s_small, 16)
            sp.dma_start(x_all[:, 0:4, :], x_v[:, 0:4, :]).then_inc(s_xall[0], 16)
            sp.dma_start(x_all[:, 8:12, :], x_v[:, 8:12, :]).then_inc(s_xall[2], 16)
            for k in range(2):
                sp.dma_start(x_ring[:, k, :, :], x_v[:, 2 * k:2 * k + 2, :]).then_inc(s_xr[k], 16)
            sp.dma_start(wa[:], w_attn).then_inc(s_weights, 16)
            sp.dma_start(wp[:], w_proj).then_inc(s_weights, 16)

            def load_x(i, n0):
                wait(sp, s_cv, n0 - 1 + 2 * i)
                b = 2 * n0 + 4 * i
                sp.dma_start(x_ring[:, n0 % 2, :, :], x_v[:, ds(b, 2), :]).then_inc(s_xr[n0 % 2], 16)
            with sp.Fori(0, PAIRS // 2 - 1) as i:
                for u in range(2):
                    load_x(i, 2 + u)

            def stack_image(i, n0):
                b, slot = n0 + RING * i, n0 % RING
                wait_apart(sp, s_p0, b + 1)
                wait(sp, s_p1, b + 1)
                wait(sp, s_p2, b + 1)
                wait(sp, s_sk, 3 * (b - RING + 1))
                for r, (kp, qp) in enumerate(SLOTS):
                    q_part = parts[0:C, ds((b * 6 + qp) * T, T)]
                    src = bass.AP(q_part.tensor, q_part.offset, [q_part.ap[0], [(3 + kp - qp) * T, 2], [1, T]])
                    dst = stack[r * HD:(r + 1) * HD, slot, :, :, :].rearrange("d h s n -> d (h s n)")
                    sp.dma_start(dst, src).then_inc(s_stack[slot], 16)

            def max_row(i, n0):
                b, slot = n0 + RING * i, n0 % RING
                wait(sp, s_mtc, b + 1)
                for t in range(NT):
                    dst = stack[KROWS:KROWS + 1, slot, :, 0, t * P:(t + 1) * P]
                    sp.dma_start(dst, nmax_t[t * HEADS:(t + 1) * HEADS, n0 % 2, :]).then_inc(s_mrow[slot], 16)

            for n in range(3):
                stack_image(0, n)
            max_row(0, 0)

            def step_b(i, n0):
                if n0 + 1 < B:
                    max_row(i, n0 + 1)
                if n0 + 3 < B:
                    stack_image(i, n0 + 3)
            run(sp, step_b, first=1, unroll=RING, laps=3, last=B + 1)

            def load_t2(i, n0):
                g = n0 + 2 * i
                wait(sp, s_t2t, g - 1)
                wait(sp, s_x2, g - 1)
                src = tok[:, ds(g * GB, GB), :, :].rearrange("p b t c -> p (b t c)")
                sp.dma_start(t2_ring[:, n0 % 2, :], src).then_inc(s_t2[n0 % 2], 16)

            sp.wait_ge(s_l2st, B)

            def store(i, n0):
                g = n0 + 2 * i
                sp.wait_ge(s_out, g + 1)
                sp.dma_start(out_v[:, ds(g * GB, GB), :],
                             out_ring[:, n0 % 2, :].rearrange("c (b n) -> c b n", b=GB)).then_inc(s_store[n0 % 2], 16)

            load_t2(0, 0)
            load_t2(0, 1)

            def step_c(i, n0):
                if 1 <= n0 < QGROUPS:
                    load_t2(i, n0 + 1)
                if n0 >= 1:
                    store(i, n0 - 1)
            run(sp, step_c, **CC)
            sp.wait_ge(s_out, QGROUPS + 1)
            sp.dma_start(out_v[:, B - 1, :], out_ring[:, 1, 0:T]).then_inc(s_store[1], 16)
            sp.wait_ge(s_store[0], 16 * 3)
            sp.wait_ge(s_store[1], 16 * 3)

        @block.gpsimd
        def _(pool):
            nc.gpsimd.memset(ident[:], 0.0)
            nc.gpsimd.memset(mask[:], 0.0)
            nc.gpsimd.memset(mhalf[:], -0.5).then_inc(s_zero, 1)
            pool.wait_ge(s_zero, 1)
            nc.gpsimd.affine_select(out=ident[:], in_=ident[:], compare_op=ALU.not_equal, fill=1.0, base=0,
                                    pattern=[[-1, P]], channel_multiplier=1).then_inc(s_ident, 1)
            nc.gpsimd.affine_select(out=mask[:], in_=mask[:], compare_op=ALU.is_ge, fill=NEG, base=0,
                                    pattern=[[-1, P]], channel_multiplier=1)
            nc.gpsimd.memset(ones[:], 1.0).then_inc(s_setup, 1)
            pool.wait_ge(s_gdve, 4)
            nc.gpsimd.tensor_tensor(gn_rstd[:], gn_tmp[:, 2, :], mhalf[0:C, 0:B], ALU.pow).then_inc(s_grstd, 1)
            pool.wait_ge(s_grstd, 1)
            nc.gpsimd.memset(stack[KROWS:KROWS + 1, :, :, 1, :].rearrange("o r h n -> o (r h) n"), 1.0).then_inc(s_kones, 1)
            pool.wait_ge(s_kones, 1)
            nc.gpsimd.memset(tok[:, B:BPAD, :, :], 0.0)
            nc.gpsimd.memset(ln2_st[:, B * NT:BPAD * NT, :], 0.0)
            nc.gpsimd.memset(v_ring[:], 1.0).then_inc(s_vones, 1)

            def rope(i, n0, u):
                b = 2 * (n0 + 2 * i) + u
                wait(pool, s_qk, b + 1)
                wait(pool, s_rope, b)
                swapped = qk_ring[:, u, :].rearrange("p (n t) -> p n t", t=2)[:, :, ::-1]
                nc.gpsimd.tensor_tensor(rs_tmp[:].rearrange("p (n t) -> p n t", t=2), swapped,
                                        cst[:, O_SIN:O_SIN + N_ROPE].rearrange("p (n t) -> p n t", t=2),
                                        ALU.mult).then_inc(s_rsin, 1)
                wait(pool, s_rsin, b + 1)
                wait(pool, s_rcos, b + 1)
                wait(pool, s_qkt, b - 1)
                nc.gpsimd.tensor_tensor(qr_ring[:, u, :].rearrange("p (k d h) -> p k d h", h=HEADS, d=HD),
                                        rc_ring[:, u, :].rearrange("p (k h d) -> p k d h", h=HEADS, d=HD),
                                        rs_tmp[:].rearrange("p (k h d) -> p k d h", h=HEADS, d=HD),
                                        ALU.add).then_inc(s_rope, 1)

            def third(i, n0, u):
                b = 2 * (n0 + 2 * i) + u
                wait(pool, s_p1, b + 1)
                nc.gpsimd.tensor_tensor(parts_v[:, ds(2 * b, 2), 2, :], rest_ring[:, u], parts_v[:, ds(2 * b, 2), 1, :],
                                        ALU.subtract).then_inc(s_p2, 1)

            def step_a(i, n0):
                if 1 <= n0 <= PAIRS:
                    wait(pool, s_lnvar, n0 + 2 * i)
                    nc.gpsimd.tensor_tensor(ln_rstd[:, (n0 - 1) % 2, :], ln_var[:, (n0 - 1) % 2, :], mhalf[:, 0:4],
                                            ALU.pow).then_inc(s_lnrstd, 1)
                if n0 >= 2:
                    for u in range(2):
                        third(i, n0 - 2, u)
                if 1 <= n0 <= PAIRS:
                    for u in range(2):
                        rope(i, n0 - 1, u)
            run(pool, step_a, **A)

            def step_b(i, n0):
                if n0 >= B:
                    return
                for hp in range(3):
                    wait_apart(pool, s_exp, 3 * (n0 + RING * i) + hp + 1)
                    v = pt_ring[:, n0 % 2, 2 * hp:2 * hp + 2, 0:2 * P]
                    nc.gpsimd.affine_select(out=v, in_=v, compare_op=ALU.is_ge, fill=0.0, base=0,
                                            pattern=[[0, 2], [0, 2], [1, P]], channel_multiplier=-1).then_inc(s_sel, 1)
            run(pool, step_b, **BB)
            pool.wait_ge(s_l2var, 1)
            nc.gpsimd.tensor_tensor(ln2_rstd[:], ln2_var[:], mhalf[:], ALU.pow).then_inc(s_l2rstd, 1)

            def step_c(i, n0):
                g = n0 + 2 * i
                if n0 < QGROUPS:
                    wait_apart(pool, s_gm1, g + 1)
                    wait_apart(pool, s_sc1, g)
                    nc.gpsimd.partition_all_reduce(gmax1[:, 1:2], gmax1[:, 0:1], P,
                                                   bass.bass_isa.ReduceOp.max).then_inc(s_ar1, 1)
                    wait_apart(pool, s_sc1, g + 1)
                    for half in range(2):
                        y = y1_ring[:, n0 % 2, half * HC * HALF:(half + 1) * HC * HALF]
                        nc.gpsimd.tensor_scalar(y, y, lim1[:, 1:2], lim1[:, 2:3], ALU.min,
                                                ALU.max).then_inc(s_clip1, 1)
                if n0 >= 1:
                    wait_apart(pool, s_gm2, g)
                    nc.gpsimd.partition_all_reduce(gmax2[0:C, 1:2], gmax2[0:C, 0:1], C,
                                                   bass.bass_isa.ReduceOp.max).then_inc(s_ar2, 1)
            run(pool, step_c, **CC)

        @block.scalar
        def _(act):
            act.dma_start(wc_bc[:], weight_coord.rearrange("o p k -> o (p k)").broadcast_to([P, POINTS * 2])).then_inc(s_small, 16)
            act.dma_start(rad_bc[:], radius.rearrange("o p a b -> o (p a b)").broadcast_to([P, POINTS])).then_inc(s_small, 16)
            act.dma_start(cw_bc[:].rearrange("p c k -> p (c k)"),
                          conv_w.rearrange("o c k -> o (c k)").broadcast_to([P, C * POINTS])).then_inc(s_small, 16)
            act.dma_start(x_all[:, 4:8, :], x_v[:, 4:8, :]).then_inc(s_xall[1], 16)
            act.dma_start(x_all[:, 12:16, :], x_v[:, 12:16, :]).then_inc(s_xall[3], 16)
            act.dma_start(w1_in[:], w1.rearrange("(c p) k -> p c k", p=P)).then_inc(s_weights, 16)
            act.dma_start(w2_in[:], w2).then_inc(s_weights, 16)
            act.dma_start(b1_s[:], b1.rearrange("(c p) -> p c", p=P), allow_slow_non_contiguous=True).then_inc(s_weights, 16)
            act.dma_start(b2_s[:], b2.rearrange("(c o) -> c o", o=1), allow_slow_non_contiguous=True).then_inc(s_weights, 16)
            for p in range(POINTS):
                act.wait_ge(s_cone, p + 1)
                m = toep[:, p].rearrange("p t y x -> p (t y x)")
                nc.scalar.activation(m, m, ACT.Relu).then_inc(s_toep, 1)
            act.wait_ge(s_wtr, 1)
            nc.scalar.copy(w1_b[:], bank[0:C, 5, 0:HID]).then_inc(s_wcopy, 1)
            act.wait_ge(s_wtr, 2)
            nc.scalar.copy(w2_b[:].rearrange("p k c -> p (k c)"), bank[:, 7, 0:HC * C]).then_inc(s_wcopy, 1)

            def step_a(i, n0):
                j = n0 + 2 * i

                def first_parts(u):
                    b = 2 * (j - 2) + u
                    wait(act, s_qkt, b + 1)
                    nc.scalar.copy(parts_v[:, ds(2 * b, 2), 0, :], bank[0:C, 7, :].rearrange("c (s n) -> c s n", s=2)).then_inc(s_p0, 1)
                if n0 >= 2:
                    first_parts(0)
                if n0 < PAIRS:
                    act.wait_ge(s_cv, j + 1)
                    nc.scalar.copy(tok[:, ds(2 * j, 2), :, :],
                                   bank[:, 2 + n0 % 2, 0:NT * 2 * C].rearrange("p (t b c) -> p b t c", t=NT, b=2)
                                   ).then_inc(s_tok, 1)
                if 1 <= n0 <= PAIRS:
                    wait(act, s_xlt, j)
                    wait(act, s_qkv, 2 * j - 4)
                    nc.scalar.copy(lt_ring[:, (n0 - 1) % 2, :], bank[0:C, 4, :]).then_inc(s_lt, 1)
                if n0 >= 2:
                    first_parts(1)
                if 1 <= n0 <= PAIRS:
                    for u in range(2):
                        b = 2 * (j - 1) + u
                        wait(act, s_qkv, b + 1)
                        wait(act, s_rope, b - 1)
                        nc.scalar.copy(v_all[:, ds(b, 1), :, :].rearrange("p o t c -> p (o t) c"),
                                       bank[:, 5:7, 2 * C:3 * C])
                        nc.scalar.copy(qk_ring[:, u, :].rearrange("p (t c) -> p t c", t=NT),
                                       bank[:, 5:7, 0:2 * C]).then_inc(s_qk, 1)
            run(act, step_a, **A)
            act.wait_ge(s_wcen, 2)
            nc.scalar.activation(w1_b[:, 0:QGROUPS * W1_ROWS], w1_b[:, 0:QGROUPS * W1_ROWS], ACT.Sign)
            nc.scalar.activation(w2_b[:, :, 0:QGROUPS * W2_ROWS], w2_b[:, :, 0:QGROUPS * W2_ROWS],
                                 ACT.Sign).then_inc(s_wsign, 1)

            def max_out(i, n0):
                b = n0 + RING * i
                wait(act, s_mt, b + 1)
                prev = (n0 - 2) % RING
                wait(act, s_mrow[prev], 16 * NT * ((n0 - 2) // RING + i + 1))
                nc.scalar.copy(nmax_t[:, n0 % 2, :], bank[0:HEADS * NT, 5, 3 * P:4 * P]).then_inc(s_mtc, 1)

            max_out(0, 0)

            def step_b(i, n0):
                b = n0 + RING * i
                s = n0 % 2
                if n0 + 1 < B:
                    max_out(i, n0 + 1)

                def exps(hp):
                    act.wait_ge(s_sk, 3 * b + hp + 1)
                    wait(act, s_pv, b - 1)
                    nc.scalar.activation(pt_ring[:, s, 2 * hp:2 * hp + 2, :], bank[:, 3:5, 0:T + P], ACT.Exp,
                                         scale=float(HD) ** -0.5).then_inc(s_exp, 1)
                if n0 < B:
                    exps(0)
                    nc.scalar.copy(v_ring[:, s, :, :, 0:HD].rearrange("p t h d -> p (t h) d"),
                                   v_all[:, ds(b, 1), :, :].rearrange("p o t (h d) -> p (o t h) d", d=HD)
                                   ).then_inc(s_v, 1)
                if n0 >= 1:
                    wait(act, s_pv, b)
                    wait(act, s_otr, b - 2)
                    nc.scalar.copy(o_ring[:, 1 - s, :], bank[0:C, 7, :]).then_inc(s_o, 1)
                if n0 < B:
                    exps(1)
                    exps(2)
                if n0 >= 1:
                    wait(act, s_ont, b)
                    wait(act, s_proj, b - 2)
                    nc.scalar.copy(ot_ring[:, 1 - s, :], bank[0:C, 6, 0:T]).then_inc(s_ontc, 1)
            act.wait_ge(s_vones, 1)
            run(act, step_b, **BB)

            def step_c(i, n0):
                g, s = n0 + 2 * i, n0 % 2
                if n0 < QGROUPS:
                    for half in range(2):
                        act.wait_ge(s_x2t, 2 * g + half + 1)
                        wait(act, s_f1, 6 * (g - 1))
                        nc.scalar.copy(x2t_ring[:, s, half * HALF:(half + 1) * HALF],
                                       bank[0:C, half, 0:HALF]).then_inc(s_x2c, 1)
                    for r in range(2 * HC):
                        act.wait_ge(s_f1, 6 * g + r + 1)
                        wait(act, s_h, 2 * (g - 1))
                        nc.scalar.activation(y1_ring[:, s, r * HALF:(r + 1) * HALF], bank[:, 2 + r % 2, 0:HALF],
                                             ACT.Identity, bias=b1_s[:, r % HC:r % HC + 1]).then_inc(s_y1, 1)
                if n0 >= 1:
                    for half in range(2):
                        act.wait_ge(s_f2, 2 * (g - 1) + half + 1)
                        wait(act, s_out, g - 1)
                        nc.scalar.activation(y2_ring[:, 1 - s, half * HALF:(half + 1) * HALF],
                                             bank[0:C, 4 + half, 0:HALF], ACT.Identity,
                                             bias=b2_s[:, 0:1]).then_inc(s_y2, 1)
                if n0 < QGROUPS:
                    for half in range(2):
                        act.wait_ge(s_clip1, 2 * g + half + 1)
                        wait(act, s_f2, 2 * (g - 1))
                        cols = slice(half * HC * HALF, (half + 1) * HC * HALF)
                        nc.scalar.activation(h_ring[:, s, cols], y1_ring[:, s, cols], ACT.Gelu,
                                             scale=lim1[:, 0:1]).then_inc(s_h, 1)
            run(act, step_c, **CC)

        @block.vector
        def _(dve):
            dve.wait_ge(s_small, 16 * 4)
            nc.vector.reciprocal(nrinv[:, 0, :], rad_bc[:])
            for p in range(POINTS):
                for k, cols in enumerate((slice(0, SIDE), slice(SIDE, N_GRID))):
                    at = wc_bc[:, 2 * p + k:2 * p + k + 1]
                    nc.vector.tensor_scalar(grid_t[:, p, cols], cst[:, cols], at, None, ALU.subtract)
                    last = nc.vector.tensor_scalar(grid_n[:, p, cols], cst[:, cols], at, -1.0, ALU.subtract, ALU.mult)
            last.then_inc(s_grid, 1)
            dve.wait_ge(s_grid, 1)
            nc.vector.tensor_tensor(grid_t[:], grid_t[:], grid_n[:], ALU.max).then_inc(s_grid, 1)
            nc.vector.tensor_scalar(nrinv[:, 1, :], nrinv[:, 0, :], -1.0, None, ALU.mult).then_inc(s_rinv, 1)
            dve.wait_ge(s_rinv, 1)
            dve.wait_ge(s_grid, 2)
            for p in range(POINTS):
                nc.vector.tensor_scalar(grid_t[:, p, 0:SIDE], grid_t[:, p, 0:SIDE], nrinv[:, 1, p:p + 1], None,
                                        ALU.mult)
                nc.vector.tensor_scalar(grid_t[:, p, SIDE:N_GRID], grid_t[:, p, SIDE:N_GRID],
                                        nrinv[:, 1, p:p + 1], 1.0, ALU.mult, ALU.add).then_inc(s_grid2, 1)
            for p in range(POINTS):
                dve.wait_ge(s_grid2, p + 1)
                gx = grid_t[:, p, 0:SIDE].unsqueeze(1).broadcast_to([P, NT * SIDE, SIDE])
                gy = grid_t[:, p, SIDE:N_GRID].unsqueeze(2).broadcast_to([P, NT * SIDE, SIDE])
                nc.vector.tensor_tensor(toep[:, p].rearrange("p t y x -> p (t y) x"), gx, gy,
                                        ALU.add).then_inc(s_cone, 1)

            for b in range(B):
                if b % 4 == 0:
                    dve.wait_ge(s_xall[b // 4], 16)
                nc.vector.bn_stats(gn_st[:, b, :], x_all[:, b, :]).then_inc(s_gst, 1)
            for b in range(B):
                dve.wait_ge(s_gst, b + 1)
                last = nc.vector.bn_aggr(gn_mv[:, b, :], gn_st[:, b, :])
            last.then_inc(s_gmv, 1)
            dve.wait_ge(s_gps, 1)
            nc.vector.tensor_scalar(gn_mean[:], bank[0:C, 4, 0:B], 1.0 / GN_GROUP, None, ALU.mult).then_inc(s_gdve, 1)
            dve.wait_ge(s_gdve, 1)
            nc.vector.tensor_tensor(gn_tmp[:, 0, :], gn_mv[:, :, 0], gn_mean[:], ALU.subtract).then_inc(s_gdve, 1)
            dve.wait_ge(s_gdve, 2)
            nc.vector.tensor_tensor(gn_tmp[:, 1, :], gn_tmp[:, 0, :], gn_tmp[:, 0, :], ALU.mult).then_inc(s_rinv, 1)
            dve.wait_ge(s_rinv, 2)
            nc.vector.tensor_tensor(gn_tmp[:, 0, :], gn_tmp[:, 1, :], gn_mv[:, :, 1], ALU.add).then_inc(s_gdve, 1)
            dve.wait_ge(s_gps, 2)
            nc.vector.tensor_scalar(gn_tmp[:, 2, :], bank[0:C, 4, B:2 * B], 1.0 / GN_GROUP, GN_EPS, ALU.mult,
                                    ALU.add).then_inc(s_gdve, 1)
            dve.wait_ge(s_setup, 1)
            nc.vector.tensor_copy(mask16[:], mask[:])
            nc.vector.tensor_copy(ident16[:], ident[:]).then_inc(s_id16, 1)

            def normalise(i, n0):
                j = n0 + 2 * i
                s = n0 % 2
                dve.wait_ge(s_xr[s], 16 * (n0 // 2 + i + 1))
                wait(dve, s_xnt, j - 1)
                for u in range(2):
                    b = 2 * j + u
                    last = nc.vector.tensor_scalar(xn_ring[:, s, u, :], x_ring[:, s, u, :], gn_mean[:, ds(b, 1)],
                                                   gn_rstd[:, ds(b, 1)], ALU.subtract, ALU.mult)
                last.then_inc(s_xn, 1)

            def weigh(i, n0):
                j, s = n0 + 2 * i, n0 % 2
                dve.wait_ge(s_xnt, j + 1)
                wait(dve, s_cv, j - 1)
                src = bank[:, s, 0:NT * 2 * C].rearrange("p (k c) -> p k c", c=C)
                for p in range(POINTS):
                    w = cw_bc[:, :, p].unsqueeze(1).broadcast_to([P, NT * 2, C])
                    last = nc.vector.tensor_tensor(xs_ring[:, s, p].rearrange("p t b c -> p (t b) c"), src, w, ALU.mult)
                last.then_inc(s_xs, 1)

            dve.wait_ge(s_grstd, 1)
            normalise(0, 0)
            normalise(0, 1)
            weigh(0, 0)

            dve.wait_ge(s_wcopy, 1)
            nc.vector.tensor_reduce(w_sum[0:C, 0, :], w1_b[:, 0:QGROUPS * W1_ROWS].rearrange(
                "c (g r) -> c g r", g=QGROUPS), op=ALU.add, axis=AX.X).then_inc(s_wsum, 1)
            dve.wait_ge(s_wcopy, 2)
            nc.vector.tensor_reduce(w_sum[:, 1, :], w2_b[:, :, 0:QGROUPS * W2_ROWS].rearrange(
                "p k (g r) -> p g k r", g=QGROUPS), op=ALU.add, axis=AX.XY).then_inc(s_wsum, 1)

            def step_a(i, n0):
                j = n0 + 2 * i
                if 2 <= n0 <= PAIRS + 1:
                    for u in range(2):
                        b = 2 * (j - 2) + u
                        dve.wait_ge(s_qk, b + 1)
                        wait(dve, s_rope, 2 * (j - 2))
                        nc.vector.tensor_tensor(rc_ring[:, u, :], qk_ring[:, u, :], cst[:, O_COS:O_COS + N_ROPE],
                                                ALU.mult).then_inc(s_rcos, 1)
                if 1 <= n0 <= PAIRS:
                    s = (n0 - 1) % 2
                    wait_apart(dve, s_tok, j)
                    for t in range(4):
                        nc.vector.bn_stats(ln_st[:, s, t, :], tok[:, ds(2 * (j - 1) + t // 2, 1), t % 2, :]
                                           .rearrange("p o c -> p (o c)")).then_inc(s_lnst, 1)
                    wait_apart(dve, s_lnst, 4 * j)
                    for t in range(4):
                        last = nc.vector.bn_aggr(ln_mv[:, s, t, :], ln_st[:, s, t, :])
                    last.then_inc(s_lnmv, 1)
                    dve.wait_ge(s_lnmv, j)
                    nc.vector.tensor_scalar(ln_var[:, s, :], ln_mv[:, s, :, 1], LN_EPS, None,
                                            ALU.add).then_inc(s_lnvar, 1)
                if n0 + 1 < PAIRS:
                    weigh(i, n0 + 1)
                if 1 <= n0 <= PAIRS:
                    s = (n0 - 1) % 2
                    dve.wait_ge(s_lnrstd, j)
                    wait(dve, s_xlt, j - 2)
                    for t in range(4):
                        last = nc.vector.tensor_scalar(
                            xl_ring[:, s, t, :], tok[:, ds(2 * (j - 1) + t // 2, 1), t % 2, :].rearrange(
                                "p o c -> p (o c)"), ln_mv[:, s, t, 0:1], ln_rstd[:, s, t:t + 1],
                            ALU.subtract, ALU.mult)
                    last.then_inc(s_xl, 1)
                if n0 + 2 < PAIRS:
                    normalise(i, n0 + 2)
                if n0 >= 2:
                    for u in range(2):
                        b = 2 * (j - 2) + u
                        dve.wait_ge(s_p0, b + 1)
                        wait(dve, s_p2, 2 * (j - 2))
                        nc.vector.tensor_tensor(rest_ring[:, u], bank[0:C, 7, :].rearrange("c (s n) -> c s n", s=2),
                                                parts_v[:, ds(2 * b, 2), 0, :], ALU.subtract).then_inc(s_rest, 1)
                        dve.wait_ge(s_rest, b + 1)
                        nc.vector.tensor_copy(parts_v[:, ds(2 * b, 2), 1, :], rest_ring[:, u]).then_inc(s_p1, 1)
            run(dve, step_a, **A)

            dve.wait_ge(s_wps, 1)
            nc.vector.tensor_scalar(w_mean[0:C, 0, :], bank[0:C, 7, 0:QGROUPS], 1.0 / (W1_ROWS * C), None, ALU.mult)
            nc.vector.tensor_scalar(w_mean[:, 1, :], bank[:, 7, QGROUPS:2 * QGROUPS], 1.0 / (W2_ROWS * HID), None,
                                    ALU.mult).then_inc(s_wmean, 1)
            dve.wait_ge(s_wmean, 1)
            v1 = w1_b[:, 0:QGROUPS * W1_ROWS].rearrange("c (g r) -> c g r", g=QGROUPS)
            nc.vector.tensor_tensor(v1, v1, w_mean[0:C, 0, :].unsqueeze(2).broadcast_to([C, QGROUPS, W1_ROWS]),
                                    ALU.subtract).then_inc(s_wcen, 1)
            for k in range(HC):
                v2 = w2_b[:, k, 0:QGROUPS * W2_ROWS].rearrange("p (g r) -> p g r", g=QGROUPS)
                last = nc.vector.tensor_tensor(
                    v2, v2, w_mean[:, 1, :].unsqueeze(2).broadcast_to([P, QGROUPS, W2_ROWS]), ALU.subtract)
            last.then_inc(s_wcen, 1)
            nc.vector.memset(w1_b[:, QGROUPS * W1_ROWS:HID], 0.0)
            nc.vector.memset(w2_b[:, :, QGROUPS * W2_ROWS:C], 0.0).then_inc(s_wready, 1)

            def maxima(i, n0, h):
                b = n0 + RING * i
                dve.wait_ge(s_sq, HEADS * b + h + 1)
                if h == 0:
                    wait(dve, s_mt, b - 1)
                for t in range(NT):
                    first = t * P
                    last = nc.vector.tensor_reduce(nmax[:, n0 % 2, HEADS * t + h:HEADS * t + h + 1],
                                                   bank[:, h % 3, first:first + (t + 1) * P],
                                                   op=ALU.max, axis=AX.X, negate=True)
                last.then_inc(s_max, 1)

            for n in range(2):
                for h in range(HEADS):
                    maxima(0, n, h)

            def step_b(i, n0):
                b = n0 + RING * i
                if n0 + 2 < B:
                    for h in range(4):
                        maxima(i, n0 + 2, h)
                if n0 >= 1:
                    dve.wait_ge(s_otr, b)
                    o = bank[:, 5, 0:4 * C].rearrange("p (n k) -> p n k", k=2 * HD)
                    nc.vector.reciprocal(rsum[:], o[:, :, HD]).then_inc(s_rsum, 1)
                    dve.wait_ge(s_rsum, b)
                    wait(dve, s_ont, b - 1)
                    nc.vector.tensor_tensor(o_norm[:].rearrange("p t (h d) -> p (t h) d", d=HD), o[:, :, 0:HD],
                                            rsum[:].unsqueeze(2).broadcast_to([P, NT * HEADS, HD]),
                                            ALU.mult).then_inc(s_on, 1)
                if n0 + 2 < B:
                    for h in range(4, HEADS):
                        maxima(i, n0 + 2, h)
                if n0 >= 1:
                    dve.wait_ge(s_proj, b)
                    t_b = tok[:, ds(b - 1, 1), :, :].rearrange("p o t c -> p (o t) c")
                    nc.vector.tensor_tensor(t_b, bank[:, 6, T:T + NT * C].rearrange("p (t c) -> p t c", t=NT), t_b,
                                            ALU.add).then_inc(s_res, 1)
                    wait_apart(dve, s_res, b)
                    for t in range(NT):
                        last = nc.vector.bn_stats(
                            ln2_st[:, ds(2 * (b - 1) + t, 1), :].rearrange("p o k -> p (o k)"),
                            tok[:, ds(b - 1, 1), t, :].rearrange("p o c -> p (o c)"))
                    last.then_inc(s_l2st, 1)
            run(dve, step_b, **BB)

            dve.wait_ge(s_l2st, B)
            nc.vector.tensor_tensor(ln2_mean[:], ln2_st[:, :, 1], ln2_st[:, :, 4], ALU.add)
            nc.vector.tensor_tensor(ln2_tmp[:, 0, :], ln2_st[:, :, 1], ln2_st[:, :, 4], ALU.subtract)
            nc.vector.tensor_tensor(ln2_tmp[:, 1, :], ln2_st[:, :, 2], ln2_st[:, :, 5], ALU.add).then_inc(s_l2mv, 1)
            dve.wait_ge(s_l2mv, 1)
            nc.vector.tensor_scalar(ln2_mean[:], ln2_mean[:], 0.5, None, ALU.mult)
            nc.vector.tensor_scalar(ln2_tmp[:, 1, :], ln2_tmp[:, 1, :], 1.0 / C, LN_EPS, ALU.mult, ALU.add)
            nc.vector.scalar_tensor_tensor(ln2_tmp[:, 2, :], ln2_tmp[:, 0, :], 0.25, ln2_tmp[:, 0, :], ALU.mult,
                                           ALU.mult).then_inc(s_l2mv, 1)
            dve.wait_ge(s_l2mv, 2)
            nc.vector.tensor_tensor(ln2_var[:], ln2_tmp[:, 1, :], ln2_tmp[:, 2, :], ALU.add).then_inc(s_l2var, 1)

            def second_norm(i, n0):
                g, s = n0 + 2 * i, n0 % 2
                dve.wait_ge(s_t2[s], 16 * (n0 // 2 + i + 1))
                wait(dve, s_x2t, 2 * (g - 1))
                for t in range(GB * NT):
                    k = GB * NT * g + t
                    last = nc.vector.tensor_scalar(x2_ring[:, s, t, :], t2_ring[:, s, t * C:(t + 1) * C],
                                                   ln2_mean[:, ds(k, 1)],
                                                   ln2_rstd[:, ds(k, 1)], ALU.subtract, ALU.mult)
                last.then_inc(s_x2, 1)

            def bounds(gmax, lim, signal, count):
                nc.vector.tensor_scalar(gmax[:, 2:3], gmax[:, 1:2], Q_EPS, None, ALU.add).then_inc(signal[0], 1)
                dve.wait_ge(signal[0], 3 * count - 2)
                nc.vector.reciprocal(gmax[:, 3:4], gmax[:, 2:3]).then_inc(signal[0], 1)
                top = (QB - Q_EPS) / QB
                nc.vector.tensor_scalar(lim[:, 1:2], gmax[:, 2:3], top, None, ALU.mult)
                nc.vector.tensor_scalar(lim[:, 2:3], gmax[:, 2:3], -top, None, ALU.mult).then_inc(signal[0], 1)
                dve.wait_ge(signal[0], 3 * count)
                nc.vector.tensor_scalar(lim[:, 0:1], gmax[:, 3:4], QB, None, ALU.mult).then_inc(signal[1], 1)

            dve.wait_ge(s_l2rstd, 1)
            second_norm(0, 0)

            def step_c(i, n0):
                g, s = n0 + 2 * i, n0 % 2
                if n0 < QGROUPS:
                    for r in range(2 * HC):
                        dve.wait_ge(s_y1, 2 * HC * g + r + 1)
                        last = nc.vector.tensor_reduce(amax1[:, r:r + 1], y1_ring[:, s, r * HALF:(r + 1) * HALF],
                                                       op=ALU.max, axis=AX.X, apply_absolute_value=True)
                    last.then_inc(s_am1, 1)
                    dve.wait_ge(s_am1, g + 1)
                    nc.vector.tensor_reduce(gmax1[:, 0:1], amax1[:], op=ALU.max, axis=AX.X).then_inc(s_gm1, 1)
                    dve.wait_ge(s_ar1, g + 1)
                    wait(dve, s_h, 2 * g)
                    bounds(gmax1[:, :], lim1, (s_bd1, s_sc1), g + 1)
                if n0 < QGROUPS:
                    second_norm(i, n0 + 1)
                if n0 >= 1:
                    y = y2_ring[:, 1 - s, :]
                    for half in range(2):
                        dve.wait_ge(s_y2, 2 * (g - 1) + half + 1)
                        last = nc.vector.tensor_reduce(amax2[0:C, half:half + 1], y[:, half * HALF:(half + 1) * HALF],
                                                       op=ALU.max, axis=AX.X, apply_absolute_value=True)
                    last.then_inc(s_am2, 1)
                    dve.wait_ge(s_am2, g)
                    nc.vector.tensor_reduce(gmax2[0:C, 0:1], amax2[0:C, :], op=ALU.max, axis=AX.X).then_inc(s_gm2, 1)
                    dve.wait_ge(s_ar2, g)
                    bounds(gmax2[0:C, :], lim2[0:C, :], (s_bd2, s_sc2), g)
                    nc.vector.tensor_scalar(y, y, lim2[0:C, 1:2], lim2[0:C, 2:3], ALU.min, ALU.max).then_inc(s_clip2, 1)
                    dve.wait_ge(s_clip2, g)
                    dve.wait_ge(s_sc2, g)
                    dve.wait_ge(s_t2t, g)
                    wait(dve, s_store[1 - s], 16 * ((n0 - 3) // 2 + i + 1))
                    for half in range(2):
                        cols = slice(half * HALF, (half + 1) * HALF)
                        last = nc.vector.scalar_tensor_tensor(out_ring[:, 1 - s, cols], y[:, cols], lim2[0:C, 0:1],
                                                              bank[0:C, 6 + half, 0:HALF], ALU.mult, ALU.add)
                    last.then_inc(s_out, 1)
            run(dve, step_c, **CC)
            dve.wait_ge(s_t2t, QGROUPS + 1)
            dve.wait_ge(s_store[1], 16 * 2)
            nc.vector.tensor_copy(out_ring[:, 1, 0:T], bank[0:C, 4, 0:T]).then_inc(s_out, 1)

        @block.tensor
        def _(pe):
            pe.wait_ge(s_ident, 1)
            pe.wait_ge(s_weights, 16 * 6)
            for k in range(HC):
                last = nc.tensor.transpose(bank[0:C, 5, k * P:(k + 1) * P], w1_in[:, k, :], ident[:])
            last.then_inc(s_wtr, 1)
            for k in range(HC):
                last = nc.tensor.transpose(bank[:, 7, k * C:(k + 1) * C], w2_in[:, k * P:(k + 1) * P], ident[0:C, 0:C])
            last.then_inc(s_wtr, 1)
            same = cst[0:C, O_SAME:O_SAME + C]
            pe.wait_ge(s_small, 16 * 4)
            pe.wait_ge(s_gmv, 1)
            nc.tensor.matmul(bank[0:C, 4, 0:B], same, gn_mv[:, :, 0], start=True, stop=True).then_inc(s_gps, 1)
            pe.wait_ge(s_gdve, 3)
            nc.tensor.matmul(bank[0:C, 4, B:2 * B], same, gn_tmp[:, 0, :], start=True, stop=True).then_inc(s_gps, 1)

            def transpose_pair(i, n0):
                j, s = n0 + 2 * i, n0 % 2
                pe.wait_ge(s_xn, j + 1)
                wait(pe, s_xs, j - 1)
                for t in range(NT):
                    for u in range(2):
                        k = 2 * t + u
                        last = nc.tensor.transpose(bank[:, s, k * C:(k + 1) * C], xn_ring[:, s, u, t * P:(t + 1) * P],
                                                   ident[0:C, 0:C])
                last.then_inc(s_xnt, 1)

            def convolve(i, n0, t):
                s = n0 % 2
                dst = bank[:, 2 + s, t * 2 * C:(t + 1) * 2 * C]
                for k in range(NT):
                    for p in range(POINTS):
                        w = toep[:, p, k].rearrange("p y x -> p (y x)")[:, t * P:(t + 1) * P]
                        nc.tensor.matmul(dst, w, xs_ring[:, s, p, k].rearrange("p b c -> p (b c)"),
                                         start=(k == 0 and p == 0), stop=False)
                for u in range(2):
                    last = nc.tensor.matmul(dst[:, u * C:(u + 1) * C], x_ring[:, s, u, t * P:(t + 1) * P],
                                            ident[0:C, 0:C], start=False, stop=(u == 1))
                return last

            def transpose_qk(i, n0, u):
                b = 2 * (n0 + 2 * i) + u
                pe.wait_ge(s_rope, b + 1)
                wait(pe, s_rest, b)
                for side in range(2):
                    for t in range(NT):
                        last = nc.tensor.transpose(bank[0:C, 7, side * T + t * P:side * T + (t + 1) * P],
                                                   qr_ring[:, u, (2 * t + side) * C:(2 * t + side + 1) * C], ident[:])
                last.then_inc(s_qkt, 1)

            def project_qkv(i, n0, u):
                b = 2 * (n0 + 2 * i) + u
                wait(pe, s_qk, b)
                for t in range(NT):
                    last = nc.tensor.matmul(bank[:, 5 + t, 0:3 * C],
                                            lt_ring[:, n0 % 2, (2 * u + t) * P:(2 * u + t + 1) * P], wa[:],
                                            start=True, stop=True)
                last.then_inc(s_qkv, 1)

            transpose_pair(0, 0)
            pe.wait_ge(s_toep, POINTS)
            pe.wait_ge(s_wcopy, 2)

            def step_a(i, n0):
                j = n0 + 2 * i
                if n0 + 1 < PAIRS:
                    transpose_pair(i, n0 + 1)
                if n0 < PAIRS:
                    pe.wait_ge(s_xs, j + 1)
                    wait(pe, s_tok, j - 1)
                    convolve(i, n0, 0)
                if n0 >= 2:
                    transpose_qk(i, n0 - 2, 0)
                if n0 < PAIRS:
                    convolve(i, n0, 1).then_inc(s_cv, 1)
                if 1 <= n0 <= PAIRS:
                    pe.wait_ge(s_xl, j)
                    wait(pe, s_lt, j - 1)
                    for t in range(4):
                        last = nc.tensor.transpose(bank[0:C, 4, t * P:(t + 1) * P], xl_ring[:, (n0 - 1) % 2, t, :],
                                                   ident[:])
                    last.then_inc(s_xlt, 1)
                if n0 >= 2:
                    transpose_qk(i, n0 - 2, 1)
                if 1 <= n0 <= PAIRS:
                    pe.wait_ge(s_lt, j)
                    for u in range(2):
                        project_qkv(i, n0 - 1, u)
            run(pe, step_a, **A)

            pe.wait_ge(s_rest, B)
            pe.wait_ge(s_tok, PAIRS)
            pe.wait_ge(s_id16, 1)
            pe.wait_ge(s_vones, 1)
            pe.wait_ge(s_setup, 1)
            pe.wait_ge(s_wsum, 2)
            nc.tensor.matmul(bank[0:C, 7, 0:QGROUPS], ones[0:C, 0:C], w_sum[0:C, 0, :], start=True, stop=True)
            nc.tensor.matmul(bank[:, 7, QGROUPS:2 * QGROUPS], ones[:], w_sum[:, 1, :], start=True,
                             stop=True).then_inc(s_wps, 1)

            def scores_q(i, n0, h):
                b, slot = n0 + RING * i, n0 % RING
                if h == 0:
                    pe.wait_ge(s_stack[slot], 16 * len(SLOTS) * (n0 // RING + i + 1))
                wait(pe, s_max, HEADS * b + h - 2)
                for t in range(NT):
                    first, size = t * P, (t + 1) * P
                    nc.tensor.matmul(bank[:, h % 3, first:first + size],
                                     stack[0:KROWS, slot, h, 0, t * P:(t + 1) * P],
                                     stack[0:KROWS, slot, h, 1, 0:size], start=True, stop=False)
                    last = nc.tensor.matmul(bank[:, h % 3, first + t * P:first + size], ident16[:], mask16[:],
                                            start=False, stop=True)
                last.then_inc(s_sq, 1)

            def scores_k(i, n0, hp):
                b, slot = n0 + RING * i, n0 % RING
                if hp == 0:
                    pe.wait_ge(s_mrow[slot], 16 * NT * (n0 // RING + i + 1))
                wait(pe, s_exp, 3 * b + hp)
                for e in range(2):
                    h = 2 * hp + e
                    nc.tensor.matmul(bank[:, 3 + e, P:P + T], stack[0:KROWS + 1, slot, h, 1, 0:P],
                                     stack[0:KROWS + 1, slot, h, 0, :], start=True, stop=True)
                    last = nc.tensor.matmul(bank[:, 3 + e, 0:P], stack[0:KROWS + 1, slot, h, 1, P:T],
                                            stack[0:KROWS + 1, slot, h, 0, P:T], start=True, stop=True)
                last.then_inc(s_sk, 1)

            def transpose_max(i, n0):
                b = n0 + RING * i
                pe.wait_ge(s_max, HEADS * (b + 1))
                wait(pe, s_mtc, b)
                wait(pe, s_on, b - 2)
                nc.tensor.transpose(bank[0:HEADS * NT, 5, 3 * P:4 * P], nmax[:, n0 % 2, :], ident[:]).then_inc(s_mt, 1)

            def weighted_values(i, n0):
                b, s = n0 + RING * i, n0 % 2
                pe.wait_ge(s_sel, 3 * (b + 1))
                pe.wait_ge(s_v, b + 1)
                wait(pe, s_o, b)
                for g in range(2):
                    for t in range(NT):
                        for e in range(3):
                            h = 3 * g + e
                            rows = slice(2 * HD * e, 2 * HD * (e + 1))
                            w = v_ring[:, s, t, h, :]
                            if t == 0:
                                nc.tensor.matmul(bank[rows, 7, g * T:(g + 1) * T], w, pt_ring[:, s, h, P:P + T],
                                                 start=True, stop=False)
                            else:
                                last = nc.tensor.matmul(bank[rows, 7, g * T + P:(g + 1) * T], w,
                                                        pt_ring[:, s, h, 0:P], start=False, stop=True)
                last.then_inc(s_pv, 1)

            def transpose_o(i, n0):
                b, s = n0 + RING * i, n0 % 2
                pe.wait_ge(s_o, b + 1)
                wait(pe, s_mtc, b + 3 if n0 + 2 < B else B)
                wait(pe, s_on, b)
                for t in range(NT):
                    for g in range(2):
                        k = 2 * t + g
                        last = nc.tensor.transpose(bank[:, 5, k * C:(k + 1) * C],
                                                   o_ring[:, s, g * T + t * P:g * T + (t + 1) * P], ident[0:C, 0:C])
                last.then_inc(s_otr, 1)

            def transpose_norm(i, n0):
                b = n0 + RING * i
                pe.wait_ge(s_on, b + 1)
                wait(pe, s_res, b)
                for t in range(NT):
                    last = nc.tensor.transpose(bank[0:C, 6, t * P:(t + 1) * P], o_norm[:, t, :], ident[:])
                last.then_inc(s_ont, 1)

            def project_out(i, n0):
                b, s = n0 + RING * i, n0 % 2
                pe.wait_ge(s_ontc, b + 1)
                for t in range(NT):
                    last = nc.tensor.matmul(bank[:, 6, T + t * C:T + (t + 1) * C], ot_ring[:, s, t * P:(t + 1) * P],
                                            wp[:], start=True, stop=True)
                last.then_inc(s_proj, 1)

            for n in range(2):
                for h in range(HEADS):
                    scores_q(0, n, h)
            transpose_max(0, 0)
            pe.wait_ge(s_wmean, 1)

            def step_b(i, n0):
                if n0 + 1 < B:
                    transpose_max(i, n0 + 1)
                for hp in range(3):
                    if n0 < B:
                        scores_k(i, n0, hp)
                    if n0 + 2 < B:
                        for h in (2 * hp, 2 * hp + 1):
                            scores_q(i, n0 + 2, h)
                    if n0 >= 1 and hp == 0:
                        weighted_values(i, n0 - 1)
                    if n0 >= 1 and hp == 1:
                        transpose_o(i, n0 - 1)
                if n0 >= 1:
                    transpose_norm(i, n0 - 1)
                    project_out(i, n0 - 1)
            run(pe, step_b, **BB)

            pe.wait_ge(s_res, B)
            pe.wait_ge(s_wsign, 1)
            pe.wait_ge(s_wready, 1)

            def step_c(i, n0):
                g, s = n0 + 2 * i, n0 % 2

                def residual():
                    pe.wait_ge(s_t2[1 - s], 16 * ((n0 - 1) // 2 + i + 1))
                    wait(pe, s_out, g - 1)
                    for half in range(2):
                        for t in range(3):
                            k = 3 * half + t
                            last = nc.tensor.transpose(bank[0:C, 6 + half, t * P:(t + 1) * P],
                                                       t2_ring[:, 1 - s, k * C:(k + 1) * C], ident[:])
                    last.then_inc(s_t2t, 1)
                if n0 < QGROUPS:
                    pe.wait_ge(s_x2, g + 1)
                    for half in range(2):
                        wait(pe, s_x2c, 2 * (g - 1) + half + 1)
                        for t in range(3):
                            last = nc.tensor.transpose(bank[0:C, half, t * P:(t + 1) * P],
                                                       x2_ring[:, s, 3 * half + t, :], ident[:])
                        last.then_inc(s_x2t, 1)
                    for r in range(2 * HC):
                        half, k = r // HC, r % HC
                        if r == HC and n0 >= 1:
                            residual()
                        pe.wait_ge(s_x2c, 2 * g + half + 1)
                        wait(pe, s_y1, 2 * HC * g + r - 1)
                        nc.tensor.matmul(bank[:, 2 + r % 2, 0:HALF], w1_b[:, k * P:(k + 1) * P],
                                         x2t_ring[:, s, half * HALF:(half + 1) * HALF],
                                         start=True, stop=True).then_inc(s_f1, 1)
                elif n0 >= 1:
                    residual()
                if n0 >= 1:
                    for half in range(2):
                        pe.wait_ge(s_h, 2 * (g - 1) + half + 1)
                        wait(pe, s_y2, 2 * (g - 1))
                        for k in range(HC):
                            r = half * HC + k
                            last = nc.tensor.matmul(bank[0:C, 4 + half, 0:HALF], w2_b[:, k, :],
                                                    h_ring[:, 1 - s, r * HALF:(r + 1) * HALF],
                                                    start=(k == 0), stop=(k == HC - 1))
                        last.then_inc(s_f2, 1)
            run(pe, step_c, **CC)
            pe.wait_ge(s_t2[1], 16 * 3)
            pe.wait_ge(s_y2, 2 * QGROUPS)
            for t in range(NT):
                last = nc.tensor.transpose(bank[0:C, 4, t * P:(t + 1) * P], t2_ring[:, 1, t * C:(t + 1) * C], ident[:])
            last.then_inc(s_t2t, 1)


_INS = ["x", "L0_conv_weight_coord", "L0_conv_radius", "L0_conv_weights", "L1_attn_w_attn", "L1_attn_w_proj",
        "L1_ffn_W1", "L1_ffn_b1", "L1_ffn_W2", "L1_ffn_b2"]


def kernel(**inputs):
    import numpy as _np
    import concourse.bacc as _bacc
    from concourse import mybir as _mybir
    from concourse.bass_utils import run_bass_kernel_spmd as _run

    nc = _bacc.Bacc("TRN2", target_bir_lowering=False, num_devices=1)
    arrays, args = {}, []
    for name in _INS:
        a = _np.ascontiguousarray(inputs[name])
        arrays[f"in_{name}"] = a
        args.append(nc.dram_tensor(f"in_{name}", a.shape, _mybir.dt.from_np(a.dtype), kind="ExternalInput").ap())
    table = shape_constants()
    arrays["in_const"] = table
    args.append(nc.dram_tensor("in_const", table.shape, _mybir.dt.float32, kind="ExternalInput").ap())
    args.append(nc.dram_tensor("out_0", (B, C, SIDE, SIDE), _mybir.dt.float32, kind="ExternalOutput").ap())
    build(nc, *args)
    r = _run(nc, [arrays], core_ids=[0])
    return r.results[0]["out_0"]
```

```python
from contextlib import ExitStack

import numpy as np

import concourse.bass as bass
from concourse import mybir

F32 = mybir.dt.float32
BF16 = mybir.dt.bfloat16
ALU = mybir.AluOpType
ACT = mybir.ActivationFunctionType
AX = mybir.AxisListType
ds = bass.ds

P = 128
B, C, SIDE = 16, 96, 16
T = SIDE * SIDE
NT = T // P
HEADS = 6
HD = C // HEADS
KSIZE = 11
POINTS = 4
PAIRS = B // 2
HID = 4 * C
HC = HID // P
QGROUPS = 5
GB = B // QGROUPS
GT = GB * T
HALF = GT // 2
GN_GROUP = 3
W1_ROWS = HID // QGROUPS
W2_ROWS = C // QGROUPS
GN_EPS, LN_EPS, Q_EPS, QB = 1e-5, 1e-5, 1e-5, 128.0
NEG = -1e30
SLOTS = [(0, 0), (0, 1), (0, 2), (1, 0), (1, 1), (2, 0)]
KROWS = len(SLOTS) * HD
LN2_COLS = [slice(0, (QGROUPS - 1) * GB * NT), slice((QGROUPS - 1) * GB * NT, QGROUPS * GB * NT)]
RING = 4


def shape_constants():
    lin = np.linspace(-1.0, 1.0, KSIZE).astype(np.float32)
    pad = KSIZE // 2
    row = np.arange(P)
    ix, o = row % SIDE, np.arange(SIDE)
    dx = ix[:, None] - o[None] + pad
    gx = np.where((dx >= 0) & (dx < KSIZE), lin[np.clip(dx, 0, KSIZE - 1)], np.float32(1e30))
    gy = []
    for half in range(NT):
        iy = half * (P // SIDE) + row // SIDE
        dy = iy[:, None] - o[None] + pad
        gy.append(np.where((dy >= 0) & (dy < KSIZE), lin[np.clip(KSIZE - 1 - dy, 0, KSIZE - 1)], np.float32(1e30)))
    inv = (1.0 / np.float32(10000.0) ** (np.arange(0, HD, 2, dtype=np.float32) / np.float32(HD))).astype(np.float32)
    ang = np.repeat(np.arange(T, dtype=np.float32)[:, None] * inv[None], 2, axis=1)
    sign = np.where(np.arange(HD) % 2 == 0, -1.0, 1.0).astype(np.float32)
    lay = lambda t: np.tile(t.reshape(NT, P, 1, HD), (1, 1, 2 * HEADS, 1)).transpose(1, 0, 2, 3).reshape(P, -1)
    same = np.zeros((P, C), np.float32)
    c = np.arange(C)
    same[:C] = (c[:, None] // GN_GROUP == c[None] // GN_GROUP)
    parts = [gx, gy[0], gy[1], lay(np.cos(ang)), lay(np.sin(ang) * sign), same]
    return np.ascontiguousarray(np.concatenate([a.astype(np.float32) for a in parts], axis=1))


N_GRID = SIDE + NT * SIDE
N_ROPE = NT * 2 * C
O_COS, O_SIN, O_SAME = N_GRID, N_GRID + N_ROPE, N_GRID + 2 * N_ROPE
N_CONST = O_SAME + C


def build(nc, x, weight_coord, radius, conv_w, w_attn, w_proj, w1, b1, w2, b2, const, out):
    x_v = x.rearrange("b c h w -> c b (h w)")
    out_v = out.rearrange("b c h w -> c b (h w)")
    with ExitStack() as ctx:
        def sb(name, shape, dt=F32):
            return ctx.enter_context(nc.sbuf_tensor(name, shape, dt))

        def sem(name):
            return ctx.enter_context(nc.semaphore(name))

        x_ring = sb("x_ring", [C, 2, 2, T])
        xn_ring = sb("xn_ring", [C, 2, 2, T])
        tok = sb("tok", [P, B, NT, C])
        xs_ring = sb("xs_ring", [P, 2, POINTS, NT, 2, C])
        toep = sb("toep", [P, POINTS, NT, SIDE, SIDE])
        cst = sb("cst", [P, N_CONST])
        wc_bc = sb("wc_bc", [P, POINTS * 2])
        rad_bc = sb("rad_bc", [P, POINTS])
        cw_bc = sb("cw_bc", [P, C, POINTS])
        grid_t = sb("grid_t", [P, POINTS, N_GRID])
        grid_n = sb("grid_n", [P, POINTS, N_GRID])
        nrinv = sb("nrinv", [P, 2, POINTS])
        ident = sb("ident", [P, P])
        ident16 = sb("ident16", [P, P], BF16)
        mask = sb("mask", [P, P])
        mask16 = sb("mask16", [P, P], BF16)
        ones = sb("ones", [P, P])
        mhalf = sb("mhalf", [P, B * NT])
        gn_st = sb("gn_st", [C, B, 6])
        gn_mv = sb("gn_mv", [C, B, 2])
        gn_tmp = sb("gn_tmp", [C, 3, B])
        gn_mean = sb("gn_mean", [C, B])
        gn_rstd = sb("gn_rstd", [C, B])
        ln_st = sb("ln_st", [P, 2, 4, 6])
        ln_mv = sb("ln_mv", [P, 2, 4, 2])
        ln_var = sb("ln_var", [P, 2, 4])
        ln_rstd = sb("ln_rstd", [P, 2, 4])
        xl_ring = sb("xl_ring", [P, 2, 4, C])
        lt_ring = sb("lt_ring", [C, 2, 4 * P])
        wa = sb("wa", [C, 3 * C])
        wp = sb("wp", [C, C])
        qk_ring = sb("qk_ring", [P, 2, N_ROPE])
        rc_ring = sb("rc_ring", [P, 2, N_ROPE])
        rs_tmp = sb("rs_tmp", [P, N_ROPE])
        qr_ring = sb("qr_ring", [P, 2, N_ROPE])
        rest_ring = sb("rest_ring", [C, 2, 2, T])
        parts = sb("parts", [P, B * 3 * 2 * T], BF16)
        v_all = sb("v_all", [P, B, NT, C])
        stack = sb("stack", [P, RING, HEADS, 2, T], BF16)
        x_all = stack[0:C, :, :, :, :].rearrange("p r h s n -> p (r h s n)").bitcast(F32)[:, 0:B * T]
        x_all = x_all.rearrange("c (b n) -> c b n", b=B)
        v_ring = sb("v_ring", [P, 2, NT, HEADS, 2 * HD])
        pt_ring = sb("pt_ring", [P, 2, HEADS, T + P])
        nmax = sb("nmax", [P, 2, NT * HEADS])
        nmax_t = sb("nmax_t", [NT * HEADS, 2, P], BF16)
        o_ring = sb("o_ring", [C, 2, 2 * T])
        rsum = sb("rsum", [P, NT * HEADS])
        o_norm = sb("o_norm", [P, NT, C])
        ot_ring = sb("ot_ring", [C, 2, T])
        ln2_st = sb("ln2_st", [P, B * NT, 6])
        ln2_mean = sb("ln2_mean", [P, B * NT])
        ln2_tmp = sb("ln2_tmp", [P, 3, B * NT])
        ln2_var = sb("ln2_var", [P, B * NT])
        ln2_rstd = sb("ln2_rstd", [P, B * NT])
        w1_in = sb("w1_in", [P, HC, C])
        w1_b = sb("w1_b", [C, HID])
        w2_in = sb("w2_in", [C, HID])
        w2_b = sb("w2_b", [P, HC, C])
        w_sum = sb("w_sum", [P, 2, QGROUPS])
        w_mean = sb("w_mean", [P, 2, QGROUPS])
        b1_s = sb("b1_s", [P, HC])
        b2_s = sb("b2_s", [C, 1])
        x2_ring = sb("x2_ring", [P, 2, GB * NT, C])
        amax1 = sb("amax1", [P, 2 * HC])
        amax2 = sb("amax2", [P, 2])
        gmax1 = sb("gmax1", [P, 4])
        gmax2 = sb("gmax2", [P, 4])
        lim1 = sb("lim1", [P, 2, 4])
        lim2 = sb("lim2", [P, 4])

        parts_v = parts[0:C, :].rearrange("c (b s k n) -> c (b s) k n", b=B, s=2, k=3)
        wide = parts[:, :].bitcast(F32)
        n_y1 = 2 * HC * HALF
        y1_ring = wide[:, 0:2 * n_y1].rearrange("p (s n) -> p s n", s=2)
        h_ring = wide[:, 2 * n_y1:4 * n_y1].rearrange("p (s n) -> p s n", s=2)
        x2t_ring = wide[0:C, 4 * n_y1:4 * n_y1 + 2 * GT].rearrange("p (s n) -> p s n", s=2)
        y2_ring = wide[0:C, 4 * n_y1 + 2 * GT:4 * n_y1 + 4 * GT].rearrange("p (s n) -> p s n", s=2)
        flat = xs_ring[:, :, :, :, :, :].rearrange("p s q t b c -> p (s q t b c)")
        out_ring = flat[0:C, 0:2 * GT].rearrange("p (s n) -> p s n", s=2)

        bank = ctx.enter_context(nc.psum_tensor("bank", [P, 8, 512], F32))

        s_xall = [sem(f"s_xall{i}") for i in range(4)]
        s_small = sem("s_small")
        s_weights = sem("s_weights")
        s_xr = [sem(f"s_xr{i}") for i in range(2)]
        s_zero = sem("s_zero")
        s_ident = sem("s_ident")
        s_setup = sem("s_setup")
        s_id16 = sem("s_id16")
        s_vones = sem("s_vones")
        s_rinv = sem("s_rinv")
        s_grid = sem("s_grid")
        s_kones = sem("s_kones")
        s_grid2 = sem("s_grid2")
        s_cone = sem("s_cone")
        s_toep = sem("s_toep")
        s_gst = sem("s_gst")
        s_gmv = sem("s_gmv")
        s_gps = sem("s_gps")
        s_gdve = sem("s_gdve")
        s_grstd = sem("s_grstd")
        s_wtr = sem("s_wtr")
        s_wcopy = sem("s_wcopy")
        s_wsum = sem("s_wsum")
        s_wps = sem("s_wps")
        s_wmean = sem("s_wmean")
        s_wcen = sem("s_wcen")
        s_wsign = sem("s_wsign")
        s_wready = sem("s_wready")
        s_xn = sem("s_xn")
        s_xnt = sem("s_xnt")
        s_xs = sem("s_xs")
        s_cv = sem("s_cv")
        s_tok = sem("s_tok")
        s_lnst = sem("s_lnst")
        s_lnmv = sem("s_lnmv")
        s_lnvar = sem("s_lnvar")
        s_lnrstd = sem("s_lnrstd")
        s_xl = sem("s_xl")
        s_xlt = sem("s_xlt")
        s_lt = sem("s_lt")
        s_qkv = sem("s_qkv")
        s_qk = sem("s_qk")
        s_vc = sem("s_vc")
        s_rcos = sem("s_rcos")
        s_rsin = sem("s_rsin")
        s_rope = sem("s_rope")
        s_qkt = sem("s_qkt")
        s_p0 = sem("s_p0")
        s_rest = sem("s_rest")
        s_p1 = sem("s_p1")
        s_p2 = sem("s_p2")
        s_stack = [sem(f"s_stack{i}") for i in range(RING)]
        s_mrow = [sem(f"s_mrow{i}") for i in range(RING)]
        s_sq = sem("s_sq")
        s_max = sem("s_max")
        s_mt = sem("s_mt")
        s_mtc = sem("s_mtc")
        s_sk = sem("s_sk")
        s_exp = sem("s_exp")
        s_sel = sem("s_sel")
        s_v = sem("s_v")
        s_pv = sem("s_pv")
        s_o = sem("s_o")
        s_otr = sem("s_otr")
        s_rsum = sem("s_rsum")
        s_on = sem("s_on")
        s_ont = sem("s_ont")
        s_ontc = sem("s_ontc")
        s_proj = sem("s_proj")
        s_res = sem("s_res")
        s_l2st = sem("s_l2st")
        s_l2mv = sem("s_l2mv")
        s_l2var = sem("s_l2var")
        s_l2rstd = sem("s_l2rstd")
        s_x2m = sem("s_x2m")
        s_x2 = sem("s_x2")
        s_x2t = sem("s_x2t")
        s_x2c = sem("s_x2c")
        s_f1 = sem("s_f1")
        s_y1 = sem("s_y1")
        s_am1 = sem("s_am1")
        s_gm1 = sem("s_gm1")
        s_ar1 = sem("s_ar1")
        s_bd1 = sem("s_bd1")
        s_sc1 = sem("s_sc1")
        s_clip1 = sem("s_clip1")
        s_h = sem("s_h")
        s_f2 = sem("s_f2")
        s_y2 = sem("s_y2")
        s_am2 = sem("s_am2")
        s_gm2 = sem("s_gm2")
        s_ar2 = sem("s_ar2")
        s_bd2 = sem("s_bd2")
        s_sc2 = sem("s_sc2")
        s_clip2 = sem("s_clip2")
        s_t2t = sem("s_t2t")
        s_out = sem("s_out")
        s_store = [sem(f"s_store{i}") for i in range(2)]

        block = ctx.enter_context(nc.Block())

        def wait(eng, semaphore, count):
            if isinstance(count, int) and count <= 0:
                return
            eng.wait_ge(semaphore, count)

        def wait_apart(eng, semaphore, count):
            if not isinstance(count, int):
                eng.compute_val(count)
            eng.wait_ge(s_ident, 1)
            wait(eng, semaphore, count)

        def run(eng, step, first, unroll, laps, last, start=0):
            for n in range(start, first):
                step(0, n)
            with eng.Fori(0, laps) as i:
                for u in range(unroll):
                    step(i, first + u)
            for n in range(first + unroll * laps, last):
                step(0, n)

        A = dict(first=3, unroll=2, laps=2, last=PAIRS)
        BB = dict(start=2, first=2, unroll=RING, laps=3, last=B + 2)
        C_STEPS = QGROUPS + 2

        @block.sync
        def _(sp):
            sp.dma_start(cst[:], const).then_inc(s_small, 16)
            sp.dma_start(x_all[:, 0:4, :], x_v[:, 0:4, :]).then_inc(s_xall[0], 16)
            sp.dma_start(x_all[:, 8:12, :], x_v[:, 8:12, :]).then_inc(s_xall[2], 16)
            for k in range(2):
                sp.dma_start(x_ring[:, k, :, :], x_v[:, 2 * k:2 * k + 2, :]).then_inc(s_xr[k], 16)
            sp.dma_start(wa[:], w_attn).then_inc(s_weights, 16)
            sp.dma_start(wp[:], w_proj).then_inc(s_weights, 16)

            def load_x(i, n0):
                wait(sp, s_cv, n0 - 1 + 2 * i)
                b = 2 * n0 + 4 * i
                sp.dma_start(x_ring[:, n0 % 2, :, :], x_v[:, ds(b, 2), :]).then_inc(s_xr[n0 % 2], 16)
            with sp.Fori(0, PAIRS // 2 - 1) as i:
                for u in range(2):
                    load_x(i, 2 + u)
            sp.wait_ge(s_xn, PAIRS)

            def stack_image(i, n0, first, last):
                b, slot = n0 + RING * i, n0 % RING
                for r in range(first, last):
                    kp, qp = SLOTS[r]
                    q_part = parts[0:C, ds((b * 6 + qp) * T, T)]
                    src = bass.AP(q_part.tensor, q_part.offset, [q_part.ap[0], [(3 + kp - qp) * T, 2], [1, T]])
                    dst = stack[r * HD:(r + 1) * HD, slot, :, :, :].rearrange("d h s n -> d (h s n)")
                    sp.dma_start(dst, src).then_inc(s_stack[slot], 16)

            def stack_ready(i, n0):
                b = n0 + RING * i
                wait_apart(sp, s_p0, b + 1)
                wait(sp, s_p1, b + 1)
                wait(sp, s_p2, b + 1)
                wait(sp, s_sk, 3 * (b - RING + 1))

            def max_row(i, n0):
                b, slot = n0 + RING * i, n0 % RING
                wait(sp, s_mtc, b + 1)
                for t in range(NT):
                    sp.dma_start(stack[KROWS:KROWS + 1, slot, :, 0, t * P:(t + 1) * P],
                                 nmax_t[t * HEADS:(t + 1) * HEADS, n0 % 2, :]).then_inc(s_mrow[slot], 16)

            for n in range(RING - 1):
                stack_ready(0, n)
                stack_image(0, n, 0, len(SLOTS))
            max_row(0, 0)

            def step_b(i, n0):
                if n0 + 3 < B:
                    stack_ready(i, n0 + 3)
                    stack_image(i, n0 + 3, 0, len(SLOTS) // 2)
                if n0 + 1 < B:
                    max_row(i, n0 + 1)
                if n0 + 3 < B:
                    stack_image(i, n0 + 3, len(SLOTS) // 2, len(SLOTS))
            run(sp, step_b, first=1, unroll=RING, laps=3, last=B)

            for g in range(QGROUPS):
                sp.wait_ge(s_out, g + 1)
                sp.dma_start(out_v[:, g * GB:(g + 1) * GB, :],
                             out_ring[:, g % 2, :].rearrange("c (b n) -> c b n", b=GB)).then_inc(s_store[g % 2], 16)
            sp.wait_ge(s_out, QGROUPS + 1)
            sp.dma_start(out_v[:, B - 1, :], out_ring[:, 1, 0:T]).then_inc(s_store[1], 16)
            sp.wait_ge(s_store[0], 16 * 3)
            sp.wait_ge(s_store[1], 16 * 3)

        @block.gpsimd
        def _(pool):
            nc.gpsimd.memset(ident[:], 0.0)
            nc.gpsimd.memset(mask[:], 0.0)
            nc.gpsimd.memset(mhalf[:], -0.5).then_inc(s_zero, 1)
            pool.wait_ge(s_zero, 1)
            nc.gpsimd.affine_select(out=ident[:], in_=ident[:], compare_op=ALU.not_equal, fill=1.0, base=0,
                                    pattern=[[-1, P]], channel_multiplier=1).then_inc(s_ident, 1)
            nc.gpsimd.affine_select(out=mask[:], in_=mask[:], compare_op=ALU.is_ge, fill=NEG, base=0,
                                    pattern=[[-1, P]], channel_multiplier=1)
            nc.gpsimd.memset(ones[:], 1.0).then_inc(s_setup, 1)
            pool.wait_ge(s_gdve, 4)
            nc.gpsimd.tensor_tensor(gn_rstd[:], gn_tmp[:, 2, :], mhalf[0:C, 0:B], ALU.pow).then_inc(s_grstd, 1)
            pool.wait_ge(s_grstd, 1)
            nc.gpsimd.memset(stack[KROWS:KROWS + 1, :, :, 1, :].rearrange("o r h n -> o (r h) n"), 1.0).then_inc(s_kones, 1)
            pool.wait_ge(s_kones, 1)
            nc.gpsimd.memset(v_ring[:], 1.0).then_inc(s_vones, 1)

            def rope(i, n0, u):
                b = 2 * (n0 + 2 * i) + u
                wait(pool, s_qk, b + 1)
                wait(pool, s_rope, b)
                swapped = qk_ring[:, u, :].rearrange("p (n t) -> p n t", t=2)[:, :, ::-1]
                nc.gpsimd.tensor_tensor(rs_tmp[:].rearrange("p (n t) -> p n t", t=2), swapped,
                                        cst[:, O_SIN:O_SIN + N_ROPE].rearrange("p (n t) -> p n t", t=2),
                                        ALU.mult).then_inc(s_rsin, 1)
                wait(pool, s_rsin, b + 1)
                wait(pool, s_rcos, b + 1)
                wait(pool, s_qkt, b - 1)
                nc.gpsimd.tensor_tensor(qr_ring[:, u, :].rearrange("p (k d h) -> p k d h", h=HEADS, d=HD),
                                        rc_ring[:, u, :].rearrange("p (k h d) -> p k d h", h=HEADS, d=HD),
                                        rs_tmp[:].rearrange("p (k h d) -> p k d h", h=HEADS, d=HD),
                                        ALU.add).then_inc(s_rope, 1)

            def third(i, n0, u):
                b = 2 * (n0 + 2 * i) + u
                wait(pool, s_p1, b + 1)
                nc.gpsimd.tensor_tensor(parts_v[:, ds(2 * b, 2), 2, :], rest_ring[:, u], parts_v[:, ds(2 * b, 2), 1, :],
                                        ALU.subtract).then_inc(s_p2, 1)

            def step_a(i, n0):
                if 1 <= n0 <= PAIRS:
                    wait(pool, s_lnvar, n0 + 2 * i)
                    nc.gpsimd.tensor_tensor(ln_rstd[:, (n0 - 1) % 2, :], ln_var[:, (n0 - 1) % 2, :], mhalf[:, 0:4],
                                            ALU.pow).then_inc(s_lnrstd, 1)
                if 2 <= n0 <= PAIRS + 1:
                    rope(i, n0 - 2, 0)
                if n0 >= 3:
                    third(i, n0 - 3, 1)
                if 2 <= n0 <= PAIRS + 1:
                    rope(i, n0 - 2, 1)
                    third(i, n0 - 2, 0)
            run(pool, step_a, **A)

            def step_b(i, n0):
                if n0 >= B:
                    return
                for hp in range(3):
                    wait_apart(pool, s_exp, 3 * (n0 + RING * i) + hp + 1)
                    v = pt_ring[:, n0 % 2, 2 * hp:2 * hp + 2, 0:2 * P]
                    nc.gpsimd.affine_select(out=v, in_=v, compare_op=ALU.is_ge, fill=0.0, base=0,
                                            pattern=[[0, 2], [0, 2], [1, P]], channel_multiplier=-1).then_inc(s_sel, 1)
            for n in range(3):
                step_a(0, PAIRS + n)
                if n:
                    step_b(0, n - 1)
            run(pool, step_b, **BB)

            def second_rstd(k):
                cols = LN2_COLS[k]
                pool.wait_ge(s_l2var, k + 1)
                nc.gpsimd.tensor_tensor(ln2_rstd[:, cols], ln2_var[:, cols], mhalf[:, cols],
                                        ALU.pow).then_inc(s_l2rstd, 1)

            def second_norm(g):
                pool.wait_ge(s_l2rstd, 1 if g < QGROUPS - 1 else 2)
                wait(pool, s_x2t, 2 * (g - 1))
                cols = slice(GB * NT * g, GB * NT * (g + 1))
                t_g = tok[:, GB * g:GB * (g + 1), :, :].rearrange("p b t c -> p (b t) c")
                nc.gpsimd.tensor_tensor(x2_ring[:, g % 2], t_g, ln2_mean[:, cols].unsqueeze(2).broadcast_to(
                    [P, GB * NT, C]), ALU.subtract).then_inc(s_x2m, 1)
                pool.wait_ge(s_x2m, g + 1)
                nc.gpsimd.tensor_tensor(x2_ring[:, g % 2], x2_ring[:, g % 2], ln2_rstd[:, cols].unsqueeze(
                    2).broadcast_to([P, GB * NT, C]), ALU.mult).then_inc(s_x2, 1)

            second_rstd(0)
            second_norm(0)
            second_rstd(1)
            for n in range(C_STEPS):
                if n + 1 < QGROUPS:
                    second_norm(n + 1)
                if 2 <= n:
                    pool.wait_ge(s_gm2, n - 1)
                    wait(pool, s_sc2, n - 2)
                    nc.gpsimd.partition_all_reduce(gmax2[0:C, 1:2], gmax2[0:C, 0:1], C,
                                                   bass.bass_isa.ReduceOp.max).then_inc(s_ar2, 1)
                if n < QGROUPS:
                    pool.wait_ge(s_gm1, n + 1)
                    wait(pool, s_sc1, n)
                    nc.gpsimd.partition_all_reduce(gmax1[:, 1:2], gmax1[:, 0:1], P,
                                                   bass.bass_isa.ReduceOp.max).then_inc(s_ar1, 1)

        @block.scalar
        def _(act):
            act.dma_start(wc_bc[:], weight_coord.rearrange("o p k -> o (p k)").broadcast_to([P, POINTS * 2])).then_inc(s_small, 16)
            act.dma_start(rad_bc[:], radius.rearrange("o p a b -> o (p a b)").broadcast_to([P, POINTS])).then_inc(s_small, 16)
            act.dma_start(cw_bc[:].rearrange("p c k -> p (c k)"),
                          conv_w.rearrange("o c k -> o (c k)").broadcast_to([P, C * POINTS])).then_inc(s_small, 16)
            act.dma_start(x_all[:, 4:8, :], x_v[:, 4:8, :]).then_inc(s_xall[1], 16)
            act.dma_start(x_all[:, 12:16, :], x_v[:, 12:16, :]).then_inc(s_xall[3], 16)
            act.dma_start(w1_in[:], w1.rearrange("(c p) k -> p c k", p=P)).then_inc(s_weights, 16)
            act.dma_start(w2_in[:], w2).then_inc(s_weights, 16)
            act.dma_start(b1_s[:], b1.rearrange("(c p) -> p c", p=P), allow_slow_non_contiguous=True).then_inc(s_weights, 16)
            act.dma_start(b2_s[:], b2.rearrange("(c o) -> c o", o=1), allow_slow_non_contiguous=True).then_inc(s_weights, 16)
            for p in range(POINTS):
                act.wait_ge(s_cone, p + 1)
                m = toep[:, p].rearrange("p t y x -> p (t y x)")
                nc.scalar.activation(m, m, ACT.Relu).then_inc(s_toep, 1)
            act.wait_ge(s_wtr, 1)
            nc.scalar.copy(w1_b[:], bank[0:C, 5, 0:HID]).then_inc(s_wcopy, 1)
            act.wait_ge(s_wtr, 2)
            nc.scalar.copy(w2_b[:].rearrange("p k c -> p (k c)"), bank[:, 7, 0:HC * C]).then_inc(s_wcopy, 1)

            def step_a(i, n0):
                j = n0 + 2 * i

                def qkv_out(q, u):
                    b = 2 * q + u
                    wait(act, s_qkv, b + 1)
                    wait(act, s_rope, b - 1)
                    nc.scalar.copy(qk_ring[:, u, :].rearrange("p (t c) -> p t c", t=NT),
                                   bank[:, 5:7, 0:2 * C]).then_inc(s_qk, 1)
                    nc.scalar.copy(v_all[:, ds(b, 1), :, :].rearrange("p o t c -> p (o t) c"),
                                   bank[:, 5:7, 2 * C:3 * C]).then_inc(s_vc, 1)

                def first_parts(u):
                    b = 2 * (j - 2) + u
                    wait(act, s_qkt, b + 1)
                    nc.scalar.copy(parts_v[:, ds(2 * b, 2), 0, :], bank[0:C, 7, :].rearrange("c (s n) -> c s n", s=2)).then_inc(s_p0, 1)
                if 2 <= n0 <= PAIRS + 1:
                    qkv_out(j - 2, 1)
                    first_parts(0)
                if 1 <= n0 <= PAIRS:
                    wait(act, s_xlt, j)
                    wait(act, s_qkv, 2 * j - 4)
                    nc.scalar.copy(lt_ring[:, (n0 - 1) % 2, :], bank[0:C, 4, :]).then_inc(s_lt, 1)
                if n0 < PAIRS:
                    act.wait_ge(s_cv, j + 1)
                    nc.scalar.copy(tok[:, ds(2 * j, 2), :, :],
                                   bank[:, 2 + n0 % 2, 0:NT * 2 * C].rearrange("p (t b c) -> p b t c", t=NT, b=2)
                                   ).then_inc(s_tok, 1)
                if 2 <= n0 <= PAIRS + 1:
                    first_parts(1)
                if 1 <= n0 <= PAIRS:
                    qkv_out(j - 1, 0)
            run(act, step_a, **A)
            def max_out(i, n0):
                b = n0 + RING * i
                wait(act, s_mt, b + 1)
                prev = (n0 - 2) % RING
                wait(act, s_mrow[prev], 16 * NT * ((n0 - 2) // RING + i + 1))
                nc.scalar.copy(nmax_t[:, n0 % 2, :], bank[0:NT * HEADS, 2, 3 * P:4 * P]).then_inc(s_mtc, 1)

            def step_b(i, n0):
                b = n0 + RING * i
                s = n0 % 2

                def exps(hp):
                    act.wait_ge(s_sk, 3 * b + hp + 1)
                    wait(act, s_pv, b - 1)
                    nc.scalar.activation(pt_ring[:, s, 2 * hp:2 * hp + 2, :], bank[:, 3:5, 0:T + P], ACT.Exp,
                                         scale=float(HD) ** -0.5).then_inc(s_exp, 1)
                if n0 < B:
                    exps(0)
                if n0 + 1 < B:
                    max_out(i, n0 + 1)
                if n0 >= 2:
                    wait(act, s_ont, b - 1)
                    wait(act, s_proj, b - 2)
                    nc.scalar.copy(ot_ring[:, s, :], bank[0:C, 6, 0:T]).then_inc(s_ontc, 1)
                if n0 < B:
                    nc.scalar.copy(v_ring[:, s, :, :, 0:HD].rearrange("p t h d -> p (t h) d"),
                                   v_all[:, ds(b, 1), :, :].rearrange("p o t (h d) -> p (o t h) d", d=HD)
                                   ).then_inc(s_v, 1)
                if 1 <= n0 <= B:
                    wait(act, s_pv, b)
                    wait(act, s_otr, b - 2)
                    nc.scalar.copy(o_ring[:, 1 - s, :], bank[0:C, 7, :]).then_inc(s_o, 1)
                if n0 < B:
                    exps(1)
                    exps(2)
            act.wait_ge(s_vones, 1)
            step_a(0, PAIRS)
            max_out(0, 0)
            step_a(0, PAIRS + 1)
            act.wait_ge(s_wcen, 2)
            nc.scalar.activation(w1_b[:, 0:QGROUPS * W1_ROWS], w1_b[:, 0:QGROUPS * W1_ROWS], ACT.Sign)
            nc.scalar.activation(w2_b[:, :, 0:QGROUPS * W2_ROWS], w2_b[:, :, 0:QGROUPS * W2_ROWS],
                                 ACT.Sign).then_inc(s_wsign, 1)

            step_b(0, 0)
            step_a(0, PAIRS + 2)
            step_b(0, 1)
            run(act, step_b, **BB)

            def channel_major(g):
                for half in range(2):
                    act.wait_ge(s_x2t, 2 * g + half + 1)
                    wait(act, s_f1, 2 * HC * (g - 1))
                    nc.scalar.copy(x2t_ring[:, g % 2, half * HALF:(half + 1) * HALF],
                                   bank[0:C, half, 0:HALF]).then_inc(s_x2c, 1)

            def hidden(g, r):
                act.wait_ge(s_f1, 2 * HC * g + r + 1)
                wait(act, s_h, 2 * (g - 1))
                nc.scalar.activation(y1_ring[:, g % 2, r * HALF:(r + 1) * HALF], bank[:, 2 + r % 2, 0:HALF],
                                     ACT.Identity, bias=b1_s[:, r % HC:r % HC + 1]).then_inc(s_y1, 1)

            def gelu(g, half):
                act.wait_ge(s_clip1, 2 * g + half + 1)
                wait(act, s_f2, 2 * (g - 1))
                cols = slice(half * HC * HALF, (half + 1) * HC * HALF)
                nc.scalar.activation(h_ring[:, g % 2, cols], y1_ring[:, g % 2, cols], ACT.Gelu,
                                     scale=lim1[:, g % 2, 0:1]).then_inc(s_h, 1)

            def output(g):
                for half in range(2):
                    act.wait_ge(s_f2, 2 * g + half + 1)
                    wait(act, s_out, g - 1)
                    nc.scalar.activation(y2_ring[:, g % 2, half * HALF:(half + 1) * HALF],
                                         bank[0:C, 4 + half, 0:HALF], ACT.Identity, bias=b2_s[:, 0:1]).then_inc(s_y2, 1)

            channel_major(0)
            for n in range(C_STEPS):
                for half in range(2):
                    if n < QGROUPS:
                        for r in range(half * HC, (half + 1) * HC):
                            hidden(n, r)
                    if 1 <= n <= QGROUPS:
                        gelu(n - 1, half)
                if n + 1 < QGROUPS:
                    channel_major(n + 1)
                if 1 <= n <= QGROUPS:
                    output(n - 1)

        @block.vector
        def _(dve):
            dve.wait_ge(s_small, 16 * 4)
            nc.vector.reciprocal(nrinv[:, 0, :], rad_bc[:])
            for p in range(POINTS):
                for k, cols in enumerate((slice(0, SIDE), slice(SIDE, N_GRID))):
                    at = wc_bc[:, 2 * p + k:2 * p + k + 1]
                    nc.vector.tensor_scalar(grid_t[:, p, cols], cst[:, cols], at, None, ALU.subtract)
                    last = nc.vector.tensor_scalar(grid_n[:, p, cols], cst[:, cols], at, -1.0, ALU.subtract, ALU.mult)
            last.then_inc(s_grid, 1)
            dve.wait_ge(s_grid, 1)
            nc.vector.tensor_tensor(grid_t[:], grid_t[:], grid_n[:], ALU.max).then_inc(s_grid, 1)
            nc.vector.tensor_scalar(nrinv[:, 1, :], nrinv[:, 0, :], -1.0, None, ALU.mult).then_inc(s_rinv, 1)
            dve.wait_ge(s_rinv, 1)
            dve.wait_ge(s_grid, 2)
            for p in range(POINTS):
                nc.vector.tensor_scalar(grid_t[:, p, 0:SIDE], grid_t[:, p, 0:SIDE], nrinv[:, 1, p:p + 1], None,
                                        ALU.mult)
                nc.vector.tensor_scalar(grid_t[:, p, SIDE:N_GRID], grid_t[:, p, SIDE:N_GRID],
                                        nrinv[:, 1, p:p + 1], 1.0, ALU.mult, ALU.add).then_inc(s_grid2, 1)
            for p in range(POINTS):
                dve.wait_ge(s_grid2, p + 1)
                gx = grid_t[:, p, 0:SIDE].unsqueeze(1).broadcast_to([P, NT * SIDE, SIDE])
                gy = grid_t[:, p, SIDE:N_GRID].unsqueeze(2).broadcast_to([P, NT * SIDE, SIDE])
                nc.vector.tensor_tensor(toep[:, p].rearrange("p t y x -> p (t y) x"), gx, gy,
                                        ALU.add).then_inc(s_cone, 1)

            for b in range(B):
                if b % 4 == 0:
                    dve.wait_ge(s_xall[b // 4], 16)
                nc.vector.bn_stats(gn_st[:, b, :], x_all[:, b, :]).then_inc(s_gst, 1)
            for b in range(B):
                dve.wait_ge(s_gst, b + 1)
                last = nc.vector.bn_aggr(gn_mv[:, b, :], gn_st[:, b, :])
            last.then_inc(s_gmv, 1)
            dve.wait_ge(s_gps, 1)
            nc.vector.tensor_scalar(gn_mean[:], bank[0:C, 4, 0:B], 1.0 / GN_GROUP, None, ALU.mult).then_inc(s_gdve, 1)
            dve.wait_ge(s_gdve, 1)
            nc.vector.tensor_tensor(gn_tmp[:, 0, :], gn_mv[:, :, 0], gn_mean[:], ALU.subtract).then_inc(s_gdve, 1)
            dve.wait_ge(s_gdve, 2)
            nc.vector.tensor_tensor(gn_tmp[:, 1, :], gn_tmp[:, 0, :], gn_tmp[:, 0, :], ALU.mult).then_inc(s_rinv, 1)
            dve.wait_ge(s_rinv, 2)
            nc.vector.tensor_tensor(gn_tmp[:, 0, :], gn_tmp[:, 1, :], gn_mv[:, :, 1], ALU.add).then_inc(s_gdve, 1)
            dve.wait_ge(s_gps, 2)
            nc.vector.tensor_scalar(gn_tmp[:, 2, :], bank[0:C, 4, B:2 * B], 1.0 / GN_GROUP, GN_EPS, ALU.mult,
                                    ALU.add).then_inc(s_gdve, 1)
            dve.wait_ge(s_setup, 1)
            nc.vector.tensor_copy(mask16[:], mask[:])
            nc.vector.tensor_copy(ident16[:], ident[:]).then_inc(s_id16, 1)

            def normalise(i, n0):
                j = n0 + 2 * i
                s = n0 % 2
                wait(dve, s_xnt, j - 1)
                for u in range(2):
                    b = 2 * j + u
                    last = nc.vector.tensor_scalar(xn_ring[:, s, u, :],
                                                   x_all[:, ds(b, 1), :].rearrange("c o n -> c (o n)"),
                                                   gn_mean[:, ds(b, 1)], gn_rstd[:, ds(b, 1)], ALU.subtract, ALU.mult)
                last.then_inc(s_xn, 1)

            def weigh(i, n0):
                j, s = n0 + 2 * i, n0 % 2
                dve.wait_ge(s_xnt, j + 1)
                wait(dve, s_cv, j - 1)
                src = bank[:, s, 0:NT * 2 * C].rearrange("p (k c) -> p k c", c=C)
                for p in range(POINTS):
                    w = cw_bc[:, :, p].unsqueeze(1).broadcast_to([P, NT * 2, C])
                    last = nc.vector.tensor_tensor(xs_ring[:, s, p].rearrange("p t b c -> p (t b) c"), src, w, ALU.mult)
                last.then_inc(s_xs, 1)

            dve.wait_ge(s_grstd, 1)
            normalise(0, 0)
            weigh(0, 0)

            dve.wait_ge(s_wcopy, 1)
            nc.vector.tensor_reduce(w_sum[0:C, 0, :], w1_b[:, 0:QGROUPS * W1_ROWS].rearrange(
                "c (g r) -> c g r", g=QGROUPS), op=ALU.add, axis=AX.X).then_inc(s_wsum, 1)
            dve.wait_ge(s_wcopy, 2)
            nc.vector.tensor_reduce(w_sum[:, 1, :], w2_b[:, :, 0:QGROUPS * W2_ROWS].rearrange(
                "p k (g r) -> p g k r", g=QGROUPS), op=ALU.add, axis=AX.XY).then_inc(s_wsum, 1)

            def cosines(i, n0, u):
                b = 2 * (n0 + 2 * i) + u
                dve.wait_ge(s_qk, b + 1)
                wait(dve, s_rope, b - 1)
                nc.vector.tensor_tensor(rc_ring[:, u, :], qk_ring[:, u, :], cst[:, O_COS:O_COS + N_ROPE],
                                        ALU.mult).then_inc(s_rcos, 1)

            def second_parts(i, n0, u):
                b = 2 * (n0 + 2 * i) + u
                dve.wait_ge(s_p0, b + 1)
                wait(dve, s_p2, b - 1)
                nc.vector.tensor_tensor(rest_ring[:, u], bank[0:C, 7, :].rearrange("c (s n) -> c s n", s=2),
                                        parts_v[:, ds(2 * b, 2), 0, :], ALU.subtract).then_inc(s_rest, 1)
                dve.wait_ge(s_rest, b + 1)
                nc.vector.tensor_copy(parts_v[:, ds(2 * b, 2), 1, :], rest_ring[:, u]).then_inc(s_p1, 1)

            def step_a(i, n0):
                j = n0 + 2 * i
                if n0 + 1 < PAIRS:
                    normalise(i, n0 + 1)
                if 1 <= n0 <= PAIRS:
                    s = (n0 - 1) % 2
                    wait_apart(dve, s_tok, j)
                    for t in range(4):
                        nc.vector.bn_stats(ln_st[:, s, t, :], tok[:, ds(2 * (j - 1) + t // 2, 1), t % 2, :]
                                           .rearrange("p o c -> p (o c)")).then_inc(s_lnst, 1)
                    wait_apart(dve, s_lnst, 4 * j)
                    for t in range(4):
                        last = nc.vector.bn_aggr(ln_mv[:, s, t, :], ln_st[:, s, t, :])
                    last.then_inc(s_lnmv, 1)
                    dve.wait_ge(s_lnmv, j)
                    nc.vector.tensor_scalar(ln_var[:, s, :], ln_mv[:, s, :, 1], LN_EPS, None,
                                            ALU.add).then_inc(s_lnvar, 1)
                if 2 <= n0 <= PAIRS + 1:
                    cosines(i, n0 - 2, 0)
                if n0 >= 3:
                    second_parts(i, n0 - 3, 1)
                if 1 <= n0 <= PAIRS:
                    s = (n0 - 1) % 2
                    dve.wait_ge(s_lnrstd, j)
                    wait(dve, s_xlt, j - 2)
                    for t in range(4):
                        last = nc.vector.tensor_scalar(
                            xl_ring[:, s, t, :], tok[:, ds(2 * (j - 1) + t // 2, 1), t % 2, :].rearrange(
                                "p o c -> p (o c)"), ln_mv[:, s, t, 0:1], ln_rstd[:, s, t:t + 1],
                            ALU.subtract, ALU.mult)
                    last.then_inc(s_xl, 1)
                if 2 <= n0 <= PAIRS + 1:
                    cosines(i, n0 - 2, 1)
                if n0 + 1 < PAIRS:
                    weigh(i, n0 + 1)
                if 2 <= n0 <= PAIRS + 1:
                    second_parts(i, n0 - 2, 0)
            run(dve, step_a, **A)

            def maxima(i, n0, h):
                b = n0 + RING * i
                dve.wait_ge(s_sq, HEADS * b + h + 1)
                if h == 0:
                    wait(dve, s_mt, b - 1)
                for t in range(NT):
                    first = t * P
                    last = nc.vector.tensor_reduce(nmax[:, n0 % 2, HEADS * t + h:HEADS * t + h + 1],
                                                   bank[:, h % 3, first:first + (t + 1) * P],
                                                   op=ALU.max, axis=AX.X, negate=True)
                last.then_inc(s_max, 1)

            def second_stats(k):
                cols = LN2_COLS[k]
                even, odd = ln2_st[:, cols, 1], ln2_st[:, cols, 4]
                dve.wait_ge(s_l2st, cols.stop // NT)
                nc.vector.tensor_tensor(ln2_mean[:, cols], even, odd, ALU.add)
                nc.vector.tensor_tensor(ln2_tmp[:, 0, cols], even, odd, ALU.subtract)
                nc.vector.tensor_tensor(ln2_tmp[:, 1, cols], ln2_st[:, cols, 2], ln2_st[:, cols, 5],
                                        ALU.add).then_inc(s_l2mv, 1)
                dve.wait_ge(s_l2mv, 2 * k + 1)
                nc.vector.tensor_scalar(ln2_mean[:, cols], ln2_mean[:, cols], 0.5, None, ALU.mult)
                nc.vector.tensor_scalar(ln2_tmp[:, 1, cols], ln2_tmp[:, 1, cols], 1.0 / C, LN_EPS, ALU.mult, ALU.add)
                nc.vector.scalar_tensor_tensor(ln2_tmp[:, 2, cols], ln2_tmp[:, 0, cols], 0.25, ln2_tmp[:, 0, cols],
                                               ALU.mult, ALU.mult).then_inc(s_l2mv, 1)
                dve.wait_ge(s_l2mv, 2 * k + 2)
                nc.vector.tensor_tensor(ln2_var[:, cols], ln2_tmp[:, 1, cols], ln2_tmp[:, 2, cols],
                                        ALU.add).then_inc(s_l2var, 1)

            def step_b(i, n0):
                b = n0 + RING * i
                if n0 == B:
                    second_stats(0)
                if n0 + 2 < B:
                    for h in range(2):
                        maxima(i, n0 + 2, h)
                if n0 + 2 < B:
                    for h in range(2, 4):
                        maxima(i, n0 + 2, h)
                if n0 >= 2:
                    dve.wait_ge(s_proj, b - 1)
                    t_b = tok[:, ds(b - 2, 1), :, :].rearrange("p o t c -> p (o t) c")
                    nc.vector.tensor_tensor(t_b, bank[:, 6, T:T + NT * C].rearrange("p (t c) -> p t c", t=NT), t_b,
                                            ALU.add).then_inc(s_res, 1)
                if n0 + 2 < B:
                    for h in range(4, HEADS):
                        maxima(i, n0 + 2, h)
                if 1 <= n0 <= B:
                    dve.wait_ge(s_otr, b)
                    o = bank[:, 5, 0:4 * C].rearrange("p (n k) -> p n k", k=2 * HD)
                    nc.vector.reciprocal(rsum[:], o[:, :, HD]).then_inc(s_rsum, 1)
                if n0 >= 2:
                    wait_apart(dve, s_res, b - 1)
                    for t in range(NT):
                        last = nc.vector.bn_stats(
                            ln2_st[:, ds(2 * (b - 2) + t, 1), :].rearrange("p o k -> p (o k)"),
                            tok[:, ds(b - 2, 1), t, :].rearrange("p o c -> p (o c)"))
                    last.then_inc(s_l2st, 1)
                if 1 <= n0 <= B:
                    dve.wait_ge(s_rsum, b)
                    wait(dve, s_ont, b - 1)
                    nc.vector.tensor_tensor(o_norm[:].rearrange("p t (h d) -> p (t h) d", d=HD), o[:, :, 0:HD],
                                            rsum[:].unsqueeze(2).broadcast_to([P, NT * HEADS, HD]),
                                            ALU.mult).then_inc(s_on, 1)

            step_a(0, PAIRS)
            for h in range(HEADS):
                maxima(0, 0, h)
            step_a(0, PAIRS + 1)
            for h in range(HEADS):
                maxima(0, 1, h)
            dve.wait_ge(s_wps, 1)
            nc.vector.tensor_scalar(w_mean[0:C, 0, :], bank[0:C, 3, 0:QGROUPS], 1.0 / (W1_ROWS * C), None, ALU.mult)
            nc.vector.tensor_scalar(w_mean[:, 1, :], bank[:, 3, QGROUPS:2 * QGROUPS], 1.0 / (W2_ROWS * HID), None,
                                    ALU.mult).then_inc(s_wmean, 1)
            dve.wait_ge(s_wmean, 1)
            v1 = w1_b[:, 0:QGROUPS * W1_ROWS].rearrange("c (g r) -> c g r", g=QGROUPS)
            nc.vector.tensor_tensor(v1, v1, w_mean[0:C, 0, :].unsqueeze(2).broadcast_to([C, QGROUPS, W1_ROWS]),
                                    ALU.subtract).then_inc(s_wcen, 1)
            for k in range(HC):
                v2 = w2_b[:, k, 0:QGROUPS * W2_ROWS].rearrange("p (g r) -> p g r", g=QGROUPS)
                last = nc.vector.tensor_tensor(
                    v2, v2, w_mean[:, 1, :].unsqueeze(2).broadcast_to([P, QGROUPS, W2_ROWS]), ALU.subtract)
            last.then_inc(s_wcen, 1)
            nc.vector.memset(w1_b[:, QGROUPS * W1_ROWS:HID], 0.0)
            nc.vector.memset(w2_b[:, :, QGROUPS * W2_ROWS:C], 0.0).then_inc(s_wready, 1)

            step_b(0, 0)
            step_a(0, PAIRS + 2)
            step_b(0, 1)
            run(dve, step_b, **BB)

            second_stats(1)

            def bounds(gmax, lim, signal, count):
                nc.vector.tensor_scalar(gmax[:, 2:3], gmax[:, 1:2], Q_EPS, None, ALU.add).then_inc(signal[0], 1)
                dve.wait_ge(signal[0], 3 * count - 2)
                nc.vector.reciprocal(gmax[:, 3:4], gmax[:, 2:3]).then_inc(signal[0], 1)
                top = (QB - Q_EPS) / QB
                nc.vector.tensor_scalar(lim[:, 1:2], gmax[:, 2:3], top, None, ALU.mult)
                nc.vector.tensor_scalar(lim[:, 2:3], gmax[:, 2:3], -top, None, ALU.mult).then_inc(signal[0], 1)
                dve.wait_ge(signal[0], 3 * count)
                nc.vector.tensor_scalar(lim[:, 0:1], gmax[:, 3:4], QB, None, ALU.mult).then_inc(signal[1], 1)

            def largest_hidden(g, r):
                dve.wait_ge(s_y1, 2 * HC * g + r + 1)
                return nc.vector.tensor_reduce(amax1[:, r:r + 1], y1_ring[:, g % 2, r * HALF:(r + 1) * HALF],
                                               op=ALU.max, axis=AX.X, apply_absolute_value=True)

            for n in range(C_STEPS):
                if 1 <= n <= QGROUPS:
                    dve.wait_ge(s_sc1, n)
                    for half in range(2):
                        y = y1_ring[:, (n - 1) % 2, half * HC * HALF:(half + 1) * HC * HALF]
                        lim = lim1[:, (n - 1) % 2, :]
                        nc.vector.tensor_scalar(y, y, lim[:, 1:2], lim[:, 2:3], ALU.min, ALU.max).then_inc(s_clip1, 1)
                if n < QGROUPS:
                    for r in range(HC):
                        largest_hidden(n, r)
                if n >= 2:
                    y = y2_ring[:, n % 2, :]
                    for half in range(2):
                        dve.wait_ge(s_y2, 2 * (n - 2) + half + 1)
                        last = nc.vector.tensor_reduce(amax2[0:C, half:half + 1], y[:, half * HALF:(half + 1) * HALF],
                                                       op=ALU.max, axis=AX.X, apply_absolute_value=True)
                    last.then_inc(s_am2, 1)
                    dve.wait_ge(s_am2, n - 1)
                    nc.vector.tensor_reduce(gmax2[0:C, 0:1], amax2[0:C, :], op=ALU.max, axis=AX.X).then_inc(s_gm2, 1)
                if n < QGROUPS:
                    for r in range(HC, 2 * HC):
                        last = largest_hidden(n, r)
                    last.then_inc(s_am1, 1)
                    dve.wait_ge(s_am1, n + 1)
                    nc.vector.tensor_reduce(gmax1[:, 0:1], amax1[:], op=ALU.max, axis=AX.X).then_inc(s_gm1, 1)
                if n >= 2:
                    dve.wait_ge(s_ar2, n - 1)
                    bounds(gmax2[0:C, :], lim2[0:C, :], (s_bd2, s_sc2), n - 1)
                    nc.vector.tensor_scalar(y, y, lim2[0:C, 1:2], lim2[0:C, 2:3], ALU.min, ALU.max).then_inc(s_clip2, 1)
                if n < QGROUPS:
                    dve.wait_ge(s_ar1, n + 1)
                    wait(dve, s_h, 2 * (n - 1))
                    bounds(gmax1[:, :], lim1[:, n % 2, :], (s_bd1, s_sc1), n + 1)
                if n >= 2:
                    dve.wait_ge(s_clip2, n - 1)
                    dve.wait_ge(s_sc2, n - 1)
                    dve.wait_ge(s_t2t, n - 1)
                    wait(dve, s_store[n % 2], 16 * ((n - 4) // 2 + 1))
                    for half in range(2):
                        cols = slice(half * HALF, (half + 1) * HALF)
                        last = nc.vector.scalar_tensor_tensor(out_ring[:, n % 2, cols], y[:, cols], lim2[0:C, 0:1],
                                                              bank[0:C, 6 + half, 0:HALF], ALU.mult, ALU.add)
                    last.then_inc(s_out, 1)
            dve.wait_ge(s_t2t, QGROUPS + 1)
            dve.wait_ge(s_store[1], 16 * 2)
            nc.vector.tensor_copy(out_ring[:, 1, 0:T], bank[0:C, 0, 0:T]).then_inc(s_out, 1)

        @block.tensor
        def _(pe):
            pe.wait_ge(s_ident, 1)
            pe.wait_ge(s_weights, 16 * 6)
            for k in range(HC):
                last = nc.tensor.transpose(bank[0:C, 5, k * P:(k + 1) * P], w1_in[:, k, :], ident[:])
            last.then_inc(s_wtr, 1)
            for k in range(HC):
                last = nc.tensor.transpose(bank[:, 7, k * C:(k + 1) * C], w2_in[:, k * P:(k + 1) * P], ident[0:C, 0:C])
            last.then_inc(s_wtr, 1)
            same = cst[0:C, O_SAME:O_SAME + C]
            pe.wait_ge(s_small, 16 * 4)
            pe.wait_ge(s_gmv, 1)
            nc.tensor.matmul(bank[0:C, 4, 0:B], same, gn_mv[:, :, 0], start=True, stop=True).then_inc(s_gps, 1)
            pe.wait_ge(s_gdve, 3)
            nc.tensor.matmul(bank[0:C, 4, B:2 * B], same, gn_tmp[:, 0, :], start=True, stop=True).then_inc(s_gps, 1)

            def transpose_pair(i, n0):
                j, s = n0 + 2 * i, n0 % 2
                pe.wait_ge(s_xn, j + 1)
                wait(pe, s_xs, j - 1)
                for t in range(NT):
                    for u in range(2):
                        k = 2 * t + u
                        last = nc.tensor.transpose(bank[:, s, k * C:(k + 1) * C], xn_ring[:, s, u, t * P:(t + 1) * P],
                                                   ident[0:C, 0:C])
                last.then_inc(s_xnt, 1)

            def convolve(i, n0, t, k):
                s = n0 % 2
                dst = bank[:, 2 + s, t * 2 * C:(t + 1) * 2 * C]
                for p in range(POINTS):
                    w = toep[:, p, k].rearrange("p y x -> p (y x)")[:, t * P:(t + 1) * P]
                    nc.tensor.matmul(dst, w, xs_ring[:, s, p, k].rearrange("p b c -> p (b c)"),
                                     start=(k == 0 and p == 0), stop=False)
                if k == NT - 1:
                    for u in range(2):
                        last = nc.tensor.matmul(dst[:, u * C:(u + 1) * C], x_ring[:, s, u, t * P:(t + 1) * P],
                                                ident[0:C, 0:C], start=False, stop=(u == 1))
                    return last

            def transpose_qk(i, n0, u):
                b = 2 * (n0 + 2 * i) + u
                pe.wait_ge(s_rope, b + 1)
                wait(pe, s_rest, b)
                for side in range(2):
                    for t in range(NT):
                        last = nc.tensor.transpose(bank[0:C, 7, side * T + t * P:side * T + (t + 1) * P],
                                                   qr_ring[:, u, (2 * t + side) * C:(2 * t + side + 1) * C], ident[:])
                last.then_inc(s_qkt, 1)

            def project_qkv(i, n0, u):
                b = 2 * (n0 + 2 * i) + u
                wait(pe, s_qk, b)
                wait(pe, s_vc, b)
                for t in range(NT):
                    last = nc.tensor.matmul(bank[:, 5 + t, 0:3 * C],
                                            lt_ring[:, n0 % 2, (2 * u + t) * P:(2 * u + t + 1) * P], wa[:],
                                            start=True, stop=True)
                last.then_inc(s_qkv, 1)

            transpose_pair(0, 0)
            pe.wait_ge(s_toep, POINTS)
            pe.wait_ge(s_wcopy, 2)

            def step_a(i, n0):
                j = n0 + 2 * i
                if n0 < PAIRS:
                    pe.wait_ge(s_xr[n0 % 2], 16 * (n0 // 2 + i + 1))
                    pe.wait_ge(s_xs, j + 1)
                    wait(pe, s_tok, j - 1)
                    convolve(i, n0, 0, 0)
                if n0 + 1 < PAIRS:
                    transpose_pair(i, n0 + 1)
                if 2 <= n0 <= PAIRS + 1:
                    project_qkv(i, n0 - 2, 1)
                if n0 < PAIRS:
                    convolve(i, n0, 0, 1)
                    convolve(i, n0, 1, 0)
                if 2 <= n0 <= PAIRS + 1:
                    transpose_qk(i, n0 - 2, 0)
                if 1 <= n0 <= PAIRS:
                    pe.wait_ge(s_xl, j)
                    wait(pe, s_lt, j - 1)
                    for t in range(4):
                        last = nc.tensor.transpose(bank[0:C, 4, t * P:(t + 1) * P], xl_ring[:, (n0 - 1) % 2, t, :],
                                                   ident[:])
                    last.then_inc(s_xlt, 1)
                if n0 < PAIRS:
                    convolve(i, n0, 1, 1).then_inc(s_cv, 1)
                if 2 <= n0 <= PAIRS + 1:
                    transpose_qk(i, n0 - 2, 1)
                if 1 <= n0 <= PAIRS:
                    pe.wait_ge(s_lt, j)
                    project_qkv(i, n0 - 1, 0)
            run(pe, step_a, **A)

            def scores_q(i, n0, h):
                b, slot = n0 + RING * i, n0 % RING
                if h == 0:
                    pe.wait_ge(s_stack[slot], 16 * len(SLOTS) * (n0 // RING + i + 1))
                wait(pe, s_max, HEADS * b + h - 2)
                if h == 2:
                    wait(pe, s_mtc, b)
                for t in range(NT):
                    first, size = t * P, (t + 1) * P
                    nc.tensor.matmul(bank[:, h % 3, first:first + size],
                                     stack[0:KROWS, slot, h, 0, t * P:(t + 1) * P],
                                     stack[0:KROWS, slot, h, 1, 0:size], start=True, stop=False)
                    last = nc.tensor.matmul(bank[:, h % 3, first + t * P:first + size], ident16[:], mask16[:],
                                            start=False, stop=True)
                last.then_inc(s_sq, 1)

            def scores_k(i, n0, hp):
                b, slot = n0 + RING * i, n0 % RING
                if hp == 0:
                    pe.wait_ge(s_mrow[slot], 16 * NT * (n0 // RING + i + 1))
                wait(pe, s_exp, 3 * b + hp)
                for e in range(2):
                    h = 2 * hp + e
                    nc.tensor.matmul(bank[:, 3 + e, P:P + T], stack[0:KROWS + 1, slot, h, 1, 0:P],
                                     stack[0:KROWS + 1, slot, h, 0, :], start=True, stop=True)
                    last = nc.tensor.matmul(bank[:, 3 + e, 0:P], stack[0:KROWS + 1, slot, h, 1, P:T],
                                            stack[0:KROWS + 1, slot, h, 0, P:T], start=True, stop=True)
                last.then_inc(s_sk, 1)

            def transpose_max(i, n0):
                b = n0 + RING * i
                pe.wait_ge(s_max, HEADS * (b + 1))
                wait(pe, s_mtc, b)
                nc.tensor.transpose(bank[0:NT * HEADS, 2, 3 * P:4 * P], nmax[:, n0 % 2, :], ident[:]).then_inc(s_mt, 1)

            def weighted_values(i, n0):
                b, s = n0 + RING * i, n0 % 2
                pe.wait_ge(s_sel, 3 * (b + 1))
                pe.wait_ge(s_v, b + 1)
                wait(pe, s_o, b)
                for g in range(2):
                    for t in range(NT):
                        for e in range(3):
                            h = 3 * g + e
                            rows = slice(2 * HD * e, 2 * HD * (e + 1))
                            w = v_ring[:, s, t, h, :]
                            if t == 0:
                                nc.tensor.matmul(bank[rows, 7, g * T:(g + 1) * T], w, pt_ring[:, s, h, P:P + T],
                                                 start=True, stop=False)
                            else:
                                last = nc.tensor.matmul(bank[rows, 7, g * T + P:(g + 1) * T], w,
                                                        pt_ring[:, s, h, 0:P], start=False, stop=True)
                last.then_inc(s_pv, 1)

            def transpose_o(i, n0):
                b, s = n0 + RING * i, n0 % 2
                pe.wait_ge(s_o, b + 1)
                wait(pe, s_on, b)
                for t in range(NT):
                    for g in range(2):
                        k = 2 * t + g
                        last = nc.tensor.transpose(bank[:, 5, k * C:(k + 1) * C],
                                                   o_ring[:, s, g * T + t * P:g * T + (t + 1) * P], ident[0:C, 0:C])
                last.then_inc(s_otr, 1)

            def transpose_norm(i, n0):
                b = n0 + RING * i
                pe.wait_ge(s_on, b + 1)
                wait(pe, s_res, b)
                for t in range(NT):
                    last = nc.tensor.transpose(bank[0:C, 6, t * P:(t + 1) * P], o_norm[:, t, :], ident[:])
                last.then_inc(s_ont, 1)

            def project_out(i, n0):
                b, s = n0 + RING * i, n0 % 2
                pe.wait_ge(s_ontc, b + 1)
                for t in range(NT):
                    last = nc.tensor.matmul(bank[:, 6, T + t * C:T + (t + 1) * C], ot_ring[:, s, t * P:(t + 1) * P],
                                            wp[:], start=True, stop=True)
                last.then_inc(s_proj, 1)

            def step_b(i, n0):
                for hp in range(3):
                    if n0 < B:
                        scores_k(i, n0, hp)
                    if n0 >= 2 and hp == 1:
                        project_out(i, n0 - 2)
                    if n0 + 2 < B:
                        for h in (2 * hp, 2 * hp + 1):
                            scores_q(i, n0 + 2, h)
                    if n0 + 1 < B and hp == 0:
                        transpose_max(i, n0 + 1)
                    if n0 >= 2 and hp == 0:
                        transpose_norm(i, n0 - 2)
                    if 1 <= n0 <= B and hp == 0:
                        weighted_values(i, n0 - 1)
                    if 1 <= n0 <= B and hp == 1:
                        transpose_o(i, n0 - 1)

            step_a(0, PAIRS)
            pe.wait_ge(s_xs, PAIRS)
            pe.wait_ge(s_tok, PAIRS)
            pe.wait_ge(s_id16, 1)
            pe.wait_ge(s_vones, 1)
            pe.wait_ge(s_setup, 1)
            pe.wait_ge(s_wsum, 2)
            nc.tensor.matmul(bank[0:C, 3, 0:QGROUPS], ones[0:C, 0:C], w_sum[0:C, 0, :], start=True, stop=True)
            nc.tensor.matmul(bank[:, 3, QGROUPS:2 * QGROUPS], ones[:], w_sum[:, 1, :], start=True,
                             stop=True).then_inc(s_wps, 1)
            for h in range(HEADS):
                scores_q(0, 0, h)
            transpose_max(0, 0)
            step_a(0, PAIRS + 1)
            for h in range(HEADS):
                scores_q(0, 1, h)
            pe.wait_ge(s_wmean, 1)
            pe.wait_ge(s_lt, PAIRS)
            step_b(0, 0)
            step_a(0, PAIRS + 2)
            pe.wait_ge(s_vc, B)
            pe.wait_ge(s_rest, B)
            step_b(0, 1)
            run(pe, step_b, **BB)

            pe.wait_ge(s_res, B)
            pe.wait_ge(s_wsign, 1)
            pe.wait_ge(s_wready, 1)

            def transpose_x2(g):
                pe.wait_ge(s_x2, g + 1)
                for half in range(2):
                    wait(pe, s_x2c, 2 * (g - 1) + half + 1)
                    for t in range(3):
                        last = nc.tensor.transpose(bank[0:C, half, t * P:(t + 1) * P], x2_ring[:, g % 2, 3 * half + t, :],
                                                   ident[:])
                    last.then_inc(s_x2t, 1)

            def first_product(g, r):
                half, k = r // HC, r % HC
                pe.wait_ge(s_x2c, 2 * g + half + 1)
                wait(pe, s_y1, 2 * HC * g + r - 1)
                nc.tensor.matmul(bank[:, 2 + r % 2, 0:HALF], w1_b[:, k * P:(k + 1) * P],
                                 x2t_ring[:, g % 2, half * HALF:(half + 1) * HALF],
                                 start=True, stop=True).then_inc(s_f1, 1)

            def second_product(g, half):
                pe.wait_ge(s_h, 2 * g + half + 1)
                wait(pe, s_y2, 2 * (g - 1) + half + 1)
                for k in range(HC):
                    r = half * HC + k
                    last = nc.tensor.matmul(bank[0:C, 4 + half, 0:HALF], w2_b[:, k, :],
                                            h_ring[:, g % 2, r * HALF:(r + 1) * HALF],
                                            start=(k == 0), stop=(k == HC - 1))
                last.then_inc(s_f2, 1)

            def residual(g):
                wait(pe, s_out, g)
                for half in range(2):
                    for t in range(3):
                        k = 3 * half + t
                        last = nc.tensor.transpose(bank[0:C, 6 + half, t * P:(t + 1) * P],
                                                   tok[:, GB * g + k // NT, k % NT, :], ident[:])
                last.then_inc(s_t2t, 1)

            transpose_x2(0)
            for n in range(C_STEPS):
                if n < QGROUPS:
                    for r in range(HC):
                        first_product(n, r)
                if n >= 2:
                    residual(n - 2)
                if n < QGROUPS:
                    for r in range(HC, 2 * HC):
                        first_product(n, r)
                if 1 <= n <= QGROUPS:
                    second_product(n - 1, 0)
                if n + 1 < QGROUPS:
                    transpose_x2(n + 1)
                if 1 <= n <= QGROUPS:
                    second_product(n - 1, 1)
            for t in range(NT):
                last = nc.tensor.transpose(bank[0:C, 0, t * P:(t + 1) * P], tok[:, B - 1, t, :], ident[:])
            last.then_inc(s_t2t, 1)


_INS = ["x", "L0_conv_weight_coord", "L0_conv_radius", "L0_conv_weights", "L1_attn_w_attn", "L1_attn_w_proj",
        "L1_ffn_W1", "L1_ffn_b1", "L1_ffn_W2", "L1_ffn_b2"]


def kernel(**inputs):
    import numpy as _np
    import concourse.bacc as _bacc
    from concourse import mybir as _mybir
    from concourse.bass_utils import run_bass_kernel_spmd as _run

    nc = _bacc.Bacc("TRN2", target_bir_lowering=False, num_devices=1)
    arrays, args = {}, []
    for name in _INS:
        a = _np.ascontiguousarray(inputs[name])
        arrays[f"in_{name}"] = a
        args.append(nc.dram_tensor(f"in_{name}", a.shape, _mybir.dt.from_np(a.dtype), kind="ExternalInput").ap())
    table = shape_constants()
    arrays["in_const"] = table
    args.append(nc.dram_tensor("in_const", table.shape, _mybir.dt.float32, kind="ExternalInput").ap())
    args.append(nc.dram_tensor("out_0", (B, C, SIDE, SIDE), _mybir.dt.float32, kind="ExternalOutput").ap())
    build(nc, *args)
    r = _run(nc, [arrays], core_ids=[0])
    return r.results[0]["out_0"]
```

```python
from contextlib import ExitStack

import numpy as np

import concourse.bass as bass
from concourse import mybir

F32 = mybir.dt.float32
BF16 = mybir.dt.bfloat16
ALU = mybir.AluOpType
ACT = mybir.ActivationFunctionType
AX = mybir.AxisListType
ds = bass.ds

P = 128
B, C, SIDE = 16, 96, 16
T = SIDE * SIDE
NT = T // P
HEADS = 6
HD = C // HEADS
KSIZE = 11
POINTS = 4
PAIRS = B // 2
HID = 4 * C
HC = HID // P
QGROUPS = 5
GB = B // QGROUPS
GT = GB * T
HALF = GT // 2
GN_GROUP = 3
W1_ROWS = HID // QGROUPS
W2_ROWS = C // QGROUPS
GN_EPS, LN_EPS, Q_EPS, QB = 1e-5, 1e-5, 1e-5, 128.0
NEG = -1e30
SLOTS = [(0, 0), (0, 1), (0, 2), (1, 0), (1, 1), (2, 0)]
KROWS = len(SLOTS) * HD
GN_COLS = [slice(0, 4), slice(4, B)]
LN2_COLS = [slice(g * GB * NT, min(g + 2, QGROUPS) * GB * NT) for g in range(0, QGROUPS, 2)]
RING = 6


def shape_constants():
    lin = np.linspace(-1.0, 1.0, KSIZE).astype(np.float32)
    pad = KSIZE // 2
    row = np.arange(P)
    ix, o = row % SIDE, np.arange(SIDE)
    dx = ix[:, None] - o[None] + pad
    gx = np.where((dx >= 0) & (dx < KSIZE), lin[np.clip(dx, 0, KSIZE - 1)], np.float32(1e30))
    gy = []
    for half in range(NT):
        iy = half * (P // SIDE) + row // SIDE
        dy = iy[:, None] - o[None] + pad
        gy.append(np.where((dy >= 0) & (dy < KSIZE), lin[np.clip(KSIZE - 1 - dy, 0, KSIZE - 1)], np.float32(1e30)))
    inv = (1.0 / np.float32(10000.0) ** (np.arange(0, HD, 2, dtype=np.float32) / np.float32(HD))).astype(np.float32)
    ang = np.repeat(np.arange(T, dtype=np.float32)[:, None] * inv[None], 2, axis=1)
    sign = np.where(np.arange(HD) % 2 == 0, -1.0, 1.0).astype(np.float32)
    lay = lambda t: np.tile(t.reshape(NT, P, 1, HD), (1, 1, 2 * HEADS, 1)).transpose(1, 0, 2, 3).reshape(P, -1)
    same = np.zeros((P, C), np.float32)
    c = np.arange(C)
    same[:C] = (c[:, None] // GN_GROUP == c[None] // GN_GROUP)
    parts = [gx, gy[0], gy[1], lay(np.cos(ang)), lay(np.sin(ang) * sign), same]
    return np.ascontiguousarray(np.concatenate([a.astype(np.float32) for a in parts], axis=1))


N_GRID = SIDE + NT * SIDE
N_ROPE = NT * 2 * C
O_COS, O_SIN, O_SAME = N_GRID, N_GRID + N_ROPE, N_GRID + 2 * N_ROPE
N_CONST = O_SAME + C


def build(nc, x, weight_coord, radius, conv_w, w_attn, w_proj, w1, b1, w2, b2, const, out):
    x_v = x.rearrange("b c h w -> c b (h w)")
    out_v = out.rearrange("b c h w -> c b (h w)")
    with ExitStack() as ctx:
        def sb(name, shape, dt=F32):
            return ctx.enter_context(nc.sbuf_tensor(name, shape, dt))

        def sem(name):
            return ctx.enter_context(nc.semaphore(name))

        x_ring = sb("x_ring", [C, 2, 2, T])
        xn_ring = sb("xn_ring", [C, 2, 2, T])
        tok = sb("tok", [P, B, NT, C])
        xs_ring = sb("xs_ring", [P, 2, POINTS, NT, 2, C])
        toep = sb("toep", [P, POINTS, NT, SIDE, SIDE])
        cst = sb("cst", [P, N_CONST])
        wc_bc = sb("wc_bc", [P, POINTS * 2])
        rad_bc = sb("rad_bc", [P, POINTS])
        cw_bc = sb("cw_bc", [P, C, POINTS])
        grid_t = sb("grid_t", [P, POINTS, N_GRID])
        grid_n = sb("grid_n", [P, POINTS, N_GRID])
        nrinv = sb("nrinv", [P, 2, POINTS])
        ident = sb("ident", [P, P])
        ident16 = sb("ident16", [P, P], BF16)
        mask = sb("mask", [P, P])
        mask16 = sb("mask16", [P, P], BF16)
        ones = sb("ones", [P, P])
        mhalf = sb("mhalf", [P, B * NT])
        gn_st = sb("gn_st", [C, B, 6])
        gn_mv = sb("gn_mv", [C, B, 2])
        gn_tmp = sb("gn_tmp", [C, 3, B])
        gn_mean = sb("gn_mean", [C, B])
        gn_rstd = sb("gn_rstd", [C, B])
        ln_st = sb("ln_st", [P, 2, 4, 6])
        ln_mv = sb("ln_mv", [P, 2, 4, 2])
        ln_var = sb("ln_var", [P, 2, 4])
        ln_rstd = sb("ln_rstd", [P, 2, 4])
        xl_ring = sb("xl_ring", [P, 2, 4, C])
        lt_ring = sb("lt_ring", [C, 2, 4 * P])
        wa = sb("wa", [C, 3 * C])
        wp = sb("wp", [C, C])
        qk_ring = sb("qk_ring", [P, 2, N_ROPE])
        rc_ring = sb("rc_ring", [P, 2, N_ROPE])
        rs_tmp = sb("rs_tmp", [P, N_ROPE])
        qr_ring = sb("qr_ring", [P, 2, N_ROPE])
        rest_ring = sb("rest_ring", [C, 2, 2, T])
        parts = sb("parts", [P, B * 3 * 2 * T], BF16)
        v_all = sb("v_all", [P, B, NT, C])
        stack = sb("stack", [P, RING, HEADS, 2, T], BF16)
        x_all = stack[0:C, :, :, :, :].rearrange("p r h s n -> p (r h s n)").bitcast(F32)[:, 0:B * T]
        x_all = x_all.rearrange("c (b n) -> c b n", b=B)
        v_ring = sb("v_ring", [P, 2, NT, HEADS, 2 * HD])
        pt_ring = sb("pt_ring", [P, 2, HEADS, T + P])
        nmax = sb("nmax", [P, 2, NT * HEADS])
        nmax_t = sb("nmax_t", [NT * HEADS, 2, P], BF16)
        o_ring = sb("o_ring", [C, 2, 2 * T])
        rsum = sb("rsum", [P, NT * HEADS])
        o_norm = sb("o_norm", [P, NT, C])
        ot_ring = sb("ot_ring", [C, 2, T])
        ln2_st = sb("ln2_st", [P, B * NT, 6])
        ln2_mean = sb("ln2_mean", [P, B * NT])
        ln2_tmp = sb("ln2_tmp", [P, 3, B * NT])
        ln2_var = sb("ln2_var", [P, B * NT])
        ln2_rstd = sb("ln2_rstd", [P, B * NT])
        w1_in = sb("w1_in", [P, HC, C])
        w1_b = sb("w1_b", [C, HID])
        w2_in = sb("w2_in", [C, HID])
        w2_b = sb("w2_b", [P, HC, C])
        w_sum = sb("w_sum", [P, 2, QGROUPS])
        w_mean = sb("w_mean", [P, 2, QGROUPS])
        b1_s = sb("b1_s", [P, HC])
        b2_s = sb("b2_s", [C, 1])
        warm = sb("warm", [1, 1])
        amax1 = sb("amax1", [P, 2 * HC])
        amax2 = sb("amax2", [P, 2])
        gmax1 = sb("gmax1", [P, 4])
        gmax2 = sb("gmax2", [P, 4])
        lim1 = sb("lim1", [P, 2, 4])
        lim2 = sb("lim2", [P, 4])

        parts_v = parts[0:C, :].rearrange("c (b s k n) -> c (b s) k n", b=B, s=2, k=3)
        wide = parts[:, :].bitcast(F32)
        n_y1 = 2 * HC * HALF
        y1_ring = wide[:, 0:2 * n_y1].rearrange("p (s n) -> p s n", s=2)
        h_ring = wide[:, 2 * n_y1:4 * n_y1].rearrange("p (s n) -> p s n", s=2)
        x2t_ring = wide[0:C, 4 * n_y1:4 * n_y1 + 2 * GT].rearrange("p (s n) -> p s n", s=2)
        y2_ring = wide[0:C, 4 * n_y1 + 2 * GT:4 * n_y1 + 4 * GT].rearrange("p (s n) -> p s n", s=2)
        flat = xs_ring[:, :, :, :, :, :].rearrange("p s q t b c -> p (s q t b c)")
        out_ring = flat[0:C, 0:2 * GT].rearrange("p (s n) -> p s n", s=2)
        last_out = flat[0:C, 2 * (GT + GB * NT * C):2 * (GT + GB * NT * C) + T]
        x2_ring = flat[:, 2 * GT:2 * GT + 2 * GB * NT * C].rearrange("p (s t c) -> p s t c", s=2, c=C)

        bank = ctx.enter_context(nc.psum_tensor("bank", [P, 8, 512], F32))

        s_xall = [sem(f"s_xall{i}") for i in range(4)]
        s_small = sem("s_small")
        s_weights = sem("s_weights")
        s_xr = [sem(f"s_xr{i}") for i in range(2)]
        s_zero = sem("s_zero")
        s_ident = sem("s_ident")
        s_setup = sem("s_setup")
        s_id16 = sem("s_id16")
        s_vones = sem("s_vones")
        s_rinv = sem("s_rinv")
        s_cw = sem("s_cw")
        s_same = sem("s_same")
        s_ropet = sem("s_ropet")
        s_gsq = sem("s_gsq")
        s_gvar = sem("s_gvar")
        s_grid = sem("s_grid")
        s_kones = sem("s_kones")
        s_cone = sem("s_cone")
        s_toep = sem("s_toep")
        s_gst = sem("s_gst")
        s_gmv = sem("s_gmv")
        s_gps = sem("s_gps")
        s_gnsteps = sem("s_gnsteps")
        s_grstd = sem("s_grstd")
        s_wtr = sem("s_wtr")
        s_wcopy = sem("s_wcopy")
        s_wsum = sem("s_wsum")
        s_wps = sem("s_wps")
        s_wmean = sem("s_wmean")
        s_wcen = sem("s_wcen")
        s_wsign = sem("s_wsign")
        s_wready = sem("s_wready")
        s_xn = sem("s_xn")
        s_xnt = sem("s_xnt")
        s_xs = sem("s_xs")
        s_cv = sem("s_cv")
        s_tok = sem("s_tok")
        s_lnst = sem("s_lnst")
        s_lnmv = sem("s_lnmv")
        s_lnvar = sem("s_lnvar")
        s_lnrstd = sem("s_lnrstd")
        s_xl = sem("s_xl")
        s_xlt = sem("s_xlt")
        s_lt = sem("s_lt")
        s_qkv = sem("s_qkv")
        s_qk = sem("s_qk")
        s_vc = sem("s_vc")
        s_rcos = sem("s_rcos")
        s_rsin = sem("s_rsin")
        s_rope = sem("s_rope")
        s_qkt = sem("s_qkt")
        s_p0 = sem("s_p0")
        s_rest = sem("s_rest")
        s_p1 = sem("s_p1")
        s_p2 = sem("s_p2")
        s_stack = [sem(f"s_stack{i}") for i in range(RING)]
        s_mrow = [sem(f"s_mrow{i}") for i in range(RING)]
        s_sq = sem("s_sq")
        s_max = sem("s_max")
        s_mt = sem("s_mt")
        s_mtc = sem("s_mtc")
        s_sk = sem("s_sk")
        s_exp = sem("s_exp")
        s_sel = sem("s_sel")
        s_v = sem("s_v")
        s_pv = sem("s_pv")
        s_o = sem("s_o")
        s_otr = sem("s_otr")
        s_rsum = sem("s_rsum")
        s_on = sem("s_on")
        s_ont = sem("s_ont")
        s_ontc = sem("s_ontc")
        s_proj = sem("s_proj")
        s_res = sem("s_res")
        s_l2st = sem("s_l2st")
        s_l2mv = sem("s_l2mv")
        s_l2var = sem("s_l2var")
        s_l2rstd = sem("s_l2rstd")
        s_x2m = sem("s_x2m")
        s_x2 = sem("s_x2")
        s_x2t = sem("s_x2t")
        s_x2c = sem("s_x2c")
        s_f1 = sem("s_f1")
        s_y1 = sem("s_y1")
        s_am1 = sem("s_am1")
        s_gm1 = sem("s_gm1")
        s_ar1 = sem("s_ar1")
        s_bd1 = sem("s_bd1")
        s_sc1 = sem("s_sc1")
        s_clip1 = sem("s_clip1")
        s_h = sem("s_h")
        s_f2 = sem("s_f2")
        s_y2 = sem("s_y2")
        s_am2 = sem("s_am2")
        s_gm2 = sem("s_gm2")
        s_ar2 = sem("s_ar2")
        s_bd2 = sem("s_bd2")
        s_sc2 = sem("s_sc2")
        s_clip2 = sem("s_clip2")
        s_t2t = sem("s_t2t")
        s_out = sem("s_out")
        s_t2last = sem("s_t2last")
        s_last = sem("s_last")
        s_last_store = sem("s_last_store")
        s_store = [sem(f"s_store{i}") for i in range(2)]

        block = ctx.enter_context(nc.Block())

        def wait(eng, semaphore, count):
            if isinstance(count, int) and count <= 0:
                return
            eng.wait_ge(semaphore, count)

        def wait_apart(eng, semaphore, count):
            if not isinstance(count, int):
                eng.compute_val(count)
            eng.wait_ge(s_ident, 1)
            wait(eng, semaphore, count)

        def run(eng, step, first, unroll, laps, last, start=0):
            for n in range(start, first):
                step(0, n)
            with eng.Fori(0, laps) as i:
                for u in range(unroll):
                    step(i, first + u)
            for n in range(first + unroll * laps, last):
                step(0, n)

        A = dict(first=3, unroll=2, laps=2, last=PAIRS)
        BB = dict(start=2, first=2, unroll=RING, laps=2, last=B - 2)
        C_STEPS = QGROUPS + 2

        @block.sync
        def _(sp):
            sp.dma_start(x_all[:, 0:4, :], x_v[:, 0:4, :]).then_inc(s_xall[0], 16)
            sp.dma_start(cst[:, 0:N_GRID], const[:, 0:N_GRID]).then_inc(s_small, 16)
            sp.dma_start(cst[:, O_SAME:N_CONST], const[:, O_SAME:N_CONST]).then_inc(s_same, 16)
            sp.dma_start(x_all[:, 8:12, :], x_v[:, 8:12, :]).then_inc(s_xall[2], 16)
            for k in range(2):
                sp.dma_start(x_ring[:, k, :, :], x_v[:, 2 * k:2 * k + 2, :]).then_inc(s_xr[k], 16)
            sp.dma_start(cst[:, O_COS:O_SAME], const[:, O_COS:O_SAME]).then_inc(s_ropet, 16)
            sp.dma_start(wa[:], w_attn).then_inc(s_weights, 16)
            sp.dma_start(wp[:], w_proj).then_inc(s_weights, 16)

            def load_x(i, n0):
                wait(sp, s_cv, n0 - 1 + 2 * i)
                b = 2 * n0 + 4 * i
                sp.dma_start(x_ring[:, n0 % 2, :, :], x_v[:, ds(b, 2), :]).then_inc(s_xr[n0 % 2], 16)
            with sp.Fori(0, PAIRS // 2 - 1) as i:
                for u in range(2):
                    load_x(i, 2 + u)
            sp.wait_ge(s_xn, PAIRS)

            def stack_image(i, n0):
                b, slot = n0 + RING * i, n0 % RING
                for r, (kp, qp) in enumerate(SLOTS):
                    q_part = parts[0:C, ds((b * 6 + qp) * T, T)]
                    src = bass.AP(q_part.tensor, q_part.offset, [q_part.ap[0], [(3 + kp - qp) * T, 2], [1, T]])
                    dst = stack[r * HD:(r + 1) * HD, slot, :, :, :].rearrange("d h s n -> d (h s n)")
                    sp.dma_start(dst, src).then_inc(s_stack[slot], 16)

            def stack_ready(i, n0):
                b = n0 + RING * i
                wait_apart(sp, s_p0, b + 1)
                wait(sp, s_p1, b + 1)
                wait(sp, s_p2, b + 1)
                wait(sp, s_sk, HEADS * (b - RING + 2))

            def max_row(i, n0):
                b, slot = n0 + RING * i, n0 % RING
                wait(sp, s_mtc, b + 1)
                for t in range(NT):
                    sp.dma_start(stack[KROWS:KROWS + 1, slot, :, 0, t * P:(t + 1) * P],
                                 nmax_t[t * HEADS:(t + 1) * HEADS, n0 % 2, :]).then_inc(s_mrow[slot], 16)

            for n in range(4):
                stack_ready(0, n)
                stack_image(0, n)
            max_row(0, 0)

            def step_b(i, n0):
                max_row(i, n0 - 3)
                stack_ready(i, n0)
                stack_image(i, n0)
            run(sp, step_b, start=4, first=4, unroll=RING, laps=2, last=B)
            for n in range(B - 3, B):
                max_row(0, n)

            for g in range(QGROUPS):
                if g == QGROUPS - 1:
                    sp.wait_ge(s_last, 1)
                    sp.dma_start(out_v[:, B - 1, :], last_out).then_inc(s_last_store, 16)
                sp.wait_ge(s_out, g + 1)
                sp.dma_start(out_v[:, g * GB:(g + 1) * GB, :],
                             out_ring[:, g % 2, :].rearrange("c (b n) -> c b n", b=GB)).then_inc(s_store[g % 2], 16)
            sp.wait_ge(s_store[0], 16 * 3)
            sp.wait_ge(s_store[1], 16 * 2)
            sp.wait_ge(s_last_store, 16)

        @block.gpsimd
        def _(pool):
            nc.gpsimd.memset(ident[:], 0.0)
            nc.gpsimd.memset(mask[:], 0.0)
            nc.gpsimd.memset(mhalf[:], -0.5).then_inc(s_zero, 1)
            pool.wait_ge(s_zero, 1)
            nc.gpsimd.affine_select(out=ident[:], in_=ident[:], compare_op=ALU.not_equal, fill=1.0, base=0,
                                    pattern=[[-1, P]], channel_multiplier=1).then_inc(s_ident, 1)
            nc.gpsimd.affine_select(out=mask[:], in_=mask[:], compare_op=ALU.is_ge, fill=NEG, base=0,
                                    pattern=[[-1, P]], channel_multiplier=1)
            nc.gpsimd.memset(ones[:], 1.0).then_inc(s_setup, 1)

            def gn_rstds(k):
                cols = GN_COLS[k]
                pool.wait_ge(s_gvar, k + 1)
                nc.gpsimd.tensor_tensor(gn_rstd[:, cols], gn_tmp[:, 2, cols], mhalf[0:C, cols],
                                        ALU.pow).then_inc(s_grstd, 1)
            gn_rstds(0)
            pool.wait_ge(s_grstd, 1)
            nc.gpsimd.memset(stack[KROWS:KROWS + 1, :, :, 1, :].rearrange("o r h n -> o (r h) n"), 1.0).then_inc(s_kones, 1)
            pool.wait_ge(s_kones, 1)
            gn_rstds(1)
            nc.gpsimd.memset(v_ring[:], 1.0).then_inc(s_vones, 1)

            def rope(i, n0, u):
                b = 2 * (n0 + 2 * i) + u
                wait(pool, s_qk, b + 1)
                wait(pool, s_rope, b)
                swapped = qk_ring[:, u, :].rearrange("p (n t) -> p n t", t=2)[:, :, ::-1]
                nc.gpsimd.tensor_tensor(rs_tmp[:].rearrange("p (n t) -> p n t", t=2), swapped,
                                        cst[:, O_SIN:O_SIN + N_ROPE].rearrange("p (n t) -> p n t", t=2),
                                        ALU.mult).then_inc(s_rsin, 1)
                wait(pool, s_rsin, b + 1)
                wait(pool, s_rcos, b + 1)
                wait(pool, s_qkt, b - 1)
                nc.gpsimd.tensor_tensor(qr_ring[:, u, :].rearrange("p (k d h) -> p k d h", h=HEADS, d=HD),
                                        rc_ring[:, u, :].rearrange("p (k h d) -> p k d h", h=HEADS, d=HD),
                                        rs_tmp[:].rearrange("p (k h d) -> p k d h", h=HEADS, d=HD),
                                        ALU.add).then_inc(s_rope, 1)

            def third(i, n0, u):
                b = 2 * (n0 + 2 * i) + u
                wait(pool, s_p1, b + 1)
                nc.gpsimd.tensor_tensor(parts_v[:, ds(2 * b, 2), 2, :], rest_ring[:, u], parts_v[:, ds(2 * b, 2), 1, :],
                                        ALU.subtract).then_inc(s_p2, 1)

            def ln_rstds(i, n0):
                wait(pool, s_lnvar, n0 + 2 * i + 1)
                nc.gpsimd.tensor_tensor(ln_rstd[:, n0 % 2, :], ln_var[:, n0 % 2, :], mhalf[:, 0:4],
                                        ALU.pow).then_inc(s_lnrstd, 1)

            pool.wait_ge(s_ropet, 16)

            def step_a(i, n0):
                if n0 >= 1:
                    ln_rstds(i, n0 - 1)
                if n0 >= 2:
                    rope(i, n0 - 2, 0)
                if n0 >= 3:
                    third(i, n0 - 3, 1)
                if n0 >= 2:
                    rope(i, n0 - 2, 1)
                    third(i, n0 - 2, 0)
            run(pool, step_a, **A)

            def step_b(i, n0):
                for hp in range(3):
                    wait_apart(pool, s_exp, HEADS * (n0 + RING * i) + 2 * (hp + 1))
                    v = pt_ring[:, n0 % 2, 2 * hp:2 * hp + 2, 0:2 * P]
                    nc.gpsimd.affine_select(out=v, in_=v, compare_op=ALU.is_ge, fill=0.0, base=0,
                                            pattern=[[0, 2], [0, 2], [1, P]], channel_multiplier=-1).then_inc(s_sel, 1)
            ln_rstds(0, PAIRS - 1)
            rope(0, PAIRS - 2, 0)
            third(0, PAIRS - 3, 1)
            rope(0, PAIRS - 2, 1)
            rope(0, PAIRS - 1, 0)
            third(0, PAIRS - 2, 0)
            rope(0, PAIRS - 1, 1)
            third(0, PAIRS - 2, 1)
            step_b(0, 0)
            third(0, PAIRS - 1, 0)
            third(0, PAIRS - 1, 1)
            step_b(0, 1)
            run(pool, step_b, **BB)

            def second_rstd(k):
                cols = LN2_COLS[k]
                pool.wait_ge(s_l2var, k + 1)
                nc.gpsimd.tensor_tensor(ln2_rstd[:, cols], ln2_var[:, cols], mhalf[:, cols],
                                        ALU.pow).then_inc(s_l2rstd, 1)

            def second_norm(g):
                pool.wait_ge(s_l2rstd, g // 2 + 1)
                wait(pool, s_x2t, 2 * (g - 1))
                cols = slice(GB * NT * g, GB * NT * (g + 1))
                t_g = tok[:, GB * g:GB * (g + 1), :, :].rearrange("p b t c -> p (b t) c")
                nc.gpsimd.tensor_tensor(x2_ring[:, g % 2], t_g, ln2_mean[:, cols].unsqueeze(2).broadcast_to(
                    [P, GB * NT, C]), ALU.subtract).then_inc(s_x2m, 1)
                pool.wait_ge(s_x2m, g + 1)
                nc.gpsimd.tensor_tensor(x2_ring[:, g % 2], x2_ring[:, g % 2], ln2_rstd[:, cols].unsqueeze(
                    2).broadcast_to([P, GB * NT, C]), ALU.mult).then_inc(s_x2, 1)

            step_b(0, B - 2)
            second_rstd(0)
            step_b(0, B - 1)
            second_norm(0)
            for n in range(C_STEPS):
                if n + 1 < QGROUPS:
                    second_norm(n + 1)
                if n < 2:
                    second_rstd(n + 1)
                if 2 <= n:
                    pool.wait_ge(s_gm2, n - 1)
                    wait(pool, s_sc2, n - 2)
                    nc.gpsimd.partition_all_reduce(gmax2[0:C, 1:2], gmax2[0:C, 0:1], C,
                                                   bass.bass_isa.ReduceOp.max).then_inc(s_ar2, 1)
                if n < QGROUPS:
                    pool.wait_ge(s_gm1, n + 1)
                    wait(pool, s_sc1, n)
                    nc.gpsimd.partition_all_reduce(gmax1[:, 1:2], gmax1[:, 0:1], P,
                                                   bass.bass_isa.ReduceOp.max).then_inc(s_ar1, 1)

        @block.scalar
        def _(act):
            act.dma_start(wc_bc[:], weight_coord.rearrange("o p k -> o (p k)").broadcast_to([P, POINTS * 2])).then_inc(s_small, 16)
            act.dma_start(rad_bc[:], radius.rearrange("o p a b -> o (p a b)").broadcast_to([P, POINTS])).then_inc(s_small, 16)
            act.dma_start(cw_bc[:].rearrange("p c k -> p (c k)"),
                          conv_w.rearrange("o c k -> o (c k)").broadcast_to([P, C * POINTS])).then_inc(s_cw, 16)
            act.dma_start(x_all[:, 4:8, :], x_v[:, 4:8, :]).then_inc(s_xall[1], 16)
            act.dma_start(x_all[:, 12:16, :], x_v[:, 12:16, :]).then_inc(s_xall[3], 16)
            act.dma_start(w1_in[:], w1.rearrange("(c p) k -> p c k", p=P)).then_inc(s_weights, 16)
            act.dma_start(w2_in[:], w2).then_inc(s_weights, 16)
            act.dma_start(b1_s[:], b1.rearrange("(c p) -> p c", p=P), allow_slow_non_contiguous=True).then_inc(s_weights, 16)
            act.dma_start(b2_s[:], b2.rearrange("(c o) -> c o", o=1), allow_slow_non_contiguous=True).then_inc(s_weights, 16)
            for p in range(POINTS):
                act.wait_ge(s_cone, p + 1)
                m = toep[:, p].rearrange("p t y x -> p (t y x)")
                nc.scalar.activation(m, m, ACT.Relu).then_inc(s_toep, 1)
            act.wait_ge(s_wtr, 1)
            nc.scalar.copy(w1_b[:], bank[0:C, 5, 0:HID]).then_inc(s_wcopy, 1)
            act.wait_ge(s_wtr, 2)
            nc.scalar.copy(w2_b[:].rearrange("p k c -> p (k c)"), bank[:, 7, 0:HC * C]).then_inc(s_wcopy, 1)

            def qkv_out(i, n0, u):
                b = 2 * (n0 + 2 * i) + u
                wait(act, s_qkv, b + 1)
                wait(act, s_rope, b - 1)
                nc.scalar.copy(qk_ring[:, u, :].rearrange("p (t c) -> p t c", t=NT),
                               bank[:, 5:7, 0:2 * C]).then_inc(s_qk, 1)
                nc.scalar.copy(v_all[:, ds(b, 1), :, :].rearrange("p o t c -> p (o t) c"),
                               bank[:, 5:7, 2 * C:3 * C]).then_inc(s_vc, 1)

            def first_parts(i, n0, u):
                b = 2 * (n0 + 2 * i) + u
                wait(act, s_qkt, b + 1)
                nc.scalar.copy(parts_v[:, ds(2 * b, 2), 0, :],
                               bank[0:C, 7, :].rearrange("c (s n) -> c s n", s=2)).then_inc(s_p0, 1)

            def ln_out(i, n0):
                q = n0 + 2 * i
                wait(act, s_xlt, q + 1)
                wait(act, s_qkv, 2 * q - 2)
                nc.scalar.copy(lt_ring[:, n0 % 2, :], bank[0:C, 4, :]).then_inc(s_lt, 1)

            def step_a(i, n0):
                j = n0 + 2 * i
                if n0 >= 2:
                    qkv_out(i, n0 - 2, 1)
                    first_parts(i, n0 - 2, 0)
                if n0 >= 1:
                    ln_out(i, n0 - 1)
                act.wait_ge(s_cv, j + 1)
                nc.scalar.copy(tok[:, ds(2 * j, 2), :, :],
                               bank[:, 2 + n0 % 2, 0:NT * 2 * C].rearrange("p (t b c) -> p b t c", t=NT, b=2)
                               ).then_inc(s_tok, 1)
                if n0 >= 2:
                    first_parts(i, n0 - 2, 1)
                if n0 >= 1:
                    qkv_out(i, n0 - 1, 0)
            run(act, step_a, **A)

            def max_out(i, n0):
                b = n0 + RING * i
                wait(act, s_mt, b + 1)
                prev = (n0 - 2) % RING
                wait(act, s_mrow[prev], 16 * NT * ((n0 - 2) // RING + i + 1))
                nc.scalar.copy(nmax_t[:, n0 % 2, :], bank[0:NT * HEADS, 2, 3 * P:4 * P]).then_inc(s_mtc, 1)

            def step_b(i, n0):
                b = n0 + RING * i
                s = n0 % 2

                def exps(hp):
                    for h in (2 * hp, 2 * hp + 1):
                        act.wait_ge(s_sk, HEADS * b + h + 1)
                        wait(act, s_pv, b - 1)
                        nc.scalar.activation(pt_ring[:, s, h, :], bank[:, 3 + h % 2, 0:T + P], ACT.Exp,
                                             scale=float(HD) ** -0.5).then_inc(s_exp, 1)
                if n0 < B:
                    exps(0)
                if n0 + 1 < B:
                    max_out(i, n0 + 1)
                if n0 >= 2:
                    wait(act, s_ont, b - 1)
                    wait(act, s_proj, b - 2)
                    nc.scalar.copy(ot_ring[:, s, :], bank[0:C, 6, 0:T]).then_inc(s_ontc, 1)
                if n0 < B:
                    nc.scalar.copy(v_ring[:, s, :, :, 0:HD].rearrange("p t h d -> p (t h) d"),
                                   v_all[:, ds(b, 1), :, :].rearrange("p o t (h d) -> p (o t h) d", d=HD)
                                   ).then_inc(s_v, 1)
                if 1 <= n0 <= B:
                    wait(act, s_pv, b)
                    wait(act, s_otr, b - 2)
                    nc.scalar.copy(o_ring[:, 1 - s, :], bank[0:C, 7, :]).then_inc(s_o, 1)
                if n0 < B:
                    exps(1)
                    exps(2)
            qkv_out(0, PAIRS - 2, 1)
            ln_out(0, PAIRS - 1)
            first_parts(0, PAIRS - 2, 0)
            qkv_out(0, PAIRS - 1, 0)
            max_out(0, 0)
            first_parts(0, PAIRS - 2, 1)
            qkv_out(0, PAIRS - 1, 1)
            first_parts(0, PAIRS - 1, 0)
            act.wait_ge(s_wcen, 2)
            nc.scalar.activation(w1_b[:, 0:QGROUPS * W1_ROWS], w1_b[:, 0:QGROUPS * W1_ROWS], ACT.Sign)
            nc.scalar.activation(w2_b[:, :, 0:QGROUPS * W2_ROWS], w2_b[:, :, 0:QGROUPS * W2_ROWS],
                                 ACT.Sign).then_inc(s_wsign, 1)

            act.wait_ge(s_vones, 1)
            step_b(0, 0)
            first_parts(0, PAIRS - 1, 1)
            step_b(0, 1)
            run(act, step_b, **BB)

            def channel_major(g):
                for half in range(2):
                    act.wait_ge(s_x2t, 2 * g + half + 1)
                    wait(act, s_f1, 2 * HC * (g - 1))
                    nc.scalar.copy(x2t_ring[:, g % 2, half * HALF:(half + 1) * HALF],
                                   bank[0:C, 0, 0:HALF]).then_inc(s_x2c, 1)

            def hidden(g, r):
                act.wait_ge(s_f1, 2 * HC * g + r + 1)
                wait(act, s_h, 2 * (g - 1))
                nc.scalar.activation(y1_ring[:, g % 2, r * HALF:(r + 1) * HALF], bank[:, 1 + (2 * HC * g + r) % 3, 0:HALF],
                                     ACT.Identity, bias=b1_s[:, r % HC:r % HC + 1]).then_inc(s_y1, 1)

            def gelu(g, half):
                act.wait_ge(s_clip1, 2 * g + half + 1)
                wait(act, s_f2, 2 * (g - 1))
                pieces = HC if g == QGROUPS - 1 else 1
                size = HC * HALF // pieces
                for k in range(pieces):
                    cols = slice(half * HC * HALF + k * size, half * HC * HALF + (k + 1) * size)
                    nc.scalar.activation(h_ring[:, g % 2, cols], y1_ring[:, g % 2, cols], ACT.Gelu,
                                         scale=lim1[:, g % 2, 0:1]).then_inc(s_h, 1)

            def output(g):
                for half in range(2):
                    act.wait_ge(s_f2, 2 * g + half + 1)
                    wait(act, s_out, g - 1)
                    nc.scalar.activation(y2_ring[:, g % 2, half * HALF:(half + 1) * HALF],
                                         bank[0:C, 4 + half, 0:HALF], ACT.Identity, bias=b2_s[:, 0:1]).then_inc(s_y2, 1)

            def hidden_half(g, half):
                for r in range(half * HC, (half + 1) * HC):
                    hidden(g, r)

            for n in range(B - 2, B + 1):
                step_b(0, n)
            nc.scalar.activation(warm[:], ones[0:1, 0:1], ACT.Gelu)
            channel_major(0)
            hidden_half(0, 0)
            step_b(0, B + 1)
            hidden_half(0, 1)
            channel_major(1)
            for n in range(1, C_STEPS):
                for half in range(2):
                    if n < QGROUPS:
                        hidden_half(n, half)
                    if n <= QGROUPS:
                        gelu(n - 1, half)
                if n + 1 < QGROUPS:
                    channel_major(n + 1)
                if n <= QGROUPS:
                    output(n - 1)
                if n == QGROUPS:
                    act.wait_ge(s_t2last, 1)
                    nc.scalar.copy(last_out, bank[0:C, 0, 0:T]).then_inc(s_last, 1)

        @block.vector
        def _(dve):
            dve.wait_ge(s_small, 16 * 3)
            nc.vector.reciprocal(nrinv[:, 0, :], rad_bc[:]).then_inc(s_rinv, 1)
            at = wc_bc[:].rearrange("p (q k) -> p q k", k=2)
            for k, cols in enumerate((slice(0, SIDE), slice(SIDE, N_GRID))):
                n = cols.stop - cols.start
                last = nc.vector.tensor_tensor(
                    grid_t[:, :, cols], cst[:, cols].unsqueeze(1).broadcast_to([P, POINTS, n]),
                    at[:, :, k].unsqueeze(2).broadcast_to([P, POINTS, n]), ALU.subtract)
            last.then_inc(s_grid, 1)
            dve.wait_ge(s_rinv, 1)
            nc.vector.tensor_scalar(nrinv[:, 1, :], nrinv[:, 0, :], -1.0, None, ALU.mult).then_inc(s_rinv, 1)
            dve.wait_ge(s_grid, 1)
            nc.vector.tensor_scalar(grid_n[:], grid_t[:], -1.0, None, ALU.mult).then_inc(s_grid, 1)

            def gn_channels(k):
                cols = GN_COLS[k]
                for b in range(cols.start, cols.stop):
                    if b % 4 == 0:
                        dve.wait_ge(s_xall[b // 4], 16)
                    nc.vector.bn_stats(gn_st[:, b, :], x_all[:, b, :]).then_inc(s_gst, 1)
                for b in range(cols.start, cols.stop):
                    dve.wait_ge(s_gst, b + 1)
                    last = nc.vector.bn_aggr(gn_mv[:, b, :], gn_st[:, b, :])
                last.then_inc(s_gmv, 1)

            def gn_means(k):
                cols = GN_COLS[k]
                dve.wait_ge(s_gps, 2 * k + 1)
                nc.vector.tensor_scalar(gn_mean[:, cols], bank[0:C, 4, cols], 1.0 / GN_GROUP, None,
                                        ALU.mult).then_inc(s_gnsteps, 1)
                dve.wait_ge(s_gnsteps, 3 * k + 1)
                nc.vector.tensor_tensor(gn_tmp[:, 0, cols], gn_mv[:, cols, 0], gn_mean[:, cols],
                                        ALU.subtract).then_inc(s_gnsteps, 1)
                dve.wait_ge(s_gnsteps, 3 * k + 2)
                nc.vector.tensor_tensor(gn_tmp[:, 1, cols], gn_tmp[:, 0, cols], gn_tmp[:, 0, cols],
                                        ALU.mult).then_inc(s_gnsteps, 1)
                dve.wait_ge(s_gnsteps, 3 * k + 3)
                nc.vector.tensor_tensor(gn_tmp[:, 0, cols], gn_tmp[:, 1, cols], gn_mv[:, cols, 1],
                                        ALU.add).then_inc(s_gsq, 1)

            def gn_vars(k):
                cols = GN_COLS[k]
                dve.wait_ge(s_gps, 2 * k + 2)
                nc.vector.tensor_scalar(gn_tmp[:, 2, cols], bank[0:C, 4, B + cols.start:B + cols.stop], 1.0 / GN_GROUP,
                                        GN_EPS, ALU.mult, ALU.add).then_inc(s_gvar, 1)

            gn_channels(0)
            dve.wait_ge(s_grid, 2)
            nc.vector.tensor_tensor(grid_t[:], grid_t[:], grid_n[:], ALU.max).then_inc(s_grid, 1)
            gn_means(0)
            dve.wait_ge(s_rinv, 2)
            dve.wait_ge(s_grid, 3)
            nc.vector.tensor_tensor(grid_t[:], grid_t[:], nrinv[:, 1, :].unsqueeze(2).broadcast_to(
                [P, POINTS, N_GRID]), ALU.mult).then_inc(s_grid, 1)
            gn_vars(0)
            dve.wait_ge(s_grid, 4)
            nc.vector.tensor_scalar(grid_t[:, :, SIDE:N_GRID], grid_t[:, :, SIDE:N_GRID], 1.0, None,
                                    ALU.add).then_inc(s_grid, 1)
            dve.wait_ge(s_grid, 5)

            def cone(p):
                gx = grid_t[:, p, 0:SIDE].unsqueeze(1).broadcast_to([P, NT * SIDE, SIDE])
                gy = grid_t[:, p, SIDE:N_GRID].unsqueeze(2).broadcast_to([P, NT * SIDE, SIDE])
                nc.vector.tensor_tensor(toep[:, p].rearrange("p t y x -> p (t y) x"), gx, gy,
                                        ALU.add).then_inc(s_cone, 1)

            def normalise(i, n0):
                j = n0 + 2 * i
                s = n0 % 2
                wait(dve, s_xnt, j - 1)
                for u in range(2):
                    b = 2 * j + u
                    last = nc.vector.tensor_scalar(xn_ring[:, s, u, :],
                                                   x_all[:, ds(b, 1), :].rearrange("c o n -> c (o n)"),
                                                   gn_mean[:, ds(b, 1)], gn_rstd[:, ds(b, 1)], ALU.subtract, ALU.mult)
                last.then_inc(s_xn, 1)

            def weigh(i, n0):
                j, s = n0 + 2 * i, n0 % 2
                dve.wait_ge(s_xnt, j + 1)
                wait(dve, s_cv, j - 1)
                src = bank[:, s, 0:NT * 2 * C].rearrange("p (k c) -> p k c", c=C)
                for p in range(POINTS):
                    w = cw_bc[:, :, p].unsqueeze(1).broadcast_to([P, NT * 2, C])
                    last = nc.vector.tensor_tensor(xs_ring[:, s, p].rearrange("p t b c -> p (t b) c"), src, w, ALU.mult)
                last.then_inc(s_xs, 1)

            cone(0)
            cone(1)
            dve.wait_ge(s_grstd, 1)
            normalise(0, 0)
            cone(2)
            cone(3)
            dve.wait_ge(s_cw, 16)
            weigh(0, 0)

            def cosines(i, n0, u):
                b = 2 * (n0 + 2 * i) + u
                dve.wait_ge(s_qk, b + 1)
                wait(dve, s_rope, b - 1)
                nc.vector.tensor_tensor(rc_ring[:, u, :], qk_ring[:, u, :], cst[:, O_COS:O_COS + N_ROPE],
                                        ALU.mult).then_inc(s_rcos, 1)

            def second_parts(i, n0, u):
                b = 2 * (n0 + 2 * i) + u
                dve.wait_ge(s_p0, b + 1)
                wait(dve, s_p2, b - 1)
                nc.vector.tensor_tensor(rest_ring[:, u], bank[0:C, 7, :].rearrange("c (s n) -> c s n", s=2),
                                        parts_v[:, ds(2 * b, 2), 0, :], ALU.subtract).then_inc(s_rest, 1)
                dve.wait_ge(s_rest, b + 1)
                nc.vector.tensor_copy(parts_v[:, ds(2 * b, 2), 1, :], rest_ring[:, u]).then_inc(s_p1, 1)

            def ln_stats(i, n0):
                q, s = n0 + 2 * i, n0 % 2
                wait_apart(dve, s_tok, q + 1)
                for t in range(4):
                    last = nc.vector.bn_stats(ln_st[:, s, t, :], tok[:, ds(2 * q + t // 2, 1), t % 2, :]
                                              .rearrange("p o c -> p (o c)"))
                last.then_inc(s_lnst, 1)
                wait_apart(dve, s_lnst, q + 1)
                for t in range(4):
                    last = nc.vector.bn_aggr(ln_mv[:, s, t, :], ln_st[:, s, t, :])
                last.then_inc(s_lnmv, 1)
                dve.wait_ge(s_lnmv, q + 1)
                nc.vector.tensor_scalar(ln_var[:, s, :], ln_mv[:, s, :, 1], LN_EPS, None, ALU.add).then_inc(s_lnvar, 1)

            def ln_apply(i, n0):
                q, s = n0 + 2 * i, n0 % 2
                dve.wait_ge(s_lnrstd, q + 1)
                wait(dve, s_xlt, q - 1)
                for t in range(4):
                    last = nc.vector.tensor_scalar(
                        xl_ring[:, s, t, :], tok[:, ds(2 * q + t // 2, 1), t % 2, :].rearrange("p o c -> p (o c)"),
                        ln_mv[:, s, t, 0:1], ln_rstd[:, s, t:t + 1], ALU.subtract, ALU.mult)
                last.then_inc(s_xl, 1)

            def step_a(i, n0):
                if n0 + 1 < PAIRS:
                    normalise(i, n0 + 1)
                if n0 >= 1:
                    ln_stats(i, n0 - 1)
                if n0 >= 2:
                    cosines(i, n0 - 2, 0)
                if n0 >= 3:
                    second_parts(i, n0 - 3, 1)
                if n0 >= 1:
                    ln_apply(i, n0 - 1)
                if n0 >= 2:
                    cosines(i, n0 - 2, 1)
                if n0 + 1 < PAIRS:
                    weigh(i, n0 + 1)
                if n0 >= 2:
                    second_parts(i, n0 - 2, 0)

            normalise(0, 1)
            gn_channels(1)
            weigh(0, 1)
            gn_means(1)
            gn_vars(1)
            dve.wait_ge(s_setup, 1)
            nc.vector.tensor_copy(mask16[:], mask[:])
            nc.vector.tensor_copy(ident16[:], ident[:]).then_inc(s_id16, 1)
            dve.wait_ge(s_grstd, 2)
            dve.wait_ge(s_ropet, 16)
            step_a(0, 1)
            dve.wait_ge(s_wcopy, 1)
            nc.vector.tensor_reduce(w_sum[0:C, 0, :], w1_b[:, 0:QGROUPS * W1_ROWS].rearrange(
                "c (g r) -> c g r", g=QGROUPS), op=ALU.add, axis=AX.X).then_inc(s_wsum, 1)
            dve.wait_ge(s_wcopy, 2)
            nc.vector.tensor_reduce(w_sum[:, 1, :], w2_b[:, :, 0:QGROUPS * W2_ROWS].rearrange(
                "p k (g r) -> p g k r", g=QGROUPS), op=ALU.add, axis=AX.XY).then_inc(s_wsum, 1)
            run(dve, step_a, start=2, **A)

            def maxima(i, n0, h):
                b = n0 + RING * i
                dve.wait_ge(s_sq, HEADS * b + h + 1)
                if h == 0:
                    wait(dve, s_mt, b - 1)
                for t in range(NT):
                    first = t * P
                    last = nc.vector.tensor_reduce(nmax[:, n0 % 2, HEADS * t + h:HEADS * t + h + 1],
                                                   bank[:, h % 3, first:first + (t + 1) * P],
                                                   op=ALU.max, axis=AX.X, negate=True)
                last.then_inc(s_max, 1)

            def second_stats(k):
                cols = LN2_COLS[k]
                even, odd = ln2_st[:, cols, 1], ln2_st[:, cols, 4]
                dve.wait_ge(s_l2st, cols.stop // NT)
                nc.vector.tensor_tensor(ln2_mean[:, cols], even, odd, ALU.add)
                nc.vector.tensor_tensor(ln2_tmp[:, 0, cols], even, odd, ALU.subtract)
                nc.vector.tensor_tensor(ln2_tmp[:, 1, cols], ln2_st[:, cols, 2], ln2_st[:, cols, 5],
                                        ALU.add).then_inc(s_l2mv, 1)
                dve.wait_ge(s_l2mv, 2 * k + 1)
                nc.vector.tensor_scalar(ln2_mean[:, cols], ln2_mean[:, cols], 0.5, None, ALU.mult)
                nc.vector.tensor_scalar(ln2_tmp[:, 1, cols], ln2_tmp[:, 1, cols], 1.0 / C, LN_EPS, ALU.mult, ALU.add)
                nc.vector.scalar_tensor_tensor(ln2_tmp[:, 2, cols], ln2_tmp[:, 0, cols], 0.25, ln2_tmp[:, 0, cols],
                                               ALU.mult, ALU.mult).then_inc(s_l2mv, 1)
                dve.wait_ge(s_l2mv, 2 * k + 2)
                nc.vector.tensor_tensor(ln2_var[:, cols], ln2_tmp[:, 1, cols], ln2_tmp[:, 2, cols],
                                        ALU.add).then_inc(s_l2var, 1)

            def step_b(i, n0):
                b = n0 + RING * i
                if n0 + 2 < B:
                    for h in range(4):
                        maxima(i, n0 + 2, h)
                if n0 >= 2:
                    dve.wait_ge(s_proj, b - 1)
                    t_b = tok[:, ds(b - 2, 1), :, :].rearrange("p o t c -> p (o t) c")
                    nc.vector.tensor_tensor(t_b, bank[:, 6, T:T + NT * C].rearrange("p (t c) -> p t c", t=NT), t_b,
                                            ALU.add).then_inc(s_res, 1)
                if 1 <= n0 <= B:
                    dve.wait_ge(s_otr, b)
                    o = bank[:, 5, 0:4 * C].rearrange("p (n k) -> p n k", k=2 * HD)
                    nc.vector.reciprocal(rsum[:], o[:, :, HD]).then_inc(s_rsum, 1)
                if n0 + 2 < B:
                    for h in range(4, HEADS):
                        maxima(i, n0 + 2, h)
                if 1 <= n0 <= B:
                    dve.wait_ge(s_rsum, b)
                    wait(dve, s_ont, b - 1)
                    nc.vector.tensor_tensor(o_norm[:].rearrange("p t (h d) -> p (t h) d", d=HD), o[:, :, 0:HD],
                                            rsum[:].unsqueeze(2).broadcast_to([P, NT * HEADS, HD]),
                                            ALU.mult).then_inc(s_on, 1)
                if n0 >= 2:
                    wait_apart(dve, s_res, b - 1)
                    for t in range(NT):
                        last = nc.vector.bn_stats(
                            ln2_st[:, ds(2 * (b - 2) + t, 1), :].rearrange("p o k -> p (o k)"),
                            tok[:, ds(b - 2, 1), t, :].rearrange("p o c -> p (o c)"))
                    last.then_inc(s_l2st, 1)

            ln_stats(0, PAIRS - 1)
            cosines(0, PAIRS - 2, 0)
            second_parts(0, PAIRS - 3, 1)
            for h in range(2):
                maxima(0, 0, h)
            ln_apply(0, PAIRS - 1)
            cosines(0, PAIRS - 2, 1)
            for h in range(2, HEADS):
                maxima(0, 0, h)
            second_parts(0, PAIRS - 2, 0)
            for h in range(3):
                maxima(0, 1, h)
            cosines(0, PAIRS - 1, 0)
            second_parts(0, PAIRS - 2, 1)
            for h in range(3, HEADS):
                maxima(0, 1, h)
            dve.wait_ge(s_wps, 1)
            nc.vector.tensor_scalar(w_mean[0:C, 0, :], bank[0:C, 3, 0:QGROUPS], 1.0 / (W1_ROWS * C), None, ALU.mult)
            nc.vector.tensor_scalar(w_mean[:, 1, :], bank[:, 3, QGROUPS:2 * QGROUPS], 1.0 / (W2_ROWS * HID), None,
                                    ALU.mult).then_inc(s_wmean, 1)
            dve.wait_ge(s_wmean, 1)
            v1 = w1_b[:, 0:QGROUPS * W1_ROWS].rearrange("c (g r) -> c g r", g=QGROUPS)
            nc.vector.tensor_tensor(v1, v1, w_mean[0:C, 0, :].unsqueeze(2).broadcast_to([C, QGROUPS, W1_ROWS]),
                                    ALU.subtract).then_inc(s_wcen, 1)
            for k in range(HC):
                v2 = w2_b[:, k, 0:QGROUPS * W2_ROWS].rearrange("p (g r) -> p g r", g=QGROUPS)
                last = nc.vector.tensor_tensor(
                    v2, v2, w_mean[:, 1, :].unsqueeze(2).broadcast_to([P, QGROUPS, W2_ROWS]), ALU.subtract)
            last.then_inc(s_wcen, 1)
            nc.vector.memset(w1_b[:, QGROUPS * W1_ROWS:HID], 0.0)
            nc.vector.memset(w2_b[:, :, QGROUPS * W2_ROWS:C], 0.0).then_inc(s_wready, 1)

            cosines(0, PAIRS - 1, 1)
            second_parts(0, PAIRS - 1, 0)
            step_b(0, 0)
            second_parts(0, PAIRS - 1, 1)
            step_b(0, 1)
            run(dve, step_b, **BB)

            def bounds(gmax, lim, signal, count):
                nc.vector.tensor_scalar(gmax[:, 2:3], gmax[:, 1:2], Q_EPS, None, ALU.add).then_inc(signal[0], 1)
                dve.wait_ge(signal[0], 3 * count - 2)
                nc.vector.reciprocal(gmax[:, 3:4], gmax[:, 2:3]).then_inc(signal[0], 1)
                top = (QB - Q_EPS) / QB
                nc.vector.tensor_scalar(lim[:, 1:2], gmax[:, 2:3], top, None, ALU.mult)
                nc.vector.tensor_scalar(lim[:, 2:3], gmax[:, 2:3], -top, None, ALU.mult).then_inc(signal[0], 1)
                dve.wait_ge(signal[0], 3 * count)
                nc.vector.tensor_scalar(lim[:, 0:1], gmax[:, 3:4], QB, None, ALU.mult).then_inc(signal[1], 1)

            def largest_hidden(g, r):
                dve.wait_ge(s_y1, 2 * HC * g + r + 1)
                return nc.vector.tensor_reduce(amax1[:, r:r + 1], y1_ring[:, g % 2, r * HALF:(r + 1) * HALF],
                                               op=ALU.max, axis=AX.X, apply_absolute_value=True)

            def hidden_bounds(g):
                dve.wait_ge(s_ar1, g + 1)
                wait(dve, s_h, 2 * (g - 1))
                bounds(gmax1[:, :], lim1[:, g % 2, :], (s_bd1, s_sc1), g + 1)

            second_stats(0)
            for n in range(B - 2, B + 1):
                step_b(0, n)
            second_stats(1)
            for r in range(HC):
                largest_hidden(0, r)
            step_b(0, B + 1)
            for r in range(HC, 2 * HC):
                last = largest_hidden(0, r)
            last.then_inc(s_am1, 1)
            dve.wait_ge(s_am1, 1)
            nc.vector.tensor_reduce(gmax1[:, 0:1], amax1[:], op=ALU.max, axis=AX.X).then_inc(s_gm1, 1)
            hidden_bounds(0)
            second_stats(2)
            def output_max(g):
                y = y2_ring[:, g % 2, :]
                for half in range(2):
                    dve.wait_ge(s_y2, 2 * g + half + 1)
                    last = nc.vector.tensor_reduce(amax2[0:C, half:half + 1], y[:, half * HALF:(half + 1) * HALF],
                                                   op=ALU.max, axis=AX.X, apply_absolute_value=True)
                last.then_inc(s_am2, 1)
                dve.wait_ge(s_am2, g + 1)
                nc.vector.tensor_reduce(gmax2[0:C, 0:1], amax2[0:C, :], op=ALU.max, axis=AX.X).then_inc(s_gm2, 1)

            def scaled_output(g):
                y = y2_ring[:, g % 2, :]
                dve.wait_ge(s_sc2, g + 1)
                nc.vector.tensor_scalar(y, y, lim2[0:C, 1:2], lim2[0:C, 2:3], ALU.min, ALU.max).then_inc(s_clip2, 1)
                dve.wait_ge(s_clip2, g + 1)
                dve.wait_ge(s_t2t, g + 1)
                wait(dve, s_store[g % 2], 16 * (g // 2))
                for half in range(2):
                    cols = slice(half * HALF, (half + 1) * HALF)
                    last = nc.vector.scalar_tensor_tensor(out_ring[:, g % 2, cols], y[:, cols], lim2[0:C, 0:1],
                                                          bank[0:C, 6 + half, 0:HALF], ALU.mult, ALU.add)
                last.then_inc(s_out, 1)

            for n in range(1, C_STEPS):
                if n <= QGROUPS:
                    dve.wait_ge(s_sc1, n)
                    for half in range(2):
                        y = y1_ring[:, (n - 1) % 2, half * HC * HALF:(half + 1) * HC * HALF]
                        lim = lim1[:, (n - 1) % 2, :]
                        nc.vector.tensor_scalar(y, y, lim[:, 1:2], lim[:, 2:3], ALU.min, ALU.max).then_inc(s_clip1, 1)
                if 3 <= n <= QGROUPS:
                    scaled_output(n - 3)
                if n < QGROUPS:
                    for r in range(HC):
                        largest_hidden(n, r)
                if n >= 2:
                    output_max(n - 2)
                if n < QGROUPS:
                    for r in range(HC, 2 * HC):
                        last = largest_hidden(n, r)
                    last.then_inc(s_am1, 1)
                    dve.wait_ge(s_am1, n + 1)
                    nc.vector.tensor_reduce(gmax1[:, 0:1], amax1[:], op=ALU.max, axis=AX.X).then_inc(s_gm1, 1)
                if n >= 2:
                    dve.wait_ge(s_ar2, n - 1)
                    bounds(gmax2[0:C, :], lim2[0:C, :], (s_bd2, s_sc2), n - 1)
                if n < QGROUPS:
                    hidden_bounds(n)
                else:
                    scaled_output(n - 2)

        @block.tensor
        def _(pe):
            same = cst[0:C, O_SAME:O_SAME + C]
            pe.wait_ge(s_same, 16)

            def gn_mean_sums(k):
                cols = GN_COLS[k]
                pe.wait_ge(s_gmv, k + 1)
                nc.tensor.matmul(bank[0:C, 4, cols], same, gn_mv[:, cols, 0], start=True, stop=True).then_inc(s_gps, 1)

            def gn_var_sums(k):
                cols = GN_COLS[k]
                pe.wait_ge(s_gsq, k + 1)
                nc.tensor.matmul(bank[0:C, 4, B + cols.start:B + cols.stop], same, gn_tmp[:, 0, cols],
                                 start=True, stop=True).then_inc(s_gps, 1)
            gn_mean_sums(0)
            gn_var_sums(0)
            pe.wait_ge(s_ident, 1)

            def transpose_pair(i, n0):
                j, s = n0 + 2 * i, n0 % 2
                pe.wait_ge(s_xn, j + 1)
                wait(pe, s_xs, j - 1)
                for t in range(NT):
                    for u in range(2):
                        k = 2 * t + u
                        last = nc.tensor.transpose(bank[:, s, k * C:(k + 1) * C], xn_ring[:, s, u, t * P:(t + 1) * P],
                                                   ident[0:C, 0:C])
                last.then_inc(s_xnt, 1)

            def convolve(i, n0, t, k):
                s = n0 % 2
                dst = bank[:, 2 + s, t * 2 * C:(t + 1) * 2 * C]
                for p in range(POINTS):
                    w = toep[:, p, k].rearrange("p y x -> p (y x)")[:, t * P:(t + 1) * P]
                    nc.tensor.matmul(dst, w, xs_ring[:, s, p, k].rearrange("p b c -> p (b c)"),
                                     start=(k == 0 and p == 0), stop=False)
                if k == NT - 1:
                    for u in range(2):
                        last = nc.tensor.matmul(dst[:, u * C:(u + 1) * C], x_ring[:, s, u, t * P:(t + 1) * P],
                                                ident[0:C, 0:C], start=False, stop=(u == 1))
                    return last

            def transpose_qk(i, n0, u):
                b = 2 * (n0 + 2 * i) + u
                pe.wait_ge(s_rope, b + 1)
                wait(pe, s_rest, b)
                for side in range(2):
                    for t in range(NT):
                        last = nc.tensor.transpose(bank[0:C, 7, side * T + t * P:side * T + (t + 1) * P],
                                                   qr_ring[:, u, (2 * t + side) * C:(2 * t + side + 1) * C], ident[:])
                last.then_inc(s_qkt, 1)

            def project_qkv(i, n0, u):
                b = 2 * (n0 + 2 * i) + u
                if u == 0:
                    pe.wait_ge(s_lt, n0 + 2 * i + 1)
                wait(pe, s_qk, b)
                wait(pe, s_vc, b)
                for t in range(NT):
                    last = nc.tensor.matmul(bank[:, 5 + t, 0:3 * C],
                                            lt_ring[:, n0 % 2, (2 * u + t) * P:(2 * u + t + 1) * P], wa[:],
                                            start=True, stop=True)
                last.then_inc(s_qkv, 1)

            def transpose_ln(i, n0):
                pe.wait_ge(s_xl, n0 + 2 * i + 1)
                wait(pe, s_lt, n0 + 2 * i)
                for t in range(4):
                    last = nc.tensor.transpose(bank[0:C, 4, t * P:(t + 1) * P], xl_ring[:, n0 % 2, t, :], ident[:])
                last.then_inc(s_xlt, 1)

            transpose_pair(0, 0)
            pe.wait_ge(s_weights, 16 * 6)
            for k in range(HC):
                last = nc.tensor.transpose(bank[0:C, 5, k * P:(k + 1) * P], w1_in[:, k, :], ident[:])
            last.then_inc(s_wtr, 1)
            for k in range(HC):
                last = nc.tensor.transpose(bank[:, 7, k * C:(k + 1) * C], w2_in[:, k * P:(k + 1) * P], ident[0:C, 0:C])
            last.then_inc(s_wtr, 1)
            pe.wait_ge(s_toep, POINTS)
            pe.wait_ge(s_wcopy, 2)

            def step_a(i, n0):
                j = n0 + 2 * i
                pe.wait_ge(s_xr[n0 % 2], 16 * (n0 // 2 + i + 1))
                pe.wait_ge(s_xs, j + 1)
                wait(pe, s_tok, j - 1)
                convolve(i, n0, 0, 0)
                if n0 + 1 < PAIRS:
                    transpose_pair(i, n0 + 1)
                if n0 >= 2:
                    project_qkv(i, n0 - 2, 1)
                convolve(i, n0, 0, 1)
                convolve(i, n0, 1, 0)
                if n0 >= 2:
                    transpose_qk(i, n0 - 2, 0)
                if n0 >= 1:
                    transpose_ln(i, n0 - 1)
                convolve(i, n0, 1, 1).then_inc(s_cv, 1)
                if n0 >= 2:
                    transpose_qk(i, n0 - 2, 1)
                if n0 >= 1:
                    project_qkv(i, n0 - 1, 0)
            pe.wait_ge(s_xr[0], 16)
            pe.wait_ge(s_xs, 1)
            convolve(0, 0, 0, 0)
            transpose_pair(0, 1)
            convolve(0, 0, 0, 1)
            gn_mean_sums(1)
            convolve(0, 0, 1, 0)
            gn_var_sums(1)
            convolve(0, 0, 1, 1).then_inc(s_cv, 1)
            run(pe, step_a, start=1, **A)

            def scores_q(i, n0, h):
                b, slot = n0 + RING * i, n0 % RING
                if h == 0:
                    pe.wait_ge(s_stack[slot], 16 * len(SLOTS) * (n0 // RING + i + 1))
                wait(pe, s_max, HEADS * b + h - 2)
                if h == 2:
                    wait(pe, s_mtc, b)
                for t in range(NT):
                    first, size = t * P, (t + 1) * P
                    nc.tensor.matmul(bank[:, h % 3, first:first + size],
                                     stack[0:KROWS, slot, h, 0, t * P:(t + 1) * P],
                                     stack[0:KROWS, slot, h, 1, 0:size], start=True, stop=False)
                    last = nc.tensor.matmul(bank[:, h % 3, first + t * P:first + size], ident16[:], mask16[:],
                                            start=False, stop=True)
                last.then_inc(s_sq, 1)

            def scores_k(i, n0, hp):
                b, slot = n0 + RING * i, n0 % RING
                if hp == 0:
                    pe.wait_ge(s_mrow[slot], 16 * NT * (n0 // RING + i + 1))
                for e in range(2):
                    h = 2 * hp + e
                    wait(pe, s_exp, HEADS * b + h - 1)
                    nc.tensor.matmul(bank[:, 3 + e, P:P + T], stack[0:KROWS + 1, slot, h, 1, 0:P],
                                     stack[0:KROWS + 1, slot, h, 0, :], start=True, stop=True)
                    nc.tensor.matmul(bank[:, 3 + e, 0:P], stack[0:KROWS + 1, slot, h, 1, P:T],
                                     stack[0:KROWS + 1, slot, h, 0, P:T], start=True, stop=True).then_inc(s_sk, 1)

            def transpose_max(i, n0):
                b = n0 + RING * i
                pe.wait_ge(s_max, HEADS * (b + 1))
                wait(pe, s_mtc, b)
                nc.tensor.transpose(bank[0:NT * HEADS, 2, 3 * P:4 * P], nmax[:, n0 % 2, :], ident[:]).then_inc(s_mt, 1)

            def weighted_values(i, n0):
                b, s = n0 + RING * i, n0 % 2
                pe.wait_ge(s_sel, 3 * (b + 1))
                pe.wait_ge(s_v, b + 1)
                wait(pe, s_o, b)
                for g in range(2):
                    for t in range(NT):
                        for e in range(3):
                            h = 3 * g + e
                            rows = slice(2 * HD * e, 2 * HD * (e + 1))
                            w = v_ring[:, s, t, h, :]
                            if t == 0:
                                nc.tensor.matmul(bank[rows, 7, g * T:(g + 1) * T], w, pt_ring[:, s, h, P:P + T],
                                                 start=True, stop=False)
                            else:
                                last = nc.tensor.matmul(bank[rows, 7, g * T + P:(g + 1) * T], w,
                                                        pt_ring[:, s, h, 0:P], start=False, stop=True)
                last.then_inc(s_pv, 1)

            def transpose_o(i, n0):
                b, s = n0 + RING * i, n0 % 2
                pe.wait_ge(s_o, b + 1)
                wait(pe, s_on, b)
                for t in range(NT):
                    for g in range(2):
                        k = 2 * t + g
                        last = nc.tensor.transpose(bank[:, 5, k * C:(k + 1) * C],
                                                   o_ring[:, s, g * T + t * P:g * T + (t + 1) * P], ident[0:C, 0:C])
                last.then_inc(s_otr, 1)

            def transpose_norm(i, n0):
                b = n0 + RING * i
                pe.wait_ge(s_on, b + 1)
                wait(pe, s_res, b)
                for t in range(NT):
                    last = nc.tensor.transpose(bank[0:C, 6, t * P:(t + 1) * P], o_norm[:, t, :], ident[:])
                last.then_inc(s_ont, 1)

            def project_out(i, n0):
                b, s = n0 + RING * i, n0 % 2
                pe.wait_ge(s_ontc, b + 1)
                for t in range(NT):
                    last = nc.tensor.matmul(bank[:, 6, T + t * C:T + (t + 1) * C], ot_ring[:, s, t * P:(t + 1) * P],
                                            wp[:], start=True, stop=True)
                last.then_inc(s_proj, 1)

            def step_b(i, n0):
                for hp in range(3):
                    if n0 < B:
                        scores_k(i, n0, hp)
                    if n0 + 2 < B:
                        for h in (2 * hp, 2 * hp + 1):
                            scores_q(i, n0 + 2, h)
                    if n0 >= 2 and hp == 1:
                        project_out(i, n0 - 2)
                    if n0 + 1 < B and hp == 0:
                        transpose_max(i, n0 + 1)
                    if n0 >= 2 and hp == 0:
                        transpose_norm(i, n0 - 2)
                    if 1 <= n0 <= B and hp == 0:
                        weighted_values(i, n0 - 1)
                    if 1 <= n0 <= B and hp == 1:
                        transpose_o(i, n0 - 1)

            project_qkv(0, PAIRS - 2, 1)
            pe.wait_ge(s_id16, 1)
            pe.wait_ge(s_kones, 1)
            pe.wait_ge(s_xs, PAIRS)
            pe.wait_ge(s_tok, PAIRS)
            for h in range(3):
                scores_q(0, 0, h)
            transpose_ln(0, PAIRS - 1)
            for h in range(3, HEADS):
                scores_q(0, 0, h)
            transpose_qk(0, PAIRS - 2, 0)
            project_qkv(0, PAIRS - 1, 0)
            for h in range(2):
                scores_q(0, 1, h)
            transpose_max(0, 0)
            scores_q(0, 1, 2)
            transpose_qk(0, PAIRS - 2, 1)
            project_qkv(0, PAIRS - 1, 1)
            for h in range(3, HEADS):
                scores_q(0, 1, h)
            pe.wait_ge(s_setup, 1)
            pe.wait_ge(s_wsum, 2)
            nc.tensor.matmul(bank[0:C, 3, 0:QGROUPS], ones[0:C, 0:C], w_sum[0:C, 0, :], start=True, stop=True)
            nc.tensor.matmul(bank[:, 3, QGROUPS:2 * QGROUPS], ones[:], w_sum[:, 1, :], start=True,
                             stop=True).then_inc(s_wps, 1)
            transpose_qk(0, PAIRS - 1, 0)
            pe.wait_ge(s_wmean, 1)
            pe.wait_ge(s_lt, PAIRS)
            step_b(0, 0)
            transpose_qk(0, PAIRS - 1, 1)
            pe.wait_ge(s_vc, B)
            pe.wait_ge(s_rest, B)
            step_b(0, 1)
            run(pe, step_b, **BB)

            def transpose_x2(g, half):
                pe.wait_ge(s_x2, g + 1)
                wait(pe, s_x2c, 2 * g + half)
                for t in range(3):
                    last = nc.tensor.transpose(bank[0:C, 0, t * P:(t + 1) * P], x2_ring[:, g % 2, 3 * half + t, :],
                                               ident[:])
                last.then_inc(s_x2t, 1)

            def first_product(g, half):
                pe.wait_ge(s_x2c, 2 * g + half + 1)
                for k in range(HC):
                    n = 2 * HC * g + half * HC + k
                    wait(pe, s_y1, n - 2)
                    nc.tensor.matmul(bank[:, 1 + n % 3, 0:HALF], w1_b[:, k * P:(k + 1) * P],
                                     x2t_ring[:, g % 2, half * HALF:(half + 1) * HALF],
                                     start=True, stop=True).then_inc(s_f1, 1)

            def second_product(g, half):
                wait(pe, s_y2, 2 * (g - 1) + half + 1)
                if g < QGROUPS - 1:
                    pe.wait_ge(s_h, 2 * g + half + 1)
                for k in range(HC):
                    r = half * HC + k
                    if g == QGROUPS - 1:
                        pe.wait_ge(s_h, 2 * g + r + 1)
                    last = nc.tensor.matmul(bank[0:C, 4 + half, 0:HALF], w2_b[:, k, :],
                                            h_ring[:, g % 2, r * HALF:(r + 1) * HALF],
                                            start=(k == 0), stop=(k == HC - 1))
                last.then_inc(s_f2, 1)

            def residual(g):
                wait(pe, s_out, g)
                for half in range(2):
                    for t in range(3):
                        k = 3 * half + t
                        last = nc.tensor.transpose(bank[0:C, 6 + half, t * P:(t + 1) * P],
                                                   tok[:, GB * g + k // NT, k % NT, :], ident[:])
                last.then_inc(s_t2t, 1)

            for n in range(B - 2, B + 1):
                step_b(0, n)
            pe.wait_ge(s_max, HEADS * B)
            for half in range(2):
                transpose_x2(0, half)
            pe.wait_ge(s_mtc, B)
            pe.wait_ge(s_exp, HEADS * B)
            pe.wait_ge(s_wsign, 1)
            pe.wait_ge(s_wready, 1)
            first_product(0, 0)
            step_b(0, B + 1)
            first_product(0, 1)
            for half in range(2):
                transpose_x2(1, half)
            pe.wait_ge(s_on, B)
            pe.wait_ge(s_res, B)
            for n in range(1, C_STEPS):
                if n < QGROUPS:
                    first_product(n, 0)
                if n < QGROUPS:
                    first_product(n, 1)
                if 2 <= n < QGROUPS:
                    residual(n - 2)
                for half in range(2):
                    if n + 1 < QGROUPS:
                        transpose_x2(n + 1, half)
                    if n <= QGROUPS:
                        second_product(n - 1, half)
                    if n >= QGROUPS and half == 0:
                        residual(n - 2)
                if n == QGROUPS - 1:
                    pe.wait_ge(s_x2c, 2 * QGROUPS)
                    for t in range(NT):
                        last = nc.tensor.transpose(bank[0:C, 0, t * P:(t + 1) * P], tok[:, B - 1, t, :], ident[:])
                    last.then_inc(s_t2last, 1)


_INS = ["x", "L0_conv_weight_coord", "L0_conv_radius", "L0_conv_weights", "L1_attn_w_attn", "L1_attn_w_proj",
        "L1_ffn_W1", "L1_ffn_b1", "L1_ffn_W2", "L1_ffn_b2"]


def kernel(**inputs):
    import numpy as _np
    import concourse.bacc as _bacc
    from concourse import mybir as _mybir
    from concourse.bass_utils import run_bass_kernel_spmd as _run

    nc = _bacc.Bacc("TRN2", target_bir_lowering=False, num_devices=1)
    arrays, args = {}, []
    for name in _INS:
        a = _np.ascontiguousarray(inputs[name])
        arrays[f"in_{name}"] = a
        args.append(nc.dram_tensor(f"in_{name}", a.shape, _mybir.dt.from_np(a.dtype), kind="ExternalInput").ap())
    table = shape_constants()
    arrays["in_const"] = table
    args.append(nc.dram_tensor("in_const", table.shape, _mybir.dt.float32, kind="ExternalInput").ap())
    args.append(nc.dram_tensor("out_0", (B, C, SIDE, SIDE), _mybir.dt.float32, kind="ExternalOutput").ap())
    build(nc, *args)
    r = _run(nc, [arrays], core_ids=[0])
    return r.results[0]["out_0"]
```
